# Optimizing a Trainium2 kernel written in Bass

```python
import numpy as np
import jax
import jax.numpy as jnp

def _softmax(x, axis=-1):
    return jax.nn.softmax(x, axis=axis)

def _gelu(x):
    return jax.nn.gelu(x, approximate=True)

def _silu(x):
    return jax.nn.silu(x)

def _sigmoid(x):
    return jax.nn.sigmoid(x)

def _layernorm(x, axis=-1, eps=1e-05):
    m = jnp.mean(x, axis=axis, keepdims=True)
    v = jnp.var(x, axis=axis, keepdims=True)
    return (x - m) / jnp.sqrt(v + eps)

def _scatter_add(tgt, idx, src, axis=0):
    return tgt.at[idx].add(src)

def _segment_sum(src, seg, n):
    return jax.ops.segment_sum(src, seg, n)
kernel_name = 'mk_flamingo_gated_d2_seqx_r8_715ac1'

def setup_inputs(seed: int=0):
    np.random.seed(seed)
    _w = jnp.asarray

    def _rec_inputs():
        import jax
        import jax.numpy as jnp
        _rk = jax.random.key(seed)
        x = -0.000125 + 0.9999 * jax.random.normal(jax.random.fold_in(_rk, 1), (8, 128, 256), jnp.float32)
        _lenS = 128 - jax.random.randint(jax.random.fold_in(_rk, 7), (8,), 0, max(1, 128 // 4) + 1, jnp.int32)
        _lenS2 = 128 - jax.random.randint(jax.random.fold_in(_rk, 8), (8,), 0, max(1, 128 // 4) + 1, jnp.int32)
        _ctx_2048P = jax.random.normal(jax.random.fold_in(_rk, 11), (8, 16, 256), jnp.float32)
        _ctx_2048c = jax.random.dirichlet(jax.random.fold_in(_rk, 511), 0.3 * jnp.ones((16,), jnp.float32), (8, 128))
        _ctx_2048t = jnp.einsum('bsk,bkd->bsd', _ctx_2048c, _ctx_2048P)
        _ctx_2048t = _ctx_2048t * jax.lax.rsqrt(jnp.mean(jnp.square(_ctx_2048t)) + 1e-12) * 0.953939
        ctx_2048 = 4.13588e-05 + 0.999923 * (_ctx_2048t + 0.3 * jax.random.normal(jax.random.fold_in(_rk, 611), (8, 128, 256), jnp.float32))
        _g = jax.random.normal(jax.random.fold_in(_rk, 9001), (2, 2), jnp.float32)
        _g = jnp.sign(_g) * jnp.maximum(jnp.abs(_g), 1.0) + (_g == 0) * 1.0
        g_xattn = _g[0]
        g_ffn = _g[1]
        return (x, ctx_2048, g_xattn, g_ffn)
    x, ctx_2048, g_xattn, g_ffn = _rec_inputs()

    def _L0_xattn_setup():
        import jax, jax.numpy as jnp
        import numpy as np
        D_MODEL = 256
        NUM_HEADS = 16
        HEAD_DIM = D_MODEL // NUM_HEADS
        key = jax.random.key(seed)
        ks = jax.random.split(key, 10)
        B, S, T = (4, 512, 128)
        s = 1.0 / np.sqrt(D_MODEL)
        inp = {'query': jax.random.normal(ks[0], (B, S, D_MODEL), jnp.float32), 'key_value': jax.random.normal(ks[1], (B, T, D_MODEL), jnp.float32), 'Wq': jax.random.normal(ks[2], (D_MODEL, D_MODEL), jnp.float32) * s, 'bq': jnp.zeros((D_MODEL,), jnp.float32), 'Wk': jax.random.normal(ks[3], (D_MODEL, D_MODEL), jnp.float32) * s, 'bk': jnp.zeros((D_MODEL,), jnp.float32), 'Wv': jax.random.normal(ks[4], (D_MODEL, D_MODEL), jnp.float32) * s, 'bv': jnp.zeros((D_MODEL,), jnp.float32), 'Wo': jax.random.normal(ks[5], (D_MODEL, D_MODEL), jnp.float32) * s, 'bo': jnp.zeros((D_MODEL,), jnp.float32)}
        return inp
    _L0_xattn_all = _L0_xattn_setup()
    _L0_xattn_in = {k: v for k, v in _L0_xattn_all.items() if k in ('Wq', 'bq', 'Wk', 'bk', 'Wv', 'bv', 'Wo', 'bo')}
    del _L0_xattn_all

    def _L0_ffn_setup():
        import jax, jax.numpy as jnp
        import numpy as np
        H, I, E = (256, 512, 8)
        B, S = (2, 256)
        key = jax.random.key(seed)
        ks = jax.random.split(key, 5)
        scale = 0.02
        return {'hidden_states': jax.random.normal(ks[0], (B, S, H), dtype=jnp.float32), 'router_w': jax.random.normal(ks[1], (H, E), dtype=jnp.float32) * scale, 'gate_w': jax.random.normal(ks[2], (E, H, I), dtype=jnp.float32) * scale, 'up_w': jax.random.normal(ks[3], (E, H, I), dtype=jnp.float32) * scale, 'down_w': jax.random.normal(ks[4], (E, I, H), dtype=jnp.float32) * scale}
    _L0_ffn_all = _L0_ffn_setup()
    _L0_ffn_in = {k: v for k, v in _L0_ffn_all.items() if k in ('router_w', 'gate_w', 'up_w', 'down_w')}
    del _L0_ffn_all

    def _L1_xattn_setup():
        import jax, jax.numpy as jnp
        import numpy as np
        DIM = 256
        NH = 16
        HD = DIM // NH
        EPS = 1e-06
        IMG_LEN = 257

        def rms_norm(x, w, eps=EPS):
            xf = x.astype(jnp.float32)
            y = xf * jax.lax.rsqrt(jnp.mean(xf * xf, axis=-1, keepdims=True) + eps)
            return y.astype(x.dtype) * w

        def linear(x, w, b):
            return jnp.einsum('blc,oc->blo', x, w) + b

        def attention(q, k, v):
            scale = 1.0 / jnp.sqrt(jnp.asarray(HD, q.dtype))
            scores = jnp.einsum('bqhd,bkhd->bhqk', q, k) * scale
            probs = jax.nn.softmax(scores, axis=-1)
            return jnp.einsum('bhqk,bkhd->bqhd', probs, v)
        key = jax.random.key(seed)
        ks = jax.random.split(key, 12)
        B, L = (2, 1024)
        s = 0.02
        inp = {'x': jax.random.normal(ks[0], (B, L, DIM), jnp.float32), 'context': jax.random.normal(ks[1], (B, 769, DIM), jnp.float32), 'q_w': jax.random.normal(ks[2], (DIM, DIM), jnp.float32) * s, 'q_b': jnp.zeros((DIM,), jnp.float32), 'k_w': jax.random.normal(ks[3], (DIM, DIM), jnp.float32) * s, 'k_b': jnp.zeros((DIM,), jnp.float32), 'v_w': jax.random.normal(ks[4], (DIM, DIM), jnp.float32) * s, 'v_b': jnp.zeros((DIM,), jnp.float32), 'k_img_w': jax.random.normal(ks[5], (DIM, DIM), jnp.float32) * s, 'k_img_b': jnp.zeros((DIM,), jnp.float32), 'v_img_w': jax.random.normal(ks[6], (DIM, DIM), jnp.float32) * s, 'v_img_b': jnp.zeros((DIM,), jnp.float32), 'o_w': jax.random.normal(ks[7], (DIM, DIM), jnp.float32) * s, 'o_b': jnp.zeros((DIM,), jnp.float32), 'norm_q_w': jnp.ones((DIM,), jnp.float32), 'norm_k_w': jnp.ones((DIM,), jnp.float32), 'norm_k_img_w': jnp.ones((DIM,), jnp.float32)}
        return inp
    _L1_xattn_all = _L1_xattn_setup()
    _L1_xattn_in = {k: v for k, v in _L1_xattn_all.items() if k in ('q_w', 'q_b', 'k_w', 'k_b', 'v_w', 'v_b', 'k_img_w', 'k_img_b', 'v_img_w', 'v_img_b', 'o_w', 'o_b', 'norm_q_w', 'norm_k_w', 'norm_k_img_w')}
    del _L1_xattn_all

    def _L1_ffn_setup():
        import jax, jax.numpy as jnp
        import numpy as np
        B, S, D = (2, 256, 256)
        H, HD = (16, 128)
        E, K, I = (16, 6, 176)
        SI = 352
        EPS = 1e-06

        def rmsnorm(x, w):
            v = jnp.mean(jnp.square(x), axis=-1, keepdims=True)
            return x * jax.lax.rsqrt(v + EPS) * w
        key = jax.random.key(seed)
        ks = jax.random.split(key, 14)
        s = 0.02
        return {'hidden_states': jax.random.normal(ks[0], (B, S, D), jnp.float32), 'ln1_w': jnp.ones((D,), jnp.float32), 'ln2_w': jnp.ones((D,), jnp.float32), 'wq': jax.random.normal(ks[1], (D, H * HD), jnp.float32) * s, 'wk': jax.random.normal(ks[2], (D, H * HD), jnp.float32) * s, 'wv': jax.random.normal(ks[3], (D, H * HD), jnp.float32) * s, 'wo': jax.random.normal(ks[4], (H * HD, D), jnp.float32) * s, 'gate_w': jax.random.normal(ks[5], (E, D), jnp.float32) * s, 'eg_w': jax.random.normal(ks[6], (E, I, D), jnp.float32) * s, 'eu_w': jax.random.normal(ks[7], (E, I, D), jnp.float32) * s, 'ed_w': jax.random.normal(ks[8], (E, D, I), jnp.float32) * s, 'sg_w': jax.random.normal(ks[9], (SI, D), jnp.float32) * s, 'su_w': jax.random.normal(ks[10], (SI, D), jnp.float32) * s, 'sd_w': jax.random.normal(ks[11], (D, SI), jnp.float32) * s}
    _L1_ffn_all = _L1_ffn_setup()
    _L1_ffn_in = {k: v for k, v in _L1_ffn_all.items() if k in ('ln1_w', 'ln2_w', 'wq', 'wk', 'wv', 'wo', 'gate_w', 'eg_w', 'eu_w', 'ed_w', 'sg_w', 'su_w', 'sd_w')}
    del _L1_ffn_all
    return {'x': x, 'ctx_2048': ctx_2048, 'g_xattn': g_xattn, 'g_ffn': g_ffn, 'L0_xattn_Wq': _L0_xattn_in['Wq'], 'L0_xattn_bq': _L0_xattn_in['bq'], 'L0_xattn_Wk': _L0_xattn_in['Wk'], 'L0_xattn_bk': _L0_xattn_in['bk'], 'L0_xattn_Wv': _L0_xattn_in['Wv'], 'L0_xattn_bv': _L0_xattn_in['bv'], 'L0_xattn_Wo': _L0_xattn_in['Wo'], 'L0_xattn_bo': _L0_xattn_in['bo'], 'L0_ffn_router_w': _L0_ffn_in['router_w'], 'L0_ffn_gate_w': _L0_ffn_in['gate_w'], 'L0_ffn_up_w': _L0_ffn_in['up_w'], 'L0_ffn_down_w': _L0_ffn_in['down_w'], 'L1_xattn_q_w': _L1_xattn_in['q_w'], 'L1_xattn_q_b': _L1_xattn_in['q_b'], 'L1_xattn_k_w': _L1_xattn_in['k_w'], 'L1_xattn_k_b': _L1_xattn_in['k_b'], 'L1_xattn_v_w': _L1_xattn_in['v_w'], 'L1_xattn_v_b': _L1_xattn_in['v_b'], 'L1_xattn_k_img_w': _L1_xattn_in['k_img_w'], 'L1_xattn_k_img_b': _L1_xattn_in['k_img_b'], 'L1_xattn_v_img_w': _L1_xattn_in['v_img_w'], 'L1_xattn_v_img_b': _L1_xattn_in['v_img_b'], 'L1_xattn_o_w': _L1_xattn_in['o_w'], 'L1_xattn_o_b': _L1_xattn_in['o_b'], 'L1_xattn_norm_q_w': _L1_xattn_in['norm_q_w'], 'L1_xattn_norm_k_w': _L1_xattn_in['norm_k_w'], 'L1_xattn_norm_k_img_w': _L1_xattn_in['norm_k_img_w'], 'L1_ffn_ln1_w': _L1_ffn_in['ln1_w'], 'L1_ffn_ln2_w': _L1_ffn_in['ln2_w'], 'L1_ffn_wq': _L1_ffn_in['wq'], 'L1_ffn_wk': _L1_ffn_in['wk'], 'L1_ffn_wv': _L1_ffn_in['wv'], 'L1_ffn_wo': _L1_ffn_in['wo'], 'L1_ffn_gate_w': _L1_ffn_in['gate_w'], 'L1_ffn_eg_w': _L1_ffn_in['eg_w'], 'L1_ffn_eu_w': _L1_ffn_in['eu_w'], 'L1_ffn_ed_w': _L1_ffn_in['ed_w'], 'L1_ffn_sg_w': _L1_ffn_in['sg_w'], 'L1_ffn_su_w': _L1_ffn_in['su_w'], 'L1_ffn_sd_w': _L1_ffn_in['sd_w']}

def reference(x, ctx_2048, g_xattn, g_ffn, L0_xattn_Wq, L0_xattn_bq, L0_xattn_Wk, L0_xattn_bk, L0_xattn_Wv, L0_xattn_bv, L0_xattn_Wo, L0_xattn_bo, L0_ffn_router_w, L0_ffn_gate_w, L0_ffn_up_w, L0_ffn_down_w, L1_xattn_q_w, L1_xattn_q_b, L1_xattn_k_w, L1_xattn_k_b, L1_xattn_v_w, L1_xattn_v_b, L1_xattn_k_img_w, L1_xattn_k_img_b, L1_xattn_v_img_w, L1_xattn_v_img_b, L1_xattn_o_w, L1_xattn_o_b, L1_xattn_norm_q_w, L1_xattn_norm_k_w, L1_xattn_norm_k_img_w, L1_ffn_ln1_w, L1_ffn_ln2_w, L1_ffn_wq, L1_ffn_wk, L1_ffn_wv, L1_ffn_wo, L1_ffn_gate_w, L1_ffn_eg_w, L1_ffn_eu_w, L1_ffn_ed_w, L1_ffn_sg_w, L1_ffn_su_w, L1_ffn_sd_w):
    import jax
    import jax.numpy as jnp

    def _L0_xattn_ref(query, key_value, Wq, bq, Wk, bk, Wv, bv, Wo, bo):
        import jax, jax.numpy as jnp
        import numpy as np
        D_MODEL = 256
        NUM_HEADS = 16
        HEAD_DIM = D_MODEL // NUM_HEADS
        B, S, _ = query.shape
        T = key_value.shape[1]
        Q = query @ Wq.T + bq
        K = key_value @ Wk.T + bk
        V = key_value @ Wv.T + bv
        Q = Q.reshape(B, S, NUM_HEADS, HEAD_DIM).transpose(0, 2, 1, 3)
        K = K.reshape(B, T, NUM_HEADS, HEAD_DIM).transpose(0, 2, 1, 3)
        V = V.reshape(B, T, NUM_HEADS, HEAD_DIM).transpose(0, 2, 1, 3)
        scale = 1.0 / np.sqrt(HEAD_DIM).astype(np.float32)
        scores = jnp.einsum('bhsd,bhtd->bhst', Q, K) * scale
        attn = jax.nn.softmax(scores, axis=-1)
        ctx = jnp.einsum('bhst,bhtd->bhsd', attn, V)
        ctx = ctx.transpose(0, 2, 1, 3).reshape(B, S, D_MODEL)
        return ctx @ Wo.T + bo

    def _L0_ffn_ref(hidden_states, router_w, gate_w, up_w, down_w):
        import jax, jax.numpy as jnp
        import numpy as np
        H, I, E = (256, 512, 8)
        B, S = (2, 256)
        hidden_shape = hidden_states.shape
        x = hidden_states.reshape(-1, hidden_shape[-1])
        route = jax.nn.sigmoid(x @ router_w)
        max_ind = jnp.argmax(route, axis=1)
        max_prob = jnp.take_along_axis(route, max_ind[:, None], axis=1)
        out = jnp.zeros_like(x)
        num_experts = gate_w.shape[0]
        for e in range(num_experts):
            mask = (max_ind == e)[:, None]
            h = jax.nn.silu(x @ gate_w[e]) * (x @ up_w[e])
            out = out + jnp.where(mask, h @ down_w[e], 0.0)
        out = out * max_prob
        return out.reshape(hidden_shape)

    def _L1_xattn_ref(x, context, q_w, q_b, k_w, k_b, v_w, v_b, k_img_w, k_img_b, v_img_w, v_img_b, o_w, o_b, norm_q_w, norm_k_w, norm_k_img_w):
        import jax, jax.numpy as jnp
        import numpy as np
        DIM = 256
        NH = 16
        HD = DIM // NH
        EPS = 1e-06
        IMG_LEN = 257

        def rms_norm(x, w, eps=EPS):
            xf = x.astype(jnp.float32)
            y = xf * jax.lax.rsqrt(jnp.mean(xf * xf, axis=-1, keepdims=True) + eps)
            return y.astype(x.dtype) * w

        def linear(x, w, b):
            return jnp.einsum('blc,oc->blo', x, w) + b

        def attention(q, k, v):
            scale = 1.0 / jnp.sqrt(jnp.asarray(HD, q.dtype))
            scores = jnp.einsum('bqhd,bkhd->bhqk', q, k) * scale
            probs = jax.nn.softmax(scores, axis=-1)
            return jnp.einsum('bhqk,bkhd->bqhd', probs, v)
        B, L, _ = x.shape
        ctx_img = context[:, :IMG_LEN]
        ctx_txt = context[:, IMG_LEN:]
        q = rms_norm(linear(x, q_w, q_b), norm_q_w).reshape(B, L, NH, HD)
        k = rms_norm(linear(ctx_txt, k_w, k_b), norm_k_w).reshape(B, -1, NH, HD)
        v = linear(ctx_txt, v_w, v_b).reshape(B, -1, NH, HD)
        k_img = rms_norm(linear(ctx_img, k_img_w, k_img_b), norm_k_img_w).reshape(B, -1, NH, HD)
        v_img = linear(ctx_img, v_img_w, v_img_b).reshape(B, -1, NH, HD)
        img_x = attention(q, k_img, v_img)
        txt_x = attention(q, k, v)
        out = (txt_x + img_x).reshape(B, L, DIM)
        return linear(out, o_w, o_b)

    def _L1_ffn_ref(hidden_states, ln1_w, ln2_w, wq, wk, wv, wo, gate_w, eg_w, eu_w, ed_w, sg_w, su_w, sd_w):
        import jax, jax.numpy as jnp
        import numpy as np
        B, S, D = (2, 256, 256)
        H, HD = (16, 128)
        E, K, I = (16, 6, 176)
        SI = 352
        EPS = 1e-06

        def rmsnorm(x, w):
            v = jnp.mean(jnp.square(x), axis=-1, keepdims=True)
            return x * jax.lax.rsqrt(v + EPS) * w
        b, s, d = hidden_states.shape
        x = hidden_states
        h = rmsnorm(x, ln1_w)
        q = (h @ wq).reshape(b, s, H, HD)
        k = (h @ wk).reshape(b, s, H, HD)
        v = (h @ wv).reshape(b, s, H, HD)
        scores = jnp.einsum('bqhd,bkhd->bhqk', q, k) / np.sqrt(HD).astype(np.float32)
        causal = jnp.tril(jnp.ones((s, s), bool))
        scores = jnp.where(causal, scores, jnp.float32(-1000000000.0))
        attn = jax.nn.softmax(scores, axis=-1)
        ao = jnp.einsum('bhqk,bkhd->bqhd', attn, v).reshape(b, s, H * HD) @ wo
        x = x + ao
        h = rmsnorm(x, ln2_w)
        t = h.reshape(-1, d)
        T = t.shape[0]
        logits = t @ gate_w.T
        probs = jax.nn.softmax(logits, axis=-1)
        topv, topi = jax.lax.top_k(probs, K)
        topv = topv / jnp.sum(topv, axis=-1, keepdims=True)
        cw = jnp.zeros((T, E), t.dtype).at[jnp.arange(T)[:, None], topi].add(topv)
        g = jnp.einsum('td,eid->eti', t, eg_w)
        u = jnp.einsum('td,eid->eti', t, eu_w)
        hh = jax.nn.silu(g) * u
        routed = jnp.einsum('eti,edi,te->td', hh, ed_w, cw)
        shared = jax.nn.silu(t @ sg_w.T) * (t @ su_w.T) @ sd_w.T
        out = x + (routed + shared).reshape(b, s, d)
        return out
    x = x + jnp.tanh(g_xattn[0]) * _L0_xattn_ref(_layernorm(x, axis=-1), ctx_2048, L0_xattn_Wq, L0_xattn_bq, L0_xattn_Wk, L0_xattn_bk, L0_xattn_Wv, L0_xattn_bv, L0_xattn_Wo, L0_xattn_bo)
    x = x + jnp.tanh(g_ffn[0]) * _L0_ffn_ref(_layernorm(x, axis=-1), L0_ffn_router_w, L0_ffn_gate_w, L0_ffn_up_w, L0_ffn_down_w)
    x = x + jnp.tanh(g_xattn[1]) * _L1_xattn_ref(_layernorm(x, axis=-1), ctx_2048, L1_xattn_q_w, L1_xattn_q_b, L1_xattn_k_w, L1_xattn_k_b, L1_xattn_v_w, L1_xattn_v_b, L1_xattn_k_img_w, L1_xattn_k_img_b, L1_xattn_v_img_w, L1_xattn_v_img_b, L1_xattn_o_w, L1_xattn_o_b, L1_xattn_norm_q_w, L1_xattn_norm_k_w, L1_xattn_norm_k_img_w)
    x = x + jnp.tanh(g_ffn[1]) * _L1_ffn_ref(_layernorm(x, axis=-1), L1_ffn_ln1_w, L1_ffn_ln2_w, L1_ffn_wq, L1_ffn_wk, L1_ffn_wv, L1_ffn_wo, L1_ffn_gate_w, L1_ffn_eg_w, L1_ffn_eu_w, L1_ffn_ed_w, L1_ffn_sg_w, L1_ffn_su_w, L1_ffn_sd_w)
    return x

_drawn_inputs = setup_inputs


def setup_inputs(seed=0):
    import zlib

    import numpy as np

    out = dict(_drawn_inputs(seed))
    spreads = {'g_ffn': (-1.0, 0.2),
     'L0_xattn_bq': (0.0, 0.392),
     'L0_xattn_bk': (0.0, 2.0),
     'L0_xattn_bv': (0.0, 0.1),
     'L0_xattn_bo': (0.0, 0.1),
     'L1_xattn_q_b': (0.0, 2.0),
     'L1_xattn_k_b': (0.0, 0.1),
     'L1_xattn_v_b': (0.0, 0.1),
     'L1_xattn_k_img_b': (0.0, 2.0),
     'L1_xattn_v_img_b': (0.0, 0.8),
     'L1_xattn_o_b': (0.0, 0.356),
     'L1_xattn_norm_q_w': (1.0, 0.6),
     'L1_xattn_norm_k_w': (1.0, 0.2),
     'L1_xattn_norm_k_img_w': (1.0, 0.6),
     'L1_ffn_ln1_w': (1.0, 0.6),
     'L1_ffn_ln2_w': (1.0, 0.6)}
    factors = {'L0_ffn_router_w': 6.137,
     'L0_ffn_gate_w': 5.822,
     'L0_ffn_up_w': 5.776,
     'L0_ffn_down_w': 5.786,
     'L1_xattn_q_w': 27.48,
     'L1_xattn_k_img_w': 22.993,
     'L1_ffn_wq': 4.056,
     'L1_ffn_wk': 4.044,
     'L1_ffn_gate_w': 4.144,
     'L1_ffn_eg_w': 3.398,
     'L1_ffn_eu_w': 3.377,
     'L1_ffn_ed_w': 3.362,
     'L1_xattn_v_img_w': 3.91,
     'L1_xattn_o_w': 3.591,
     'L1_ffn_sg_w': 6.045,
     'L1_ffn_su_w': 5.892,
     'L1_ffn_sd_w': 5.918}
    for name, (base, spread) in spreads.items():
        noise = np.random.default_rng([zlib.crc32(name.encode()), seed]).standard_normal(out[name].shape)
        drawn = base * np.exp(spread * noise) if base else spread * noise
        out[name] = jnp.asarray(drawn.astype(out[name].dtype))
    for name, factor in factors.items():
        out[name] = (out[name] * factor).astype(out[name].dtype)
    return out
```

```python
from contextlib import ExitStack

import concourse.bass as bass
from concourse import mybir

F32 = mybir.dt.float32
F32R = mybir.dt.float32r
BF16 = mybir.dt.bfloat16
ALU = mybir.AluOpType
ACT = mybir.ActivationFunctionType
AX = mybir.AxisListType

B, S, D = 8, 128, 256
P = 128
T = B * S
C = D // P
XH, XD = 16, 16
AH, AD = 16, 128
E0, I0 = 8, 512
E1, I1, SI = 16, 176, 352
TOPK = 6
HALF = T // 2
NEG = -3.0e38
LN_EPS, RMS_EPS = 1e-5, 1e-6
J0 = E0 * I0 // P
J1 = -(-(E1 * I1 + SI) // P)
VEC = ["bk0", "bv0", "bq0", "bo0", "bk1", "bv1", "bq1", "bo1", "nk1", "nq1", "ln1", "ln2"]


class Chain:

    def __init__(self, eng, sem):
        self.eng, self.sem, self.base, self.n = eng, sem, 0, 0

    def link(self, ins):
        self.n += 1
        ins.then_inc(self.sem, 1)
        self.eng.wait_ge(self.sem, self.base + self.n)

    def leave(self, start, steps, count):
        assert self.n == steps, (self.n, steps)
        self.base, self.n = start + count * steps, 0


def after(eng, sem, n):
    if isinstance(n, int) and n <= 0:
        return
    eng.wait_ge(sem, n)


def build(nc, ctx_d, x_d, wx_d, vec_d, gate_d, rw0_d, rw1_d, moe0_d, moe1_d, attn_d, out_d):
    stack = ExitStack()
    with stack:
        def sb(name, shape, dt=F32, where=None):
            return (where or stack).enter_context(nc.sbuf_tensor(name, shape, dt))

        def sem(name):
            return stack.enter_context(nc.semaphore(name))

        PS = stack.enter_context(nc.psum_tensor("PS", [P, 8, 512], F32))

        X = sb("X", [P, B, D])
        ctxT = sb("ctxT", [P, B, C, S])
        WXraw = sb("WXraw", [P, C, 4 * D])
        WXh = [sb(f"WXh{i}", [P, C, 4 * D], F32R) for i in range(2)]
        WXl = [sb(f"WXl{i}", [P, C, 4 * D], F32R) for i in range(2)]
        vecs = sb("vecs", [P, len(VEC), D])
        gates = sb("gates", [P, 4])
        tg = sb("tg", [P, 4])
        ident = sb("ident", [P, P])
        identb = sb("identb", [P, P], BF16)
        zeros = sb("zeros", [P, 512], F32R)
        rank8 = sb("rank8", [P, E0])
        rw = sb("rw", [P, C, E0 + E1])
        rwh = sb("rwh", [P, C, E0 + E1], F32R)
        rwl = sb("rwl", [P, C, E0 + E1], F32R)
        tTh = sb("tTh", [P, C, T], F32R)
        tTl = sb("tTl", [P, C, T], F32R)
        Z = sb("Z", [P, B, D])
        st = sb("st", [P, B, 6])
        mv = sb("mv", [P, B, 2])
        ms = sb("ms", [P, B])
        rstd = sb("rstd", [P, B])
        mhalf = sb("mhalf", [P, B])
        kms = sb("kms", [P, 4])

        def vec(name):
            return vecs[:, VEC.index(name), :]

        a = ExitStack()
        xn = sb("xn", [P, D], where=a)
        xTh = sb("xTh", [P, C, S], F32R, a)
        xTl = sb("xTl", [P, C, S], F32R, a)
        cTh = sb("cTh", [P, C, S], F32R, a)
        cTl = sb("cTl", [P, C, S], F32R, a)
        ks = sb("ks", [P, D], where=a)
        qs = sb("qs", [P, D], where=a)
        junk = sb("junk", [P, D], where=a)
        v17 = [sb(f"v17_{i}", [P, XH, XD + 1], where=a) for i in range(2)]
        k4 = sb("k4", [P, XH, 2, 2, XD], F32R, a)
        q4 = sb("q4", [P, XH, 2, 2, XD], F32R, a)
        kT4 = [sb(f"kT4_{i}", [P, XH // 2, S], F32R, a) for i in range(2)]
        qT4 = [sb(f"qT4_{i}", [P, XH // 2, S], F32R, a) for i in range(2)]
        prob = sb("prob", [P, XH, S], where=a)
        probT = sb("probT", [P, XH, S], where=a)
        mx = sb("mx", [P, XH], where=a)
        rden = sb("rden", [P, XH], where=a)
        cx = sb("cx", [P, XH, XD], where=a)
        cxTh = sb("cxTh", [P, C, S], F32R, a)
        cxTl = sb("cxTl", [P, C, S], F32R, a)
        otmp = sb("otmp", [P, D], where=a)
        a.close()
        f = ExitStack()
        rows = 3 * 32
        sel = sb("sel", [rows, J0 * P], BF16, f)
        selj = [sb(f"selj{i}", [rows, P], BF16, f) for i in range(2)]
        cwT = sb("cwT", [rows, T], BF16, f)
        wraw = [sb(f"wraw{i}", [P, 3 * D], where=f) for i in range(2)]
        wh = [sb(f"wh{i}", [P, 3 * D], F32R, f) for i in range(2)]
        wl = [sb(f"wl{i}", [P, 3 * D], F32R, f) for i in range(2)]
        act_s = [sb(f"act_s{i}", [P, HALF], where=f) for i in range(2)]
        hh = [sb(f"hh{i}", [P, HALF], where=f) for i in range(2)]
        hhh = [sb(f"hhh{i}", [P, HALF], F32R, f) for i in range(2)]
        hhl = [sb(f"hhl{i}", [P, HALF], F32R, f) for i in range(2)]
        yT = sb("yT", [P, C, T], where=f)
        lg = sb("lg", [P, B, E1], where=f)
        pr = sb("pr", [P, B, E1], where=f)
        wk = sb("wk", [P, B, E1], where=f)
        cw = sb("cw", [P, B, E1 + 2], where=f)
        cr = sb("cr", [P, B, E1 + 2], where=f)
        top8 = sb("top8", [P, B, 8], where=f)
        red = sb("red", [P, B], where=f)
        cw3 = sb("cw3", [P, B, 3, 32], BF16, f)
        fxn = [sb(f"fxn{i}", [P, D], where=f) for i in range(2)]
        fjunk = sb("fjunk", [P, D], where=f)
        f.close()
        g = ExitStack()
        ayT = sb("ayT", [P, C, T], where=g)
        araw = [sb(f"araw{i}", [P, 4 * D], where=g) for i in range(2)]
        ah = [sb(f"ah{i}", [P, 4 * D], F32R, g) for i in range(2)]
        al = [sb(f"al{i}", [P, 4 * D], F32R, g) for i in range(2)]
        qTh = [sb(f"qTh{i}", [P, T], F32R, g) for i in range(2)]
        qTl = [sb(f"qTl{i}", [P, T], F32R, g) for i in range(2)]
        kTh = [sb(f"kTh{i}", [P, T], F32R, g) for i in range(2)]
        kTl = [sb(f"kTl{i}", [P, T], F32R, g) for i in range(2)]
        vh = [sb(f"vh{i}", [P, T], F32R, g) for i in range(2)]
        vl = [sb(f"vl{i}", [P, T], F32R, g) for i in range(2)]
        sm = sb("sm", [P, B, S], where=g)
        pTh = sb("pTh", [P, T], F32R, g)
        pTl = sb("pTl", [P, T], F32R, g)
        oTh = sb("oTh", [P, T], F32R, g)
        oTl = sb("oTl", [P, T], F32R, g)
        nmx = sb("nmx", [P, B], where=g)
        sums = sb("sums", [P, B], where=g)
        rsum = sb("rsum", [P, B], where=g)
        causal = sb("causal", [P, S], where=g)
        gxn = [sb(f"gxn{i}", [P, D], where=g) for i in range(2)]
        gjunk = sb("gjunk", [P, D], where=g)
        g.close()

        x_in, ctx_in, vec_in, out_done = sem("x_in"), sem("ctx_in"), sem("vec_in"), sem("out_done")
        wx_in = [sem("wx_in0"), sem("wx_in1")]
        wx_split = sem("wx_split")
        const_done, tg_done, rw_split = sem("const_done"), sem("tg_done"), sem("rw_split")
        pool_turns, stats_done, rstd_done = sem("pool_turns"), sem("stats_done"), sem("rstd_done")
        dve_chain, pool_chain = sem("dve_chain"), sem("pool_chain")
        phase_end = sem("phase_end")

        class Xs:
            def __init__(s, n):
                s.ln_done = sem(f"x{n}_ln_done")
                s.ctx_split = sem(f"x{n}_ctx_split")
                s.small_done = sem(f"x{n}_small_done")
                s.small_free = sem(f"x{n}_small_free")
                s.hi_done = sem(f"x{n}_hi_done")
                s.tr_done = sem(f"x{n}_tr_done")
                s.tr_free = sem(f"x{n}_tr_free")
                s.k_ready = sem(f"x{n}_k_ready")
                s.q_ready = sem(f"x{n}_q_ready")
                s.heads_split = sem(f"x{n}_heads_split")
                s.scores_done = sem(f"x{n}_scores_done")
                s.sub_done = sem(f"x{n}_sub_done")
                s.exp_done = sem(f"x{n}_exp_done")
                s.k_biased = sem(f"x{n}_k_biased")
                s.pool_steps = sem(f"x{n}_pool_steps")

        class Fs:
            def __init__(s, n):
                s.n_done = sem(f"f{n}_n_done")
                s.t_done = sem(f"f{n}_t_done")
                s.thi = sem(f"f{n}_thi")
                s.tlo = sem(f"f{n}_tlo")
                s.lg_done = sem(f"f{n}_lg_done")
                s.lg_out = sem(f"f{n}_lg_out")
                s.ex_done = sem(f"f{n}_ex_done")
                s.cw_done = sem(f"f{n}_cw_done")
                s.ct_done = sem(f"f{n}_ct_done")
                s.cwt_ready = sem(f"f{n}_cwt_ready")
                s.w_in = sem(f"f{n}_w_in")
                s.w_in1 = sem(f"f{n}_w_in1")
                s.w_split = sem(f"f{n}_w_split")
                s.g_done = sem(f"f{n}_g_done")
                s.u_done = sem(f"f{n}_u_done")
                s.c_done = sem(f"f{n}_c_done")
                s.d_done = sem(f"f{n}_d_done")
                s.silu_done = sem(f"f{n}_silu_done")
                s.a_done = sem(f"f{n}_a_done")
                s.h_done = sem(f"f{n}_h_done")
                s.hi_done = sem(f"f{n}_hi_done")
                s.lo_done = sem(f"f{n}_lo_done")
                s.acc_done = sem(f"f{n}_acc_done")
                s.y_out = sem(f"f{n}_y_out")
                s.yt_done = sem(f"f{n}_yt_done")
                s.y_free = sem(f"f{n}_y_free")
                s.tile_out = sem(f"f{n}_tile_out")

        xs = [Xs(0), Xs(1)]
        fs = [Fs(0), Fs(1)]
        n_done, t_done, thi_done, tlo_done = (sem("n_" + k) for k in ("n_done", "t_done", "thi_done", "tlo_done"))
        aw_in = [sem("aw_in0"), sem("aw_in1")]
        aw_split, ring_done, ring_free, ahi_done = (sem(k) for k in ("aw_split", "ring_done", "ring_free", "ahi_done"))
        masked, aexp_done, norm_done, wo_done = (sem(k) for k in ("masked", "aexp_done", "norm_done", "wo_done"))
        ay_out, ayt_done, ay_free = (sem(k) for k in ("ay_out", "ayt_done", "ay_free"))

        block = stack.enter_context(nc.Block())

        def pool_wait(pool, sm_, n):
            after(pool, sm_, n)
            if not isinstance(n, int):
                pool.sem_inc(pool_turns, 1)

        def barrier(eng, k):
            eng.drain().then_inc(phase_end, 1)
            eng.wait_ge(phase_end, 5 * k)

        def three(pe, out, wh_, wl_, xh_, xl_, first, last, **kw):
            nc.tensor.matmul(out, wh_, xh_, start=first, stop=False, **kw)
            nc.tensor.matmul(out, wh_, xl_, start=False, stop=False, **kw)
            return nc.tensor.matmul(out, wl_, xh_, start=False, stop=last, **kw)

        PRE_SMALL, PER_SMALL, PRE_TR, PER_TR = 6, 6, 4, 8
        LOOPED = B - 2

        def small(i):
            return PS[:, 6 + i % 2, :]

        def small_n(n):
            if not isinstance(n, int) or n < LOOPED:
                return PRE_SMALL + n * PER_SMALL, PRE_SMALL
            k = PRE_SMALL + LOOPED * PER_SMALL + 3 * (n - LOOPED)
            return k, k

        def xattn_pe(pe, L):
            s = xs[L]
            wH, wL = WXh[L], WXl[L]

            def small_use(k, si):
                after(pe, s.small_free, k - 1)

            def t1(b, k, si):
                small_use(k, si)
                pe.wait_ge(s.ln_done, b + 1)
                for c in range(C):
                    m = nc.tensor.transpose(small(si)[:, c * P:(c + 1) * P], xn[:, c * P:(c + 1) * P], ident[:, :])
                m.then_inc(s.small_done, 1)

            def kv(b, k, si):
                small_use(k, si)
                pe.wait_ge(s.ctx_split, 2 * b + 2)
                for c in range(C):
                    m = three(pe, small(si)[:, :], cTh[:, c, :], cTl[:, c, :], wH[:, c, 0:512], wL[:, c, 0:512], c == 0, c == C - 1)
                m.then_inc(s.small_done, 1)

            def proj(lh, ll, col, k, si):
                for c in range(C):
                    m = three(pe, small(si)[:, 0:D], lh[:, c, :], ll[:, c, :], wH[:, c, col:col + D], wL[:, c, col:col + D], c == 0, c == C - 1)
                m.then_inc(s.small_done, 1)

            def q(b, k, si, t1_k):
                small_use(k, si)
                pe.wait_ge(s.small_free, t1_k + 1)
                proj(xTh, xTl, 2 * D, k, si)

            def t2(b, r):
                for part, (src, need) in enumerate(((k4, 2), (q4, 4))):
                    pe.wait_ge(s.heads_split, 4 * b + need)
                    v = src[:, :, :, :, :].rearrange("p h a b d -> p (h a b d)").bitcast(F32)
                    for half in range(2):
                        i = 2 * part + half
                        after(pe, s.tr_free, r + i - 1)
                        for t in range(4):
                            m = nc.tensor.transpose(PS[:, 4 + i % 2, t * P:(t + 1) * P], v[:, (4 * half + t) * P:(4 * half + t + 1) * P], ident[:, :])
                        m.then_inc(s.tr_done, 1)

            def scores(b, par, r):
                after(pe, s.sub_done, 2 * b)
                pe.wait_ge(s.tr_free, r + 4)
                for gq in range(2):
                    for t in range(4):
                        for half in range(2):
                            h0 = 64 * half
                            m = nc.tensor.matmul(PS[:, 2 * gq + half, t * P:(t + 1) * P], qT4[par][h0:h0 + 64, 4 * gq + t, :],
                                                 kT4[par][h0:h0 + 64, 4 * gq + t, :], start=True, stop=True)
                    m.then_inc(s.scores_done, 1)

            def pt(n, r):
                for i in range(4):
                    if i % 2 == 0:
                        pe.wait_ge(s.exp_done, 2 * n + i // 2 + 1)
                    after(pe, s.tr_free, r + i - 1)
                    for t in range(4):
                        m = nc.tensor.transpose(PS[:, 4 + i % 2, t * P:(t + 1) * P], prob[:, 4 * i + t, :], ident[:, :])
                    m.then_inc(s.tr_done, 1)

            def pv(n, par, k, si, r):
                small_use(k, si)
                pe.wait_ge(s.tr_free, r + 4)
                o = small(si)[:, 0:XH * (XD + 1)].rearrange("p (h d) -> p h d", d=XD + 1)
                for slot in range(XH):
                    h = head_of(slot)
                    m = nc.tensor.matmul(o[:, h, :], probT[:, slot, :], v17[par][:, h, :], start=True, stop=True)
                m.then_inc(s.small_done, 1)

            def t3(n, k, si):
                small_use(k, si)
                pe.wait_ge(s.small_free, k)
                for c in range(C):
                    m = nc.tensor.transpose(small(si)[:, c * P:(c + 1) * P], cx[:, :, :].rearrange("p h d -> p (h d)")[:, c * P:(c + 1) * P], ident[:, :])
                m.then_inc(s.small_done, 1)

            def o(n, k, si, t3_k):
                small_use(k, si)
                pe.wait_ge(s.small_free, t3_k + 1)
                proj(cxTh, cxTl, 3 * D, k, si)

            def sequence(n, par, nxt, far):
                k, si = small_n(n)
                r = PRE_TR + n * PER_TR
                pt(n, r)
                if nxt:
                    t2(n + 1, r + 4)
                pv(n, par, k, si, r)
                if nxt:
                    scores(n + 1, 1 - par, r + 4)
                t3(n, k + 1, si + 1)
                if far:
                    t1(n + 2, k + 2, si + 2)
                    kv(n + 2, k + 3, si + 3)
                    o(n, k + 4, si + 4, k + 1)
                    q(n + 2, k + 5, si + 5, k + 2)
                else:
                    o(n, k + 2, si + 2, k + 1)

            pe.wait_ge(wx_split, 2 * L + 2)
            t1(0, 0, 0)
            kv(0, 1, 1)
            t1(1, 2, 2)
            q(0, 3, 3, 0)
            kv(1, 4, 4)
            q(1, 5, 5, 2)
            t2(0, 0)
            scores(0, 0, 0)
            with pe.Fori(0, LOOPED // 2) as i:
                n = 2 * i
                sequence(n, 0, True, True)
                sequence(n + 1, 1, True, True)
            sequence(LOOPED, 0, True, False)
            sequence(LOOPED + 1, 1, False, False)

        def head_of(slot):
            gq, half, t = slot // 8, slot // 4 % 2, slot % 4
            return 2 * (4 * gq + t) + half

        def split_lo(lo, src, hi):
            return nc.vector.tensor_tensor(lo, src, hi.bitcast(F32), ALU.subtract)

        def xattn_act(act, L):
            s = xs[L]

            def hi(k, si, dst, wait_q=None):
                act.wait_ge(s.small_done, k + 1)
                if wait_q is not None:
                    act.wait_ge(s.small_done, wait_q + 1)
                nc.scalar.activation(dst[:, :, :].rearrange("p c s -> p (c s)"), small(si)[:, 0:D], ACT.Copy).then_inc(s.hi_done, 1)

            def t2(b, par, r):
                for i, dst in enumerate((kT4, kT4, qT4, qT4)):
                    act.wait_ge(s.tr_done, r + i + 1)
                    d = dst[par][:, 4 * (i % 2):4 * (i % 2) + 4, :].rearrange("p t s -> p (t s)")
                    nc.scalar.activation(d, PS[:, 4 + i % 2, :], ACT.Copy).then_inc(s.tr_free, 1)

            def exps(b):
                for gq in range(2):
                    act.wait_ge(s.sub_done, 2 * b + gq + 1)
                    pr_ = prob[:, 8 * gq:8 * gq + 8, :]
                    nc.scalar.activation(pr_, pr_, ACT.Exp, scale=XD ** -0.5).then_inc(s.exp_done, 1)

            def pt(n, r):
                for i in range(4):
                    act.wait_ge(s.tr_done, r + i + 1)
                    nc.scalar.activation(probT[:, 4 * i:4 * i + 4, :].rearrange("p t s -> p (t s)"), PS[:, 4 + i % 2, :], ACT.Copy).then_inc(s.tr_free, 1)

            def sequence(n, par, nxt, far):
                k, si = small_n(n)
                r = PRE_TR + n * PER_TR
                pt(n, r)
                if nxt:
                    t2(n + 1, 1 - par, r + 4)
                hi(k + 1, si + 1, cxTh)
                if far:
                    hi(k + 2, si + 2, xTh)
                if nxt:
                    exps(n + 1)

            hi(0, 0, xTh)
            hi(2, 2, xTh, wait_q=3)
            t2(0, 0, 0)
            exps(0)
            with act.Fori(0, LOOPED // 2) as i:
                n = 2 * i
                sequence(n, 0, True, True)
                sequence(n + 1, 1, True, True)
            sequence(LOOPED, 0, True, False)
            sequence(LOOPED + 1, 1, False, False)

        def mean_square(src, tmp, dst):
            return nc.vector.tensor_tensor_reduce(out=tmp, in0=src, in1=src, scale=1.0 / D, scalar=RMS_EPS, op0=ALU.mult, op1=ALU.add, accum_out=dst)

        def ln_stats(dve, ch, src, use):
            for b in range(B):
                i = nc.vector.bn_stats(st[:, b, :], src[:, b, :])
            ch.link(i)
            for b in range(B):
                i = nc.vector.bn_aggr(mv[:, b, :], st[:, b, :])
            ch.link(i)
            nc.vector.tensor_scalar(ms[:, :].unsqueeze(2), mv[:, :, 1:2], LN_EPS, None, ALU.add).then_inc(stats_done, 1)
            dve.wait_ge(rstd_done, use)

        def ln_scale(out, src, b):
            return nc.vector.tensor_scalar(out, src, mv[:, b, 0:1], rstd[:, b:b + 1], ALU.subtract, ALU.mult)

        def power(pool, use):
            pool.wait_ge(stats_done, use)
            nc.gpsimd.tensor_tensor(rstd[:, :], ms[:, :], mhalf[:, :], ALU.pow).then_inc(rstd_done, 1)

        def xattn_dve(dve, L, ch):
            s = xs[L]

            def ln(b):
                nc.vector.tensor_scalar(xn[:, :], X[:, b, :], mv[:, bass.ds(b, 1), 0], rstd[:, bass.ds(b, 1)], ALU.subtract, ALU.mult).then_inc(s.ln_done, 1)

            def lo(k, si, hi_count, h_, l_):
                dve.wait_ge(s.hi_done, hi_count)
                split_lo(l_[:, :, :].rearrange("p c s -> p (c s)"), small(si)[:, 0:D], h_[:, :, :].rearrange("p c s -> p (c s)")).then_inc(s.small_free, 1)

            def kv(b, par, k, si):
                dve.wait_ge(s.small_done, k + 1)
                after(dve, s.heads_split, 4 * b)
                keys = nc.vector.tensor_tensor(ks[:, :], small(si)[:, 0:D], vec(f"bk{L}"), ALU.add)
                keys.then_inc((s.k_ready, s.k_biased)[L], 1)
                nc.vector.tensor_tensor(v17[par][:, :, 0:XD], small(si)[:, D:2 * D].rearrange("p (h d) -> p h d", d=XD),
                                        vec(f"bv{L}").rearrange("p (h d) -> p h d", d=XD), ALU.add).then_inc(s.small_free, 1)
                if L:
                    dve.wait_ge(s.k_biased, b + 1)
                    mean_square(ks[:, :], junk[:, :], kms[:, 0:1]).then_inc(s.k_ready, 1)

            def q(b, k, si):
                dve.wait_ge(s.small_done, k + 1)
                nc.vector.tensor_tensor(qs[:, :], small(si)[:, 0:D], vec(f"bq{L}"), ALU.add).then_inc(s.small_free, 1)
                if L:
                    dve.wait_ge(s.small_free, k + 1)
                    mean_square(qs[:, :], junk[:, :], kms[:, 1:2]).then_inc(s.q_ready, 1)

            def softmax(b):
                for gq in range(2):
                    dve.wait_ge(s.scores_done, 2 * b + gq + 1)
                    sc = PS[:, 2 * gq:2 * gq + 2, :].rearrange("p a (t s) -> p (a t) s", s=S)
                    m8 = mx[:, 8 * gq:8 * gq + 8]
                    ch.link(nc.vector.tensor_reduce(m8, sc, AX.X, ALU.max))
                    nc.vector.tensor_tensor(prob[:, 8 * gq:8 * gq + 8, :], sc, m8.unsqueeze(2).broadcast_to([P, 8, S]), ALU.subtract).then_inc(s.sub_done, 1)

            def pv(n, k, si):
                dve.wait_ge(s.small_done, k + 1)
                o = small(si)[:, 0:XH * (XD + 1)].rearrange("p (h d) -> p h d", d=XD + 1)
                ch.link(nc.vector.reciprocal(rden[:, :].unsqueeze(2), o[:, :, XD:XD + 1]))
                nc.vector.tensor_tensor(cx[:, :, :], o[:, :, 0:XD], rden[:, :].unsqueeze(2).broadcast_to([P, XH, XD]), ALU.mult).then_inc(s.small_free, 1)

            def o(n, k, si):
                dve.wait_ge(s.small_done, k + 1)
                nc.vector.tensor_tensor(otmp[:, :], small(si)[:, 0:D], vec(f"bo{L}"), ALU.add).then_inc(s.small_free, 1)
                dve.wait_ge(s.small_free, k + 1)
                ch.link(nc.vector.scalar_tensor_tensor(out=X[:, n, :], in0=otmp[:, :], scalar=tg[:, L:L + 1], in1=X[:, n, :], op0=ALU.mult, op1=ALU.add))

            def sequence(n, par, nxt, far, more):
                k, si = small_n(n)
                hc = 2 + 2 * n if (not isinstance(n, int) or n < LOOPED) else 2 + 2 * LOOPED + (n - LOOPED)
                pv(n, k, si)
                lo(k + 1, si + 1, hc + 1, cxTh, cxTl)
                if far:
                    lo(k + 2, si + 2, hc + 2, xTh, xTl)
                if nxt:
                    softmax(n + 1)
                if far:
                    kv(n + 2, par, k + 3, si + 3)
                    o(n, k + 4, si + 4)
                    q(n + 2, k + 5, si + 5)
                    if more:
                        ln(n + 3)
                else:
                    o(n, k + 2, si + 2)

            ln_stats(dve, ch, X, 1 + 2 * L)
            ln(0)
            dve.wait_ge(s.small_done, 1)
            lo(0, 0, 1, xTh, xTl)
            ln(1)
            kv(0, 0, 1, 1)
            dve.wait_ge(s.small_done, 4)
            lo(2, 2, 2, xTh, xTl)
            q(0, 3, 3)
            kv(1, 1, 4, 4)
            q(1, 5, 5)
            softmax(0)
            ln(2)
            start = ch.base + ch.n
            steps = 8
            with dve.Fori(0, (LOOPED - 2) // 2) as i:
                n = 2 * i
                ch.base, ch.n = start + i * steps, 0
                sequence(n, 0, True, True, True)
                sequence(n + 1, 1, True, True, True)
            ch.leave(start, steps, LOOPED // 2 - 1)
            sequence(LOOPED - 2, 0, True, True, True)
            sequence(LOOPED - 1, 1, True, True, False)
            sequence(LOOPED, 0, True, False, False)
            sequence(LOOPED + 1, 1, False, False, False)

        def xattn_pool(pool, L):
            s = xs[L]

            def ctx_part(b):
                if isinstance(b, int) and b == 0:
                    pool_wait(pool, ctx_in, 16)
                else:
                    pool_wait(pool, s.k_ready, b)
                nc.gpsimd.tensor_copy(cTh[:, :, :], ctxT[:, b, :, :]).then_inc(s.ctx_split, 1)
                pool_wait(pool, s.ctx_split, 2 * b + 1)
                nc.gpsimd.tensor_tensor(cTl[:, :, :], ctxT[:, b, :, :], cTh[:, :, :].bitcast(F32), ALU.subtract).then_inc(s.ctx_split, 1)

            def heads(b, r):
                pool_wait(pool, s.tr_done, r)
                for src, dst, ready, j, pat in ((ks, k4, s.k_ready, 0, "k"), (qs, q4, s.q_ready, 2, "q")):
                    if L or pat == "k":
                        pool_wait(pool, ready, b + 1)
                    else:
                        pool_wait(pool, s.small_free, 4 if isinstance(b, int) and b == 0 else PER_SMALL * b)
                    if L:
                        c0, w = ("k", "q").index(pat), vec(("nk1", "nq1")[("k", "q").index(pat)])
                        nc.gpsimd.tensor_tensor(kms[:, c0 + 2:c0 + 3], kms[:, c0:c0 + 1], mhalf[:, 0:1], ALU.pow).then_inc(s.pool_steps, 1)
                        pool_wait(pool, s.pool_steps, 6 * b + 3 * c0 + 1)
                        nc.gpsimd.tensor_scalar(src[:, :], src[:, :], kms[:, c0 + 2:c0 + 3], None, ALU.mult).then_inc(s.pool_steps, 1)
                        pool_wait(pool, s.pool_steps, 6 * b + 3 * c0 + 2)
                        nc.gpsimd.tensor_tensor(src[:, :], src[:, :], w, ALU.mult).then_inc(s.pool_steps, 1)
                        pool_wait(pool, s.pool_steps, 6 * b + 3 * c0 + 3)
                    v = src[:, :].rearrange("p (h d) -> p h d", d=XD).unsqueeze(2).broadcast_to([P, XH, 2, XD])
                    hi_, lo_ = (dst[:, :, :, 0, :], dst[:, :, :, 1, :]) if pat == "k" else (dst[:, :, 0, :, :], dst[:, :, 1, :, :])
                    nc.gpsimd.tensor_copy(hi_, v).then_inc(s.heads_split, 1)
                    pool_wait(pool, s.heads_split, 4 * b + j + 1)
                    nc.gpsimd.tensor_tensor(lo_, v, hi_.bitcast(F32), ALU.subtract).then_inc(s.heads_split, 1)

            power(pool, 1 + 2 * L)
            ctx_part(0)
            ctx_part(1)
            heads(0, 0)
            heads(1, 4)
            ctx_part(2)
            with pool.Fori(2, B - 1) as b:
                heads(b, PRE_TR + (b - 1) * PER_TR)
                ctx_part(b + 1)
            heads(B - 1, PRE_TR + (B - 2) * PER_TR)

        def columns_pe(pe, src, ready, done, lo_done):
            for b in range(B):
                pe.wait_ge(ready, b + 1)
                after(pe, lo_done, b - 1)
                for c in range(C):
                    m = nc.tensor.transpose(PS[:, b % 2, c * P:(c + 1) * P], src[b % 2][:, c * P:(c + 1) * P], ident[:, :])
                m.then_inc(done, 1)

        def columns_act(act, done, hi_done):
            for b in range(B):
                act.wait_ge(done, b + 1)
                nc.scalar.activation(tTh[:, :, b * S:(b + 1) * S], PS[:, b % 2, 0:D].rearrange("p (c s) -> p c s", c=C), ACT.Copy).then_inc(hi_done, 1)

        def columns_lo(dve, b, hi_done, lo_done):
            dve.wait_ge(hi_done, b + 1)
            split_lo(tTl[:, :, b * S:(b + 1) * S], PS[:, b % 2, 0:D].rearrange("p (c s) -> p c s", c=C), tTh[:, :, b * S:(b + 1) * S]).then_inc(lo_done, 1)

        def route_pe(pe, L):
            s = fs[L]
            lo_, hi_ = (0, E0) if L == 0 else (E0, E0 + E1)
            n = hi_ - lo_
            pe.wait_ge(rw_split, 2)
            for b in range(B):
                pe.wait_ge(s.tlo, b + 1)
                for c in range(C):
                    m = three(pe, PS[:, 2, b * E1:b * E1 + n], tTh[:, c, b * S:(b + 1) * S], tTl[:, c, b * S:(b + 1) * S],
                              rwh[:, c, lo_:hi_], rwl[:, c, lo_:hi_], c == 0, c == C - 1)
            m.then_inc(s.lg_done, 1)
            pe.wait_ge(s.cw_done, 1)
            psb = PS[:, 3, :].bitcast(BF16)
            for b in range(B):
                m = nc.tensor.transpose(psb[0:rows, b * P:(b + 1) * P], cw3[:, b, :, :].rearrange("p a e -> p (a e)"), identb[:, :])
            m.then_inc(s.ct_done, 1)

        def route_act(act, L):
            s = fs[L]
            n = (E0, E1)[L]
            act.wait_ge(s.lg_out, 1)
            nc.scalar.activation(pr[:, :, 0:n], lg[:, :, 0:n], ACT.Exp, scale=(-1.0, 1.0)[L]).then_inc(s.ex_done, 1)
            act.wait_ge(s.ct_done, 1)
            nc.scalar.activation(cwT[:, :], PS[0:rows, 3, :].bitcast(BF16), ACT.Copy).then_inc(s.cwt_ready, 1)

        def route_dve(dve, L, ch):
            s = fs[L]
            n = (E0, E1)[L]
            full = n + 2 * L
            v = nc.vector

            def wide(x):
                return x.unsqueeze(2).broadcast_to([P, B, n])

            dve.wait_ge(s.lg_done, 1)
            scores = PS[:, 2, 0:B * E1].rearrange("p (b e) -> p b e", e=E1)[:, :, 0:n]
            ch.link(v.memset(cw3[:, :, :, :], 0.0))
            if L == 0:
                v.tensor_copy(lg[:, :, 0:n], scores).then_inc(s.lg_out, 1)
                dve.wait_ge(s.ex_done, 1)
                ch.link(v.tensor_scalar(wk[:, :, 0:n], pr[:, :, 0:n], 1.0, None, ALU.add))
                ch.link(v.reciprocal(pr[:, :, 0:n], wk[:, :, 0:n]))
                ch.link(v.tensor_reduce(red[:, :], pr[:, :, 0:n], AX.X, ALU.max))
                ch.link(v.tensor_tensor(wk[:, :, 0:n], pr[:, :, 0:n], wide(red[:, :]), ALU.is_equal))
                ch.link(v.tensor_tensor(wk[:, :, 0:n], wk[:, :, 0:n], rank8[:, :].unsqueeze(1).broadcast_to([P, B, n]), ALU.mult))
                ch.link(v.tensor_reduce(red[:, :], wk[:, :, 0:n], AX.X, ALU.max))
                ch.link(v.tensor_tensor(wk[:, :, 0:n], wk[:, :, 0:n], wide(red[:, :]), ALU.is_equal))
                ch.link(v.tensor_tensor(cw[:, :, 0:n], wk[:, :, 0:n], pr[:, :, 0:n], ALU.mult))
            else:
                ch.link(v.tensor_reduce(red[:, :], scores, AX.X, ALU.max))
                v.tensor_tensor(lg[:, :, :], scores, wide(red[:, :]), ALU.subtract).then_inc(s.lg_out, 1)
                dve.wait_ge(s.ex_done, 1)
                ch.link(v.tensor_reduce(red[:, :], pr[:, :, :], AX.X, ALU.add))
                ch.link(v.reciprocal(red[:, :], red[:, :]))
                ch.link(v.tensor_tensor(pr[:, :, :], pr[:, :, :], wide(red[:, :]), ALU.mult))
                for b in range(B):
                    ch.link(v.max(top8[:, b, :], pr[:, b, :]))
                ch.link(v.memset(top8[:, :, TOPK:8], -1.0))
                for b in range(B):
                    ch.link(v.match_replace(wk[:, b, :], top8[:, b, :], pr[:, b, :], -2.0))
                ch.link(v.tensor_tensor(wk[:, :, :], wk[:, :, :], pr[:, :, :], ALU.not_equal))
                ch.link(v.tensor_tensor(wk[:, :, :], wk[:, :, :], pr[:, :, :], ALU.mult))
                ch.link(v.tensor_reduce(red[:, :], wk[:, :, :], AX.X, ALU.add))
                ch.link(v.reciprocal(red[:, :], red[:, :]))
                ch.link(v.memset(cw[:, :, E1:E1 + 2], 1.0))
                ch.link(v.tensor_tensor(cw[:, :, 0:E1], wk[:, :, :], wide(red[:, :]), ALU.mult))
            src = cw[:, :, 0:full]
            for part in range(3):
                last = v.tensor_copy(cw3[:, :, part, 0:full], src)
                if part == 2:
                    last.then_inc(s.cw_done, 1)
                    break
                ch.link(last)
                ch.link(v.tensor_tensor(cr[:, :, 0:full], src, cw3[:, :, part, 0:full], ALU.subtract))
                src = cr[:, :, 0:full]

        def loop_tiles(eng, J, body):
            body(0, 0, 0)
            body(1, 1, 0)
            pairs = (J - 2) // 2
            with eng.Fori(0, pairs) as i:
                body(2 * i + 2, 0, i + 1)
                body(2 * i + 3, 1, i + 1)
            if J % 2:
                body(J - 1, 0, pairs + 1)

        def acc(half, c):
            return PS[:, 4 + 2 * half + c, :]

        def open_acc(value):
            for i in range(4):
                m = nc.tensor.matmul(PS[:, 4 + i, :], zeros[:, 0:P], zeros[:, :], start=not value, stop=value, skip_group_check=True)
            return m

        def experts_pe(pe, L, J):
            s = fs[L]
            open_acc(False)
            pe.wait_ge(s.cwt_ready, 1)

            def down(u, half, par):
                pe.wait_ge(s.lo_done, u + 1)
                for c in range(C):
                    w0 = 2 * D + c * P
                    m = three(pe, acc(half, c), wh[par][:, w0:w0 + P], wl[par][:, w0:w0 + P], hhh[half][:, :], hhl[half][:, :], False, False, skip_group_check=True)
                m.then_inc(s.d_done, 1)

            def tile(j, par, cnt):
                pe.wait_ge(s.w_split, 3 * j + 3)
                for half in range(2):
                    u = 2 * j + half
                    t0 = half * HALF
                    for mat, bank, done, free in ((0, 0, s.g_done, s.silu_done), (1, 1, s.u_done, s.a_done)):
                        after(pe, free, u)
                        for c in range(C):
                            w0 = mat * D + c * P
                            m = three(pe, PS[:, bank, :], wh[par][:, w0:w0 + P], wl[par][:, w0:w0 + P],
                                      tTh[:, c, t0:t0 + HALF], tTl[:, c, t0:t0 + HALF], c == 0, c == C - 1)
                        m.then_inc(done, 1)
                    after(pe, s.h_done, u)
                    nc.tensor.matmul(PS[:, 2, :], selj[par][:, :], cwT[:, t0:t0 + HALF], start=True, stop=True).then_inc(s.c_done, 1)
                    if half:
                        down(u - 1, 0, par)
                    elif not (isinstance(j, int) and j == 0):
                        down(u - 1, 1, 1 - par)

            loop_tiles(pe, J, tile)
            down(2 * J - 1, 1, (J - 1) % 2)
            open_acc(True).then_inc(s.acc_done, 1)

        def experts_act(act, L, J):
            s = fs[L]

            def tile(j, par, cnt):
                for half in range(2):
                    u = 2 * j + half
                    act.wait_ge(s.g_done, u + 1)
                    after(act, s.a_done, u - 1)
                    nc.scalar.activation(act_s[half][:, :], PS[:, 0, :], ACT.Silu).then_inc(s.silu_done, 1)
                    act.wait_ge(s.h_done, u + 1)
                    after(act, s.d_done, u - 1)
                    nc.scalar.activation(hhh[half][:, :], hh[half][:, :], ACT.Copy).then_inc(s.hi_done, 1)

            loop_tiles(act, J, tile)

        def experts_dve(dve, L, J):
            s = fs[L]

            def tile(j, par, cnt):
                for half in range(2):
                    u = 2 * j + half
                    dve.wait_ge(s.u_done, u + 1)
                    dve.wait_ge(s.silu_done, u + 1)
                    nc.vector.tensor_tensor(act_s[half][:, :], act_s[half][:, :], PS[:, 1, :], ALU.mult).then_inc(s.a_done, 1)
                    dve.wait_ge(s.a_done, u + 1)
                    dve.wait_ge(s.c_done, u + 1)
                    nc.vector.tensor_tensor(hh[half][:, :], act_s[half][:, :], PS[:, 2, :], ALU.mult).then_inc(s.h_done, 1)
                    dve.wait_ge(s.hi_done, u + 1)
                    split_lo(hhl[half][:, :], hh[half][:, :], hhh[half][:, :]).then_inc(s.lo_done, 1)

            loop_tiles(dve, J, tile)

        def experts_pool(pool, L, J, start=0):
            s = fs[L]

            def tile(j, par, cnt):
                pool_wait(pool, (s.w_in, s.w_in1)[par], 16 * cnt + 16)
                if not (isinstance(j, int) and j == 0):
                    pool_wait(pool, s.d_done, 2 * j - 2)
                nc.gpsimd.tensor_copy(wh[par][:, :], wraw[par][:, :]).then_inc(s.w_split, 1)
                nc.gpsimd.tensor_copy(selj[par][:, :], sel[:, bass.ds(j * P, P)]).then_inc(s.w_split, 1)
                pool_wait(pool, s.w_split, 3 * j + 2)
                nc.gpsimd.tensor_tensor(wl[par][:, :], wraw[par][:, :], wh[par][:, :].bitcast(F32), ALU.subtract).then_inc(s.w_split, 1)

            loop_tiles(pool, J, tile)

        def experts_sp(sp, L, J, w_d):
            s = fs[L]

            def tile(j, par, cnt):
                after(sp, s.w_split, 3 * j - 3)
                sp.dma_start(wraw[par][:, :], w_d[bass.ds(j, 1), :, :].rearrange("a p n -> (a p) n")).then_inc((s.w_in, s.w_in1)[par], 16)

            loop_tiles(sp, J, tile)

        def rows_pe(pe, acc_ready, done, free):
            pe.wait_ge(acc_ready, 4)
            for b in range(B):
                after(pe, free, b - 1)
                for c in range(C):
                    m = nc.tensor.transpose(PS[:, b % 2, c * P:(c + 1) * P], yT[:, c, b * S:(b + 1) * S], ident[:, :])
                m.then_inc(done, 1)

        def acc_act(act, acc_done, out):
            for half in range(2):
                for c in range(C):
                    act.wait_ge(acc_done, 1)
                    nc.scalar.activation(yT[:, c, half * HALF:(half + 1) * HALF], acc(half, c), ACT.Copy).then_inc(out, 1)

        PRE_RING, PER_RING, PER_HI = 6, 12, 10

        def attn_pe(pe):
            def use(r):
                after(pe, ring_free, r - 3)

            def proj(h, par, which, half, r, si):
                use(r)
                pe.wait_ge(aw_split, 4 * h + 2)
                w, bank = which * D, PS[:, si % 4, :]
                if which < 2:
                    for c in range(C):
                        m = three(pe, bank, ah[par][:, w + c * P:w + (c + 1) * P], al[par][:, w + c * P:w + (c + 1) * P],
                                  tTh[:, c, half * HALF:(half + 1) * HALF], tTl[:, c, half * HALF:(half + 1) * HALF], c == 0, c == C - 1)
                else:
                    for t in range(4):
                        t0 = half * HALF + t * S
                        for c in range(C):
                            m = three(pe, bank[:, t * S:(t + 1) * S], tTh[:, c, t0:t0 + S], tTl[:, c, t0:t0 + S],
                                      ah[par][:, w + c * P:w + (c + 1) * P], al[par][:, w + c * P:w + (c + 1) * P], c == 0, c == C - 1)
                m.then_inc(ring_done, 1)

            def pairs(lh, ll, rh, rl, half, r, si):
                use(r)
                for t in range(4):
                    a0 = half * HALF + t * S
                    m = three(pe, PS[:, si % 4, t * S:(t + 1) * S], lh[:, a0:a0 + S], ll[:, a0:a0 + S], rh[:, a0:a0 + S], rl[:, a0:a0 + S], True, True)
                m.then_inc(ring_done, 1)

            def wo(h, par):
                pe.wait_ge(aw_split, 4 * h + 4)
                for half in range(2):
                    for c in range(C):
                        w0 = 3 * D + c * P
                        m = three(pe, acc(half, c), ah[par][:, w0:w0 + P], al[par][:, w0:w0 + P],
                                  oTh[:, half * HALF:(half + 1) * HALF], oTl[:, half * HALF:(half + 1) * HALF], False, False, skip_group_check=True)
                m.then_inc(wo_done, 1)

            def head(h, par, first, last):
                r, si = PRE_RING + h * PER_RING, PRE_RING
                n = 1 - par
                pe.wait_ge(ring_free, r)
                pairs(qTh[par], qTl[par], kTh[par], kTl[par], 0, r, si)
                if last:
                    pairs(qTh[par], qTl[par], kTh[par], kTl[par], 1, r + 1, si + 1)
                    wo(h - 1, n)
                    at, vt = 2, 4
                else:
                    proj(h + 1, n, 0, 0, r + 1, si + 1)
                    pairs(qTh[par], qTl[par], kTh[par], kTl[par], 1, r + 2, si + 2)
                    proj(h + 1, n, 0, 1, r + 3, si + 3)
                    if not first:
                        wo(h - 1, n)
                    proj(h + 1, n, 1, 0, r + 4, si + 4)
                    proj(h + 1, n, 1, 1, r + 5, si + 5)
                    at, vt = 6, 10
                for half in range(2):
                    use(r + at + half)
                    pe.wait_ge(norm_done, 2 * h + half + 1)
                    for t in range(4):
                        m = nc.tensor.transpose(PS[:, (si + at + half) % 4, t * S:(t + 1) * S], sm[:, 4 * half + t, :], ident[:, :])
                    m.then_inc(ring_done, 1)
                if not last:
                    proj(h + 1, n, 2, 0, r + 8, si + 8)
                    proj(h + 1, n, 2, 1, r + 9, si + 9)
                for half in range(2):
                    pe.wait_ge(ring_free, r + at + half + 1)
                    pairs(vh[par], vl[par], pTh, pTl, half, r + vt + half, si + vt + half)

            open_acc(False)
            pe.wait_ge(tlo_done, B)
            for i, (which, half) in enumerate(((0, 0), (0, 1), (1, 0), (1, 1), (2, 0), (2, 1))):
                proj(0, 0, which, half, i, i)
            head(0, 0, True, False)
            with pe.Fori(0, (AH - 2) // 2) as i:
                h = 2 * i + 1
                head(h, 1, False, False)
                head(h + 1, 0, False, False)
            head(AH - 1, 1, False, True)
            pe.wait_ge(ring_free, PRE_RING + (AH - 1) * PER_RING + 6)
            wo(AH - 1, 1)
            open_acc(True).then_inc(wo_done, 1)

        def attn_act(act):
            def hi(dst, half, r, si):
                act.wait_ge(ring_done, r + 1)
                nc.scalar.activation(dst[:, half * HALF:(half + 1) * HALF], PS[:, si % 4, :], ACT.Copy).then_inc(ahi_done, 1)

            def exps(h, half):
                act.wait_ge(masked, 2 * h + half + 1)
                for t in range(4):
                    b = 4 * half + t
                    nc.scalar.activation(sm[:, b, :], sm[:, b, :], ACT.Exp, bias=nmx[:, b:b + 1], scale=AD ** -0.5,
                                         accum_out=sums[:, b:b + 1]).then_inc(aexp_done, 1)

            def head(h, par, last):
                r, si, n = PRE_RING + h * PER_RING, PRE_RING, 1 - par
                if last:
                    exps(h, 0)
                    exps(h, 1)
                    at, vt = 2, 4
                else:
                    exps(h, 0)
                    hi(qTh[n], 0, r + 1, si + 1)
                    exps(h, 1)
                    hi(qTh[n], 1, r + 3, si + 3)
                    hi(kTh[n], 0, r + 4, si + 4)
                    hi(kTh[n], 1, r + 5, si + 5)
                    at, vt = 6, 10
                for half in range(2):
                    hi(pTh, half, r + at + half, si + at + half)
                if not last:
                    hi(vh[n], 0, r + 8, si + 8)
                    hi(vh[n], 1, r + 9, si + 9)
                for half in range(2):
                    hi(oTh, half, r + vt + half, si + vt + half)

            for i, (dst, half) in enumerate(((qTh, 0), (qTh, 1), (kTh, 0), (kTh, 1), (vh, 0), (vh, 1))):
                hi(dst[0], half, i, i)
            head(0, 0, False)
            with act.Fori(0, (AH - 2) // 2) as i:
                h = 2 * i + 1
                head(h, 1, False)
                head(h + 1, 0, False)
            head(AH - 1, 1, True)

        def attn_dve(dve, ch):
            v = nc.vector

            def lo(h_, l_, half, hc, si):
                dve.wait_ge(ahi_done, hc)
                a0 = half * HALF
                split_lo(l_[:, a0:a0 + HALF], PS[:, si % 4, :], h_[:, a0:a0 + HALF]).then_inc(ring_free, 1)

            def mask(h, half, r, si):
                dve.wait_ge(ring_done, r + 1)
                part = sm[:, 4 * half:4 * half + 4, :]
                v.tensor_tensor(part, PS[:, si % 4, :].rearrange("p (t s) -> p t s", s=S),
                                causal[:, :].unsqueeze(1).broadcast_to([P, 4, S]), ALU.add).then_inc(ring_free, 1)
                dve.wait_ge(ring_free, r + 1)
                m4 = nmx[:, 4 * half:4 * half + 4]
                ch.link(v.tensor_reduce(m4, part, AX.X, ALU.max))
                v.tensor_scalar(m4, m4, -(AD ** -0.5), None, ALU.mult).then_inc(masked, 1)

            def norm(h, half):
                dve.wait_ge(aexp_done, 8 * h + 4 * half + 4)
                part = sm[:, 4 * half:4 * half + 4, :]
                r4 = rsum[:, 4 * half:4 * half + 4]
                ch.link(v.reciprocal(r4, sums[:, 4 * half:4 * half + 4]))
                v.tensor_tensor(part, part, r4.unsqueeze(2).broadcast_to([P, 4, S]), ALU.mult).then_inc(norm_done, 1)

            def head(h, par, last):
                r, si, n = PRE_RING + h * PER_RING, PRE_RING, 1 - par
                hc = PRE_RING + h * PER_HI
                if last:
                    mask(h, 0, r, si)
                    mask(h, 1, r + 1, si + 1)
                    norm(h, 0)
                    norm(h, 1)
                    at, vt, hc = 2, 4, hc - 4
                else:
                    mask(h, 0, r, si)
                    lo(qTh[n], qTl[n], 0, hc + 1, si + 1)
                    mask(h, 1, r + 2, si + 2)
                    lo(qTh[n], qTl[n], 1, hc + 2, si + 3)
                    norm(h, 0)
                    lo(kTh[n], kTl[n], 0, hc + 3, si + 4)
                    norm(h, 1)
                    lo(kTh[n], kTl[n], 1, hc + 4, si + 5)
                    at, vt = 6, 10
                for half in range(2):
                    lo(pTh, pTl, half, hc + 5 + half, si + at + half)
                if not last:
                    lo(vh[n], vl[n], 0, hc + 7, si + 8)
                    lo(vh[n], vl[n], 1, hc + 8, si + 9)
                for half in range(2):
                    lo(oTh, oTl, half, hc + (7 if last else 9) + half, si + vt + half)

            for i, (h_, l_, half) in enumerate(((qTh, qTl, 0), (qTh, qTl, 1), (kTh, kTl, 0), (kTh, kTl, 1), (vh, vl, 0), (vh, vl, 1))):
                lo(h_[0], l_[0], half, i + 1, i)
            head(0, 0, False)
            start = ch.base + ch.n
            with dve.Fori(0, (AH - 2) // 2) as i:
                h = 2 * i + 1
                ch.base, ch.n = start + i * 8, 0
                head(h, 1, False)
                head(h + 1, 0, False)
            ch.leave(start, 8, (AH - 2) // 2)
            head(AH - 1, 1, True)

        def attn_pool(pool):
            def split(h, par, a0, a1, k):
                nc.gpsimd.tensor_copy(ah[par][:, a0:a1], araw[par][:, a0:a1]).then_inc(aw_split, 1)
                pool_wait(pool, aw_split, 4 * h + k + 1)
                nc.gpsimd.tensor_tensor(al[par][:, a0:a1], araw[par][:, a0:a1], ah[par][:, a0:a1].bitcast(F32), ALU.subtract).then_inc(aw_split, 1)

            def head(h, par, cnt, first=False):
                pool_wait(pool, aw_in[par], 16 * cnt + 16)
                if not first:
                    pool_wait(pool, ring_done, PRE_RING + (h - 2) * PER_RING)
                split(h, par, 0, 3 * D, 0)
                if not first:
                    pool_wait(pool, wo_done, h - 1)
                split(h, par, 3 * D, 4 * D, 2)

            head(0, 0, 0, True)
            head(1, 1, 0, True)
            with pool.Fori(1, AH // 2) as i:
                head(2 * i, 0, i)
                head(2 * i + 1, 1, i)

        def attn_sp(sp):
            def head(h, par, src):
                after(sp, aw_split, 4 * h - 4)
                sp.dma_start(araw[par][:, :], src).then_inc(aw_in[par], 16)

            head(0, 0, attn_d[0])
            head(1, 1, attn_d[1])
            with sp.Fori(1, AH // 2) as i:
                for par in range(2):
                    head(2 * i + par, par, attn_d[bass.ds(2 * i + par, 1), :, :].rearrange("a p n -> (a p) n"))

        Js = (J0, J1)
        Is = (I0, I1)

        @block.sync
        def _(sp):
            sp.dma_start(X[:, :, :], x_d.rearrange("b s d -> s b d")).then_inc(x_in, 16)
            sp.dma_start(WXraw[:, :, :], wx_d[0]).then_inc(wx_in[0], 16)
            sp.dma_start(ctxT[:, :, :, :], ctx_d).then_inc(ctx_in, 16)
            sp.dma_start(vecs[:, :, :].rearrange("p a d -> p (a d)"), vec_d.partition_broadcast(P)).then_inc(vec_in, 16)
            sp.dma_start(gates[:, :], gate_d.partition_broadcast(P)).then_inc(vec_in, 16)
            sp.dma_start(rw[:, :, 0:E0], rw0_d).then_inc(vec_in, 16)
            sp.dma_start(rw[:, :, E0:E0 + E1], rw1_d).then_inc(vec_in, 16)
            sp.wait_ge(wx_split, 2)
            sp.dma_start(WXraw[:, :, :], wx_d[1]).then_inc(wx_in[1], 16)
            barrier(sp, 1)
            experts_sp(sp, 0, J0, moe0_d)
            barrier(sp, 2)
            barrier(sp, 3)
            attn_sp(sp)
            barrier(sp, 4)
            experts_sp(sp, 1, J1, moe1_d)
            for b in range(B):
                sp.wait_ge(fs[1].tile_out, b + 1)
                sp.dma_start(out_d[b], X[:, b, :]).then_inc(out_done, 16)
            sp.wait_ge(out_done, 16 * B)

        @block.gpsimd
        def _(pool):
            gp = nc.gpsimd
            gp.memset(ident[:, :], 0.0).then_inc(pool_chain, 1)
            gp.memset(identb[:, :], 0.0).then_inc(pool_chain, 1)
            pool.wait_ge(pool_chain, 2)
            for m in (ident, identb):
                gp.affine_select(out=m[:, :], in_=m[:, :], compare_op=ALU.not_equal, fill=1.0, base=0,
                                 pattern=[[-1, P]], channel_multiplier=1).then_inc(const_done, 1)
            pool.wait_ge(wx_in[0], 16)
            for L in range(2):
                if L:
                    pool.wait_ge(wx_in[1], 16)
                gp.tensor_copy(WXh[L][:, :, :], WXraw[:, :, :]).then_inc(wx_split, 1)
                pool.wait_ge(wx_split, 2 * L + 1)
                gp.tensor_tensor(WXl[L][:, :, :], WXraw[:, :, :], WXh[L][:, :, :].bitcast(F32), ALU.subtract).then_inc(wx_split, 1)
                if L == 0:
                    xattn_pool(pool, 0)
            pool.wait_ge(vec_in, 64)
            gp.tensor_copy(rwh[:, :, :], rw[:, :, :]).then_inc(rw_split, 1)
            pool.wait_ge(rw_split, 1)
            gp.tensor_tensor(rwl[:, :, :], rw[:, :, :], rwh[:, :, :].bitcast(F32), ALU.subtract).then_inc(rw_split, 1)
            barrier(pool, 1)
            for L in range(2):
                power(pool, 2 + 4 * L)
                n, I, J = (E0, E1 + 2)[L], Is[L], Js[L]
                gp.memset(sel[:, :], 1.0).then_inc(pool_chain, 1)
                k = 3 + L * 3
                pool.wait_ge(pool_chain, k)
                for step, (base, sign) in enumerate(((0, 1), (I - 1, -1))):
                    for part in range(3):
                        v = sel[32 * part:32 * part + 32, 0:J * P]
                        i = gp.affine_select(out=v, in_=v, compare_op=ALU.is_ge, fill=0.0, base=base,
                                             pattern=[[sign, J * P]], channel_multiplier=-sign * I)
                    i.then_inc(pool_chain, 1)
                    pool.wait_ge(pool_chain, k + step + 1)
                experts_pool(pool, L, J)
                if L == 0:
                    barrier(pool, 2)
                    xattn_pool(pool, 1)
                    barrier(pool, 3)
                    power(pool, 4)
                    power(pool, 5)
                    gp.memset(causal[:, :], 0.0).then_inc(const_done, 1)
                    pool.wait_ge(const_done, 3)
                    gp.affine_select(out=causal[:, :], in_=causal[:, :], compare_op=ALU.is_ge, fill=NEG, base=0,
                                     pattern=[[-1, S]], channel_multiplier=1).then_inc(const_done, 1)
                    attn_pool(pool)
                    barrier(pool, 4)

        @block.scalar
        def _(act):
            act.wait_ge(vec_in, 64)
            nc.scalar.activation(tg[:, :], gates[:, :], ACT.Tanh).then_inc(tg_done, 1)
            xattn_act(act, 0)
            barrier(act, 1)
            columns_act(act, fs[0].t_done, fs[0].thi)
            route_act(act, 0)
            experts_act(act, 0, J0)
            acc_act(act, fs[0].acc_done, fs[0].y_out)
            barrier(act, 2)
            xattn_act(act, 1)
            barrier(act, 3)
            columns_act(act, t_done, thi_done)
            attn_act(act)
            for half in range(2):
                for c in range(C):
                    act.wait_ge(wo_done, AH + 1)
                    nc.scalar.activation(ayT[:, c, half * HALF:(half + 1) * HALF], acc(half, c), ACT.Copy).then_inc(ay_out, 1)
            barrier(act, 4)
            columns_act(act, fs[1].t_done, fs[1].thi)
            route_act(act, 1)
            experts_act(act, 1, J1)
            acc_act(act, fs[1].acc_done, fs[1].y_out)

        @block.tensor
        def _(pe):
            pe.wait_ge(const_done, 2)
            xattn_pe(pe, 0)
            barrier(pe, 1)
            columns_pe(pe, fxn, fs[0].n_done, fs[0].t_done, fs[0].tlo)
            route_pe(pe, 0)
            experts_pe(pe, 0, J0)
            rows_pe(pe, fs[0].y_out, fs[0].yt_done, fs[0].y_free)
            barrier(pe, 2)
            xattn_pe(pe, 1)
            barrier(pe, 3)
            columns_pe(pe, gxn, n_done, t_done, tlo_done)
            attn_pe(pe)
            pe.wait_ge(ay_out, 4)
            for b in range(B):
                after(pe, ay_free, b - 1)
                for c in range(C):
                    m = nc.tensor.transpose(PS[:, b % 2, c * P:(c + 1) * P], ayT[:, c, b * S:(b + 1) * S], ident[:, :])
                m.then_inc(ayt_done, 1)
            barrier(pe, 4)
            columns_pe(pe, fxn, fs[1].n_done, fs[1].t_done, fs[1].tlo)
            route_pe(pe, 1)
            experts_pe(pe, 1, J1)
            rows_pe(pe, fs[1].y_out, fs[1].yt_done, fs[1].y_free)

        @block.vector
        def _(dve):
            v = nc.vector
            ch = Chain(dve, dve_chain)
            ch.link(v.memset(zeros[:, :].bitcast(F32), 0.0))
            ch.link(v.memset(mhalf[:, :], -0.5))
            for i in range(2):
                ch.link(v.memset(v17[i][:, :, :], 1.0))
            for e in range(E0):
                ch.link(v.memset(rank8[:, e:e + 1], float(E0 - e)))
            dve.wait_ge(x_in, 16)
            dve.wait_ge(vec_in, 64)
            dve.wait_ge(tg_done, 1)
            xattn_dve(dve, 0, ch)
            barrier(dve, 1)

            def normed(b, s_n, s_hi, s_lo, make):
                make(b)
                if b:
                    columns_lo(dve, b - 1, s_hi, s_lo)
                if b == B - 1:
                    columns_lo(dve, b, s_hi, s_lo)

            s = fs[0]
            ln_stats(dve, ch, X, 2)
            for b in range(B):
                after(dve, s.t_done, b - 1)
                normed(b, s.n_done, s.thi, s.tlo, lambda b: ln_scale(fxn[b % 2][:, :], X[:, b, :], b).then_inc(s.n_done, 1))
            route_dve(dve, 0, ch)
            experts_dve(dve, 0, J0)
            for b in range(B):
                dve.wait_ge(s.yt_done, b + 1)
                v.scalar_tensor_tensor(out=X[:, b, :], in0=PS[:, b % 2, 0:D], scalar=tg[:, 2:3], in1=X[:, b, :], op0=ALU.mult, op1=ALU.add).then_inc(s.y_free, 1)
            dve.wait_ge(s.y_free, B)
            barrier(dve, 2)
            for i in range(2):
                ch.link(v.memset(v17[i][:, :, :], 1.0))
            xattn_dve(dve, 1, ch)
            barrier(dve, 3)

            ln_stats(dve, ch, X, 4)
            for b in range(B):
                ch.link(ln_scale(Z[:, b, :], X[:, b, :], b))

            def row_scales(use, tmp):
                for b in range(B):
                    scale = mean_square(Z[:, b, :], tmp[:, :], ms[:, b:b + 1])
                    if b < B - 1:
                        ch.link(scale)
                scale.then_inc(stats_done, 1)
                dve.wait_ge(rstd_done, use)

            def scaled(out, b, weight):
                return v.scalar_tensor_tensor(out=out[b % 2][:, :], in0=Z[:, b, :], scalar=rstd[:, b:b + 1], in1=vec(weight), op0=ALU.mult, op1=ALU.mult)

            row_scales(5, gjunk)
            for b in range(B):
                after(dve, t_done, b - 1)
                normed(b, n_done, thi_done, tlo_done, lambda b: scaled(gxn, b, "ln1").then_inc(n_done, 1))
            dve.wait_ge(const_done, 4)
            attn_dve(dve, ch)
            for b in range(B):
                dve.wait_ge(ayt_done, b + 1)
                v.tensor_tensor(Z[:, b, :], PS[:, b % 2, 0:D], Z[:, b, :], ALU.add).then_inc(ay_free, 1)
            dve.wait_ge(ay_free, B)
            barrier(dve, 4)
            s = fs[1]
            row_scales(6, fjunk)
            for b in range(B):
                after(dve, s.t_done, b - 1)
                normed(b, s.n_done, s.thi, s.tlo, lambda b: scaled(fxn, b, "ln2").then_inc(s.n_done, 1))
            route_dve(dve, 1, ch)
            experts_dve(dve, 1, J1)
            for b in range(B):
                dve.wait_ge(s.yt_done, b + 1)
                v.tensor_tensor(Z[:, b, :], PS[:, b % 2, 0:D], Z[:, b, :], ALU.add).then_inc(s.y_free, 1)
                dve.wait_ge(s.y_free, b + 1)
                v.scalar_tensor_tensor(out=X[:, b, :], in0=Z[:, b, :], scalar=tg[:, 3:4], in1=X[:, b, :], op0=ALU.mult, op1=ALU.add).then_inc(s.tile_out, 1)


def kernel(**inputs):
    import numpy as np
    import concourse.bacc as bacc
    from concourse.bass_utils import run_bass_kernel_spmd

    a = {k: np.asarray(v) for k, v in inputs.items()}

    def columns(m):
        return m.reshape(C, P, -1).transpose(1, 0, 2)

    def cross(k, v, q, o):
        return columns(np.concatenate([m.T for m in (k, v, q, o)], axis=1))

    def expert_tiles(gate, up, down, J):
        pad = ((0, J * P - gate.shape[0]), (0, 0))
        g, u, d = (np.pad(m, pad) for m in (gate, up, down))
        cols = [m.reshape(J, P, C, P).transpose(0, 3, 2, 1).reshape(J, P, D) for m in (g, u)]
        return np.concatenate(cols + [d.reshape(J, P, D)], axis=2)

    def rows_of(w):
        return w.transpose(0, 2, 1).reshape(-1, D)

    heads = [a["L1_ffn_" + k].reshape(C, P, AH, AD).transpose(2, 1, 0, 3).reshape(AH, P, D) for k in ("wq", "wk", "wv")]
    arrays = {
        "ctx": a["ctx_2048"].transpose(2, 0, 1).reshape(C, P, B, S).transpose(1, 2, 0, 3),
        "x": a["x"],
        "wx": np.stack([cross(*(a["L0_xattn_" + k] for k in ("Wk", "Wv", "Wq", "Wo"))),
                        cross(*(a["L1_xattn_" + k] for k in ("k_img_w", "v_img_w", "q_w", "o_w")))]),
        "vec": np.concatenate([a[k] for k in (
            "L0_xattn_bk", "L0_xattn_bv", "L0_xattn_bq", "L0_xattn_bo", "L1_xattn_k_img_b", "L1_xattn_v_img_b",
            "L1_xattn_q_b", "L1_xattn_o_b", "L1_xattn_norm_k_img_w", "L1_xattn_norm_q_w", "L1_ffn_ln1_w", "L1_ffn_ln2_w")]),
        "gate": np.concatenate([a["g_xattn"], a["g_ffn"]]),
        "rw0": columns(a["L0_ffn_router_w"]),
        "rw1": columns(a["L1_ffn_gate_w"].T),
        "moe0": expert_tiles(rows_of(a["L0_ffn_gate_w"]), rows_of(a["L0_ffn_up_w"]), a["L0_ffn_down_w"].reshape(-1, D), J0),
        "moe1": expert_tiles(np.concatenate([a["L1_ffn_eg_w"].reshape(-1, D), a["L1_ffn_sg_w"]]),
                             np.concatenate([a["L1_ffn_eu_w"].reshape(-1, D), a["L1_ffn_su_w"]]),
                             np.concatenate([a["L1_ffn_ed_w"].transpose(0, 2, 1).reshape(-1, D), a["L1_ffn_sd_w"].T]), J1),
        "attn": np.concatenate(heads + [a["L1_ffn_wo"].reshape(AH, P, D)], axis=2),
    }
    arrays = {k: np.ascontiguousarray(v) for k, v in arrays.items()}
    nc = bacc.Bacc("TRN2", target_bir_lowering=False, num_devices=1)
    aps = [nc.dram_tensor(k, v.shape, mybir.dt.from_np(v.dtype), kind="ExternalInput").ap() for k, v in arrays.items()]
    out = nc.dram_tensor("out", (B, S, D), F32, kind="ExternalOutput").ap()
    build(nc, *aps, out)
    return run_bass_kernel_spmd(nc, [arrays], core_ids=[0]).results[0]["out"]
```

```python
from contextlib import ExitStack

import concourse.bass as bass
from concourse import mybir

F32 = mybir.dt.float32
F32R = mybir.dt.float32r
BF16 = mybir.dt.bfloat16
ALU = mybir.AluOpType
ACT = mybir.ActivationFunctionType
AX = mybir.AxisListType

B, S, D = 8, 128, 256
P = 128
T = B * S
C = D // P
XH, XD = 16, 16
AH, AD = 16, 128
E0, I0 = 8, 512
E1, I1, SI = 16, 176, 352
TOPK = 6
HALF = T // 2
NEG = -3.0e38
LN_EPS, RMS_EPS = 1e-5, 1e-6
HT = P // XD
J0 = E0 * I0 // P
J1 = -(-(E1 * I1 + SI) // P)
VEC = ["bk0", "bv0", "bq0", "bo0", "bk1", "bv1", "bq1", "bo1", "nk1", "nq1", "ln1", "ln2"]


class Chain:

    def __init__(self, eng, sem):
        self.eng, self.sem, self.base, self.n = eng, sem, 0, 0

    def link(self, ins):
        self.n += 1
        ins.then_inc(self.sem, 1)
        self.eng.wait_ge(self.sem, self.base + self.n)

    def leave(self, start, steps, count):
        assert self.n == steps, (self.n, steps)
        self.base, self.n = start + count * steps, 0


def after(eng, sem, n):
    if isinstance(n, int) and n <= 0:
        return
    eng.wait_ge(sem, n)


def build(nc, ctx_d, x_d, wx_d, vec_d, gate_d, rw0_d, rw1_d, moe0_d, moe1_d, attn_d, out_d):
    stack = ExitStack()
    with stack:
        def sb(name, shape, dt=F32, where=None):
            return (where or stack).enter_context(nc.sbuf_tensor(name, shape, dt))

        def sem(name):
            return stack.enter_context(nc.semaphore(name))

        PS = stack.enter_context(nc.psum_tensor("PS", [P, 8, 512], F32))

        X = sb("X", [P, B, D])
        WX = [sb(f"WX{i}", [P, C, 4 * D]) for i in range(2)]
        head_rows = sb("head_rows", [P, HT])
        vecs = sb("vecs", [P, len(VEC), D])
        gates = sb("gates", [P, 4])
        tg = sb("tg", [P, 4])
        ident = sb("ident", [P, P])
        identb = sb("identb", [P, P], BF16)
        zeros = sb("zeros", [P, 512], F32R)
        rank8 = sb("rank8", [P, E0])
        rw = sb("rw", [P, C, E0 + E1])
        tT = sb("tT", [P, C, T])
        tTh = sb("tTh", [P, C, T], F32R)
        tTl = sb("tTl", [P, C, T], F32R)
        Z = sb("Z", [P, B, D])
        st = sb("st", [P, B, 6])
        mv = sb("mv", [P, B, 2])
        ms = sb("ms", [P, B])
        rstd = sb("rstd", [P, B])
        mhalf = sb("mhalf", [P, B])
        kms = sb("kms", [P, 4])

        def vec(name):
            return vecs[:, VEC.index(name), :]

        a = ExitStack()
        xn = sb("xn", [P, D], where=a)
        xT = sb("xT", [P, C, S], where=a)
        cT = [sb(f"cT{i}", [P, C, S], where=a) for i in range(2)]
        kvs = sb("kvs", [P, 2 * D], where=a)
        qs = sb("qs", [P, D], where=a)
        junk = sb("junk", [P, D], where=a)
        v17 = [sb(f"v17_{i}", [P, XH, XD + 1], where=a) for i in range(2)]
        k8T = [sb(f"k8T{i}", [P, C, HT, S], where=a) for i in range(2)]
        qT = [sb(f"qT{i}", [P, C, S], where=a) for i in range(2)]
        prob = [sb(f"prob{i}", [P, XH, S], where=a) for i in range(2)]
        probT = sb("probT", [P, XH, S], where=a)
        mx = sb("mx", [P, XH], where=a)
        rden = sb("rden", [P, XH], where=a)
        cx = sb("cx", [P, XH, XD], where=a)
        cxT = sb("cxT", [P, C, S], where=a)
        otmp = sb("otmp", [P, D], where=a)
        a.close()
        f = ExitStack()
        rows = 3 * 32
        sel = sb("sel", [rows, J0 * P], BF16, f)
        selj = [sb(f"selj{i}", [rows, P], BF16, f) for i in range(2)]
        cwT = sb("cwT", [rows, T], BF16, f)
        wraw = [sb(f"wraw{i}", [P, 3 * D], where=f) for i in range(2)]
        wh = [sb(f"wh{i}", [P, 3 * D], F32R, f) for i in range(2)]
        wl = [sb(f"wl{i}", [P, 3 * D], F32R, f) for i in range(2)]
        act_s = [sb(f"act_s{i}", [P, HALF], where=f) for i in range(2)]
        hh = [sb(f"hh{i}", [P, HALF], where=f) for i in range(2)]
        hhh = [sb(f"hhh{i}", [P, HALF], F32R, f) for i in range(2)]
        hhl = [sb(f"hhl{i}", [P, HALF], F32R, f) for i in range(2)]
        yT = sb("yT", [P, C, T], where=f)
        lg = sb("lg", [P, B, E1], where=f)
        pr = sb("pr", [P, B, E1], where=f)
        wk = sb("wk", [P, B, E1], where=f)
        cw = sb("cw", [P, B, E1 + 2], where=f)
        cr = sb("cr", [P, B, E1 + 2], where=f)
        top8 = sb("top8", [P, B, 8], where=f)
        red = sb("red", [P, B], where=f)
        cw3 = sb("cw3", [P, B, 3, 32], BF16, f)
        fxn = [sb(f"fxn{i}", [P, D], where=f) for i in range(2)]
        fjunk = sb("fjunk", [P, D], where=f)
        f.close()
        g = ExitStack()
        ayT = sb("ayT", [P, C, T], where=g)
        araw = [sb(f"araw{i}", [P, 4 * D], where=g) for i in range(2)]
        ah = [sb(f"ah{i}", [P, 3 * D], F32R, g) for i in range(2)]
        al = [sb(f"al{i}", [P, 3 * D], F32R, g) for i in range(2)]
        qT_ = [sb(f"aqT{i}", [P, T], where=g) for i in range(2)]
        kT_ = [sb(f"akT{i}", [P, T], where=g) for i in range(2)]
        v_ = [sb(f"av{i}", [P, T], where=g) for i in range(2)]
        sm = sb("sm", [P, B, S], where=g)
        pT = sb("pT", [P, T], where=g)
        oTh = sb("oTh", [P, T], F32R, g)
        oTl = sb("oTl", [P, T], F32R, g)
        nmx = sb("nmx", [P, B], where=g)
        sums = sb("sums", [P, B], where=g)
        rsum = sb("rsum", [P, B], where=g)
        causal = sb("causal", [P, S], where=g)
        gxn = [sb(f"gxn{i}", [P, D], where=g) for i in range(2)]
        gjunk = sb("gjunk", [P, D], where=g)
        g.close()

        x_in, vec_in, out_done = sem("x_in"), sem("vec_in"), sem("out_done")
        wx_in = sem("wx_in")
        const_done, tg_done = sem("const_done"), sem("tg_done")
        pool_turns, stats_done, rstd_done = sem("pool_turns"), sem("stats_done"), sem("rstd_done")
        dve_chain, pool_chain = sem("dve_chain"), sem("pool_chain")
        phase_end = sem("phase_end")

        class Xs:
            def __init__(s, n):
                s.ln_done = sem(f"x{n}_ln_done")
                s.small_done = sem(f"x{n}_small_done")
                s.act_free = sem(f"x{n}_act_free")
                s.dve_free = sem(f"x{n}_dve_free")
                s.tr_done = sem(f"x{n}_tr_done")
                s.tr_free = sem(f"x{n}_tr_free")
                s.k_ready = sem(f"x{n}_k_ready")
                s.q_ready = sem(f"x{n}_q_ready")
                s.v_ready = sem(f"x{n}_v_ready")
                s.normed = sem(f"x{n}_normed")
                s.pool_steps = sem(f"x{n}_pool_steps")
                s.scores_done = sem(f"x{n}_scores_done")
                s.sub_done = sem(f"x{n}_sub_done")
                s.exp_done = sem(f"x{n}_exp_done")
                s.ctx_in = [sem(f"x{n}_ctx_in{i}") for i in range(2)]

        class Fs:
            def __init__(s, n):
                s.n_done = sem(f"f{n}_n_done")
                s.t_done = sem(f"f{n}_t_done")
                s.thi = sem(f"f{n}_thi")
                s.tlo = sem(f"f{n}_tlo")
                s.lg_done = sem(f"f{n}_lg_done")
                s.lg_out = sem(f"f{n}_lg_out")
                s.ex_done = sem(f"f{n}_ex_done")
                s.cw_done = sem(f"f{n}_cw_done")
                s.ct_done = sem(f"f{n}_ct_done")
                s.cwt_ready = sem(f"f{n}_cwt_ready")
                s.w_in = sem(f"f{n}_w_in")
                s.w_in1 = sem(f"f{n}_w_in1")
                s.w_split = sem(f"f{n}_w_split")
                s.g_done = sem(f"f{n}_g_done")
                s.u_done = sem(f"f{n}_u_done")
                s.c_done = sem(f"f{n}_c_done")
                s.d_done = sem(f"f{n}_d_done")
                s.silu_done = sem(f"f{n}_silu_done")
                s.a_done = sem(f"f{n}_a_done")
                s.h_done = sem(f"f{n}_h_done")
                s.hi_done = sem(f"f{n}_hi_done")
                s.lo_done = sem(f"f{n}_lo_done")
                s.acc_done = sem(f"f{n}_acc_done")
                s.y_out = sem(f"f{n}_y_out")
                s.yt_done = sem(f"f{n}_yt_done")
                s.y_free = sem(f"f{n}_y_free")
                s.tile_out = sem(f"f{n}_tile_out")

        xs = [Xs(0), Xs(1)]
        fs = [Fs(0), Fs(1)]
        n_done, t_done, thi_done, tlo_done = (sem("n_" + k) for k in ("n_done", "t_done", "thi_done", "tlo_done"))
        aw_in = [sem("aw_in0"), sem("aw_in1")]
        aw_split, ring_done, ring_act, ring_dve, ahi_done = (
            sem(k) for k in ("aw_split", "ring_done", "ring_act", "ring_dve", "ahi_done"))
        masked, aexp_done, norm_done, wo_done = (sem(k) for k in ("masked", "aexp_done", "norm_done", "wo_done"))
        ay_out, ayt_done, ay_free = (sem(k) for k in ("ay_out", "ayt_done", "ay_free"))

        block = stack.enter_context(nc.Block())

        def pool_wait(pool, sm_, n):
            after(pool, sm_, n)
            if not isinstance(n, int):
                pool.sem_inc(pool_turns, 1)

        def barrier(eng, k):
            eng.drain().then_inc(phase_end, 1)
            eng.wait_ge(phase_end, 5 * k)

        def three(pe, out, wh_, wl_, xh_, xl_, first, last, **kw):
            nc.tensor.matmul(out, wh_, xh_, start=first, stop=False, **kw)
            nc.tensor.matmul(out, wh_, xl_, start=False, stop=False, **kw)
            return nc.tensor.matmul(out, wl_, xh_, start=False, stop=last, **kw)

        PRE_SMALL, PER_SMALL, PRE_A, PER_A, PRE_D, PER_D = 11, 7, 5, 3, 6, 4
        FULL = B - 3
        LOOPED = FULL // 2 * 2

        def counts(n, par):
            if isinstance(n, int) and n > FULL:
                short = n - FULL
                k = PRE_SMALL + FULL * PER_SMALL + 3 * short + 1
                return k, k, PRE_A + PER_A * FULL + short + 1, PRE_D + PER_D * FULL + 2 * short
            k = PRE_SMALL + n * PER_SMALL
            return k, PRE_SMALL + par * PER_SMALL, PRE_A + n * PER_A, PRE_D + n * PER_D

        def parts_of(n):
            return [not isinstance(n, int) or n + ahead < B for ahead in (1, 2, 3)]

        def small(i):
            return PS[:, 6 + i % 2, :]

        def xattn_pe(pe, L):
            s = xs[L]
            W = WX[L]

            def t1(b, si):
                pe.wait_ge(s.ln_done, b + 1)
                for c in range(C):
                    m = nc.tensor.transpose(small(si)[:, c * P:(c + 1) * P], xn[:, c * P:(c + 1) * P], ident[:, :])
                m.then_inc(s.small_done, 1)

            def proj(cols, w0, n, si):
                for c in range(C):
                    m = nc.tensor.matmul(small(si)[:, 0:n], cols[:, c, :], W[:, c, w0:w0 + n], start=(c == 0), stop=(c == C - 1))
                m.then_inc(s.small_done, 1)

            def kv(par, loads, si):
                pe.wait_ge(s.ctx_in[par], 16 * loads)
                proj(cT[par], 0, 2 * D, si)

            def t2(b, si):
                if L:
                    pe.wait_ge(s.normed, 2 * b + 2)
                for i, src in enumerate((kvs, qs)):
                    for c in range(C):
                        m = nc.tensor.transpose(small(si)[:, (2 * i + c) * P:(2 * i + c + 1) * P], src[:, c * P:(c + 1) * P], ident[:, :])
                m.then_inc(s.small_done, 1)

            def scores(par, j):
                c = j // 2
                m = nc.tensor.matmul(PS[:, j, :], qT[par][:, c, :], k8T[par][:, c, 4 * (j % 2):4 * (j % 2) + 4, :], start=True, stop=True)
                if j % 2:
                    m.then_inc(s.scores_done, 1)

            def pt(n, par):
                for i in range(4):
                    if i % 2 == 0:
                        pe.wait_ge(s.exp_done, 2 * n + i // 2 + 1)
                    if i >= 2:
                        pe.wait_ge(s.tr_free, 4 * n + i - 1)
                    for t in range(4):
                        m = nc.tensor.transpose(PS[:, 4 + i % 2, t * P:(t + 1) * P], prob[par][:, 4 * i + t, :], ident[:, :])
                    m.then_inc(s.tr_done, 1)

            def pv(n, par, si, j):
                pe.wait_ge(s.tr_free, 4 * n + j + 1)
                o = small(si)[:, 0:XH * (XD + 1)].rearrange("p (h d) -> p h d", d=XD + 1)
                for h in range(4 * j, 4 * j + 4):
                    m = nc.tensor.matmul(o[:, h, :], probT[:, h, :], v17[par][:, h, :], start=True, stop=True)
                if j == 3:
                    m.then_inc(s.small_done, 1)

            def t3(si):
                for c in range(C):
                    m = nc.tensor.transpose(small(si)[:, c * P:(c + 1) * P], cx[:, :, :].rearrange("p h d -> p (h d)")[:, c * P:(c + 1) * P], ident[:, :])
                m.then_inc(s.small_done, 1)

            def sequence(n, par, loads=None):
                k, si, a, d = counts(n, par)
                has_s, has_t2, has_next = parts_of(n)
                pt(n, par)
                if has_t2:
                    pe.wait_ge(s.dve_free, d - 1)
                    t2(n + 2, si)
                    si, a = si + 1, a + 1
                pe.wait_ge(s.dve_free, d)
                pe.wait_ge(s.v_ready, n + 1)
                if has_s:
                    pe.wait_ge(s.sub_done, 2 * n + 2)
                for j in range(4):
                    if has_s:
                        scores(1 - par, j)
                    pv(n, par, si, j)
                if has_next:
                    pe.wait_ge(s.act_free, a)
                    t1(n + 3, si + 1)
                    pe.wait_ge(s.dve_free, d + 1)
                    kv(1 - par, loads, si + 2)
                    si, a, d = si + 2, a + 1, d + 1
                    pe.wait_ge(s.act_free, a)
                    t3(si + 1)
                    pe.wait_ge(s.dve_free, d + 1)
                    proj(xT, 2 * D, D, si + 2)
                    si = si + 1
                else:
                    pe.wait_ge(s.act_free, a)
                    pe.wait_ge(s.dve_free, d + 1)
                    t3(si + 1)
                pe.wait_ge(s.act_free, a + 1)
                proj(cxT, 3 * D, D, si + 2)

            pe.wait_ge(wx_in, 32)
            t1(0, 0)
            kv(0, 1, 1)
            pe.wait_ge(s.act_free, 1)
            proj(xT, 2 * D, D, 2)
            pe.wait_ge(s.dve_free, 2)
            t2(0, 3)
            t1(1, 4)
            pe.wait_ge(s.act_free, 2)
            kv(1, 1, 5)
            pe.wait_ge(s.act_free, 3)
            proj(xT, 2 * D, D, 6)
            pe.wait_ge(s.dve_free, 4)
            t2(1, 7)
            for j in range(4):
                scores(0, j)
            t1(2, 8)
            pe.wait_ge(s.act_free, 4)
            kv(0, 2, 9)
            pe.wait_ge(s.act_free, 5)
            proj(xT, 2 * D, D, 10)
            with pe.Fori(0, LOOPED // 2) as i:
                sequence(2 * i, 0, i + 2)
                sequence(2 * i + 1, 1, i + 3)
            for n in range(LOOPED, B):
                sequence(n, n % 2, (n + 3) // 2 + 1)

        def split_lo(lo, src, hi):
            return nc.vector.tensor_tensor(lo, src, hi.bitcast(F32), ALU.subtract)

        def xattn_act(act, L):
            s = xs[L]

            def copy_cols(si, k, dst):
                act.wait_ge(s.small_done, k + 1)
                nc.scalar.activation(dst[:, :, :].rearrange("p c s -> p (c s)"), small(si)[:, 0:D], ACT.Copy).then_inc(s.act_free, 1)

            def t2(si, k, par):
                act.wait_ge(s.small_done, k + 1)
                kc = small(si)[:, 0:D].rearrange("p (c s) -> p c s", c=C)
                for h in range(HT):
                    nc.scalar.activation(k8T[par][:, :, h, :], kc, ACT.Copy, scale=head_rows[:, h:h + 1])
                nc.scalar.activation(qT[par][:, :, :].rearrange("p c s -> p (c s)"), small(si)[:, D:2 * D], ACT.Copy).then_inc(s.act_free, 1)

            def exps(b, par, gq):
                act.wait_ge(s.sub_done, 2 * b + gq + 1)
                pr_ = prob[par][:, 8 * gq:8 * gq + 8, :]
                nc.scalar.activation(pr_, pr_, ACT.Exp, scale=XD ** -0.5).then_inc(s.exp_done, 1)

            def pt(n, i):
                act.wait_ge(s.tr_done, 4 * n + i + 1)
                nc.scalar.activation(probT[:, 4 * i:4 * i + 4, :].rearrange("p t s -> p (t s)"), PS[:, 4 + i % 2, :], ACT.Copy).then_inc(s.tr_free, 1)

            def sequence(n, par):
                k, si, _, _ = counts(n, par)
                has_s, has_t2, has_next = parts_of(n)
                for i in range(4):
                    pt(n, i)
                if has_t2:
                    t2(si, k, par)
                    k, si = k + 1, si + 1
                if has_s:
                    exps(n + 1, 1 - par, 0)
                if has_next:
                    copy_cols(si + 1, k + 1, xT)
                    k, si = k + 2, si + 2
                copy_cols(si + 1, k + 1, cxT)
                if has_s:
                    exps(n + 1, 1 - par, 1)

            copy_cols(0, 0, xT)
            t2(3, 3, 0)
            copy_cols(4, 4, xT)
            t2(7, 7, 1)
            exps(0, 0, 0)
            copy_cols(8, 8, xT)
            exps(0, 0, 1)
            with act.Fori(0, LOOPED // 2) as i:
                sequence(2 * i, 0)
                sequence(2 * i + 1, 1)
            for n in range(LOOPED, B):
                sequence(n, n % 2)

        def mean_square(src, tmp, dst):
            return nc.vector.tensor_tensor_reduce(out=tmp, in0=src, in1=src, scale=1.0 / D, scalar=RMS_EPS, op0=ALU.mult, op1=ALU.add, accum_out=dst)

        def ln_stats(dve, ch, src, use):
            for b in range(B):
                i = nc.vector.bn_stats(st[:, b, :], src[:, b, :])
            ch.link(i)
            for b in range(B):
                i = nc.vector.bn_aggr(mv[:, b, :], st[:, b, :])
            ch.link(i)
            nc.vector.tensor_scalar(ms[:, :].unsqueeze(2), mv[:, :, 1:2], LN_EPS, None, ALU.add).then_inc(stats_done, 1)
            dve.wait_ge(rstd_done, use)

        def ln_scale(out, src, b):
            return nc.vector.tensor_scalar(out, src, mv[:, b, 0:1], rstd[:, b:b + 1], ALU.subtract, ALU.mult)

        def power(pool, use):
            pool.wait_ge(stats_done, use)
            nc.gpsimd.tensor_tensor(rstd[:, :], ms[:, :], mhalf[:, :], ALU.pow).then_inc(rstd_done, 1)

        def xattn_dve(dve, L, ch):
            s = xs[L]

            def ln(b):
                nc.vector.tensor_scalar(xn[:, :], X[:, b, :], mv[:, bass.ds(b, 1), 0], rstd[:, bass.ds(b, 1)], ALU.subtract, ALU.mult).then_inc(s.ln_done, 1)

            def kv(b, si, k, d):
                dve.wait_ge(s.small_done, k + 1)
                after(dve, s.v_ready, b)
                nc.vector.tensor_tensor(kvs[:, :], small(si)[:, :], vecs[:, 4 * L:4 * L + 2, :].rearrange("p a d -> p (a d)"), ALU.add).then_inc(s.dve_free, 1)
                if L:
                    dve.wait_ge(s.dve_free, d + 1)
                    mean_square(kvs[:, 0:D], junk[:, :], kms[:, 0:1]).then_inc(s.k_ready, 1)

            def q(b, si, k, d):
                dve.wait_ge(s.small_done, k + 1)
                nc.vector.tensor_tensor(qs[:, :], small(si)[:, 0:D], vec(f"bq{L}"), ALU.add).then_inc(s.dve_free, 1)
                if L:
                    dve.wait_ge(s.dve_free, d + 1)
                    dve.wait_ge(s.k_ready, b + 1)
                    mean_square(qs[:, :], junk[:, :], kms[:, 1:2]).then_inc(s.q_ready, 1)

            def softmax(b, par, gq):
                dve.wait_ge(s.scores_done, 2 * b + gq + 1)
                sc = PS[:, 2 * gq:2 * gq + 2, :].rearrange("p a (t s) -> p (a t) s", s=S)
                m8 = mx[:, 8 * gq:8 * gq + 8]
                ch.link(nc.vector.tensor_reduce(m8, sc, AX.X, ALU.max))
                nc.vector.tensor_tensor(prob[par][:, 8 * gq:8 * gq + 8, :], sc, m8.unsqueeze(2).broadcast_to([P, 8, S]), ALU.subtract).then_inc(s.sub_done, 1)

            def pv(si, k):
                dve.wait_ge(s.small_done, k + 1)
                o = small(si)[:, 0:XH * (XD + 1)].rearrange("p (h d) -> p h d", d=XD + 1)
                ch.link(nc.vector.reciprocal(rden[:, :].unsqueeze(2), o[:, :, XD:XD + 1]))
                nc.vector.tensor_tensor(cx[:, :, :], o[:, :, 0:XD], rden[:, :].unsqueeze(2).broadcast_to([P, XH, XD]), ALU.mult).then_inc(s.dve_free, 1)

            def o(n, si, k, d):
                dve.wait_ge(s.small_done, k + 1)
                nc.vector.tensor_tensor(otmp[:, :], small(si)[:, 0:D], vec(f"bo{L}"), ALU.add).then_inc(s.dve_free, 1)
                dve.wait_ge(s.dve_free, d + 1)
                ch.link(nc.vector.scalar_tensor_tensor(out=X[:, n, :], in0=otmp[:, :], scalar=tg[:, L:L + 1], in1=X[:, n, :], op0=ALU.mult, op1=ALU.add))

            def sequence(n, par, more=True):
                k, si, _, d = counts(n, par)
                has_s, has_t2, has_next = parts_of(n)
                if has_t2:
                    k, si = k + 1, si + 1
                if has_s:
                    softmax(n + 1, 1 - par, 0)
                pv(si, k)
                if has_s:
                    softmax(n + 1, 1 - par, 1)
                if has_next:
                    kv(n + 3, si + 2, k + 2, d + 1)
                    q(n + 3, si + 4, k + 4, d + 2)
                    if more:
                        ln(n + 4)
                    o(n, si + 5, k + 5, d + 3)
                else:
                    o(n, si + 2, k + 2, d + 1)

            ln_stats(dve, ch, X, 1 + 2 * L)
            ln(0)
            kv(0, 1, 1, 0)
            q(0, 2, 2, 1)
            ln(1)
            kv(1, 5, 5, 2)
            q(1, 6, 6, 3)
            ln(2)
            softmax(0, 0, 0)
            kv(2, 9, 9, 4)
            q(2, 10, 10, 5)
            ln(3)
            softmax(0, 0, 1)
            start, steps = ch.base + ch.n, 8
            with dve.Fori(0, LOOPED // 2) as i:
                ch.base, ch.n = start + i * steps, 0
                sequence(2 * i, 0)
                sequence(2 * i + 1, 1)
            ch.leave(start, steps, LOOPED // 2)
            for n in range(LOOPED, B):
                sequence(n, n % 2, n + 4 < B)

        def xattn_pool(pool, L):
            s = xs[L]

            def norm(b, part, src, ready):
                base = 6 * b + 3 * part
                pool_wait(pool, ready, b + 1)
                nc.gpsimd.tensor_tensor(kms[:, part + 2:part + 3], kms[:, part:part + 1], mhalf[:, 0:1], ALU.pow).then_inc(s.pool_steps, 1)
                pool_wait(pool, s.pool_steps, base + 1)
                nc.gpsimd.tensor_scalar(src, src, kms[:, part + 2:part + 3], None, ALU.mult).then_inc(s.pool_steps, 1)
                pool_wait(pool, s.pool_steps, base + 2)
                nc.gpsimd.tensor_tensor(src, src, vec(("nk1", "nq1")[part]), ALU.mult).then_inc(s.normed, 1)
                pool.sem_inc(s.pool_steps, 1)

            def sequence(b, par, kv_read, pv_done):
                pool_wait(pool, s.dve_free, kv_read)
                if L:
                    norm(b, 0, kvs[:, 0:D], s.k_ready)
                if L:
                    norm(b, 1, qs[:, :], s.q_ready)
                if pv_done is not None:
                    pool_wait(pool, s.small_done, pv_done)
                nc.gpsimd.tensor_copy(v17[par][:, :, 0:XD], kvs[:, D:2 * D].rearrange("p (h d) -> p h d", d=XD)).then_inc(s.v_ready, 1)

            power(pool, 1 + 2 * L)
            sequence(0, 0, 1, None)
            sequence(1, 1, 3, None)
            sequence(2, 0, 5, PRE_SMALL + 2)
            with pool.Fori(0, LOOPED // 2) as i:
                for par in range(2):
                    n = 2 * i + par
                    sequence(n + 3, 1 - par, PRE_D + PER_D * n + 2, PRE_SMALL + PER_SMALL * (n + 1) + 2)
            for n in range(LOOPED, FULL):
                sequence(n + 3, (n + 3) % 2, PRE_D + PER_D * n + 2, PRE_SMALL + PER_SMALL * (n + 1) + 2)

        def xattn_sp(sp, L):
            s = xs[L]

            def load(par, src):
                sp.dma_start(cT[par][:, :, :], src).then_inc(s.ctx_in[par], 16)

            load(0, ctx_d[0])
            load(1, ctx_d[1])
            for b, small_uses in ((2, 2), (3, 6), (4, 10)):
                sp.wait_ge(s.small_done, small_uses)
                load(b % 2, ctx_d[b])
            for n in range(B - 5):
                sp.wait_ge(s.small_done, PRE_SMALL + PER_SMALL * n + 4)
                load((n + 5) % 2, ctx_d[n + 5])

        def columns_pe(pe, src, ready, done, lo_done):
            for b in range(B):
                pe.wait_ge(ready, b + 1)
                after(pe, lo_done, b - 1)
                for c in range(C):
                    m = nc.tensor.transpose(PS[:, b % 2, c * P:(c + 1) * P], src[b % 2][:, c * P:(c + 1) * P], ident[:, :])
                m.then_inc(done, 1)

        def columns_act(act, done, hi_done):
            for b in range(B):
                act.wait_ge(done, b + 1)
                nc.scalar.activation(tT[:, :, b * S:(b + 1) * S], PS[:, b % 2, 0:D].rearrange("p (c s) -> p c s", c=C), ACT.Copy)
                nc.scalar.activation(tTh[:, :, b * S:(b + 1) * S], PS[:, b % 2, 0:D].rearrange("p (c s) -> p c s", c=C), ACT.Copy).then_inc(hi_done, 1)

        def columns_lo(dve, b, hi_done, lo_done):
            dve.wait_ge(hi_done, b + 1)
            split_lo(tTl[:, :, b * S:(b + 1) * S], PS[:, b % 2, 0:D].rearrange("p (c s) -> p c s", c=C), tTh[:, :, b * S:(b + 1) * S]).then_inc(lo_done, 1)

        def route_pe(pe, L):
            s = fs[L]
            lo_, hi_ = (0, E0) if L == 0 else (E0, E0 + E1)
            n = hi_ - lo_
            pe.wait_ge(vec_in, 64)
            for b in range(B):
                pe.wait_ge(s.tlo, b + 1)
                for c in range(C):
                    m = nc.tensor.matmul(PS[:, 2, b * E1:b * E1 + n], tT[:, c, b * S:(b + 1) * S], rw[:, c, lo_:hi_], start=(c == 0), stop=(c == C - 1))
            m.then_inc(s.lg_done, 1)
            pe.wait_ge(s.cw_done, 1)
            psb = PS[:, 3, :].bitcast(BF16)
            for b in range(B):
                m = nc.tensor.transpose(psb[0:rows, b * P:(b + 1) * P], cw3[:, b, :, :].rearrange("p a e -> p (a e)"), identb[:, :])
            m.then_inc(s.ct_done, 1)

        def route_act(act, L):
            s = fs[L]
            n = (E0, E1)[L]
            act.wait_ge(s.lg_out, 1)
            nc.scalar.activation(pr[:, :, 0:n], lg[:, :, 0:n], ACT.Exp, scale=(-1.0, 1.0)[L]).then_inc(s.ex_done, 1)
            act.wait_ge(s.ct_done, 1)
            nc.scalar.activation(cwT[:, :], PS[0:rows, 3, :].bitcast(BF16), ACT.Copy).then_inc(s.cwt_ready, 1)

        def route_dve(dve, L, ch):
            s = fs[L]
            n = (E0, E1)[L]
            full = n + 2 * L
            v = nc.vector

            def wide(x):
                return x.unsqueeze(2).broadcast_to([P, B, n])

            dve.wait_ge(s.lg_done, 1)
            scores = PS[:, 2, 0:B * E1].rearrange("p (b e) -> p b e", e=E1)[:, :, 0:n]
            ch.link(v.memset(cw3[:, :, :, :], 0.0))
            if L == 0:
                v.tensor_copy(lg[:, :, 0:n], scores).then_inc(s.lg_out, 1)
                dve.wait_ge(s.ex_done, 1)
                ch.link(v.tensor_scalar(wk[:, :, 0:n], pr[:, :, 0:n], 1.0, None, ALU.add))
                ch.link(v.reciprocal(pr[:, :, 0:n], wk[:, :, 0:n]))
                ch.link(v.tensor_reduce(red[:, :], pr[:, :, 0:n], AX.X, ALU.max))
                ch.link(v.tensor_tensor(wk[:, :, 0:n], pr[:, :, 0:n], wide(red[:, :]), ALU.is_equal))
                ch.link(v.tensor_tensor(wk[:, :, 0:n], wk[:, :, 0:n], rank8[:, :].unsqueeze(1).broadcast_to([P, B, n]), ALU.mult))
                ch.link(v.tensor_reduce(red[:, :], wk[:, :, 0:n], AX.X, ALU.max))
                ch.link(v.tensor_tensor(wk[:, :, 0:n], wk[:, :, 0:n], wide(red[:, :]), ALU.is_equal))
                ch.link(v.tensor_tensor(cw[:, :, 0:n], wk[:, :, 0:n], pr[:, :, 0:n], ALU.mult))
            else:
                ch.link(v.tensor_reduce(red[:, :], scores, AX.X, ALU.max))
                v.tensor_tensor(lg[:, :, :], scores, wide(red[:, :]), ALU.subtract).then_inc(s.lg_out, 1)
                dve.wait_ge(s.ex_done, 1)
                ch.link(v.tensor_reduce(red[:, :], pr[:, :, :], AX.X, ALU.add))
                ch.link(v.reciprocal(red[:, :], red[:, :]))
                ch.link(v.tensor_tensor(pr[:, :, :], pr[:, :, :], wide(red[:, :]), ALU.mult))
                for b in range(B):
                    ch.link(v.max(top8[:, b, :], pr[:, b, :]))
                ch.link(v.memset(top8[:, :, TOPK:8], -1.0))
                for b in range(B):
                    ch.link(v.match_replace(wk[:, b, :], top8[:, b, :], pr[:, b, :], -2.0))
                ch.link(v.tensor_tensor(wk[:, :, :], wk[:, :, :], pr[:, :, :], ALU.not_equal))
                ch.link(v.tensor_tensor(wk[:, :, :], wk[:, :, :], pr[:, :, :], ALU.mult))
                ch.link(v.tensor_reduce(red[:, :], wk[:, :, :], AX.X, ALU.add))
                ch.link(v.reciprocal(red[:, :], red[:, :]))
                ch.link(v.memset(cw[:, :, E1:E1 + 2], 1.0))
                ch.link(v.tensor_tensor(cw[:, :, 0:E1], wk[:, :, :], wide(red[:, :]), ALU.mult))
            src = cw[:, :, 0:full]
            for part in range(3):
                last = v.tensor_copy(cw3[:, :, part, 0:full], src)
                if part == 2:
                    last.then_inc(s.cw_done, 1)
                    break
                ch.link(last)
                ch.link(v.tensor_tensor(cr[:, :, 0:full], src, cw3[:, :, part, 0:full], ALU.subtract))
                src = cr[:, :, 0:full]

        def loop_tiles(eng, J, body):
            body(0, 0, 0)
            body(1, 1, 0)
            pairs = (J - 2) // 2
            with eng.Fori(0, pairs) as i:
                body(2 * i + 2, 0, i + 1)
                body(2 * i + 3, 1, i + 1)
            if J % 2:
                body(J - 1, 0, pairs + 1)

        def acc(half, c):
            return PS[:, 4 + 2 * half + c, :]

        def open_acc(value):
            for i in range(4):
                m = nc.tensor.matmul(PS[:, 4 + i, :], zeros[:, 0:P], zeros[:, :], start=not value, stop=value, skip_group_check=True)
            return m

        def experts_pe(pe, L, J):
            s = fs[L]
            open_acc(False)
            pe.wait_ge(s.cwt_ready, 1)

            def down(u, half, par):
                pe.wait_ge(s.lo_done, u + 1)
                for c in range(C):
                    w0 = 2 * D + c * P
                    m = three(pe, acc(half, c), wh[par][:, w0:w0 + P], wl[par][:, w0:w0 + P], hhh[half][:, :], hhl[half][:, :], False, False, skip_group_check=True)
                m.then_inc(s.d_done, 1)

            def tile(j, par, cnt):
                pe.wait_ge(s.w_split, 3 * j + 3)
                for half in range(2):
                    u = 2 * j + half
                    t0 = half * HALF
                    for mat, bank, done, free in ((0, 0, s.g_done, s.silu_done), (1, 1, s.u_done, s.a_done)):
                        after(pe, free, u)
                        for c in range(C):
                            w0 = mat * D + c * P
                            m = three(pe, PS[:, bank, :], wh[par][:, w0:w0 + P], wl[par][:, w0:w0 + P],
                                      tTh[:, c, t0:t0 + HALF], tTl[:, c, t0:t0 + HALF], c == 0, c == C - 1)
                        m.then_inc(done, 1)
                    after(pe, s.h_done, u)
                    nc.tensor.matmul(PS[:, 2, :], selj[par][:, :], cwT[:, t0:t0 + HALF], start=True, stop=True).then_inc(s.c_done, 1)
                    if half:
                        down(u - 1, 0, par)
                    elif not (isinstance(j, int) and j == 0):
                        down(u - 1, 1, 1 - par)

            loop_tiles(pe, J, tile)
            down(2 * J - 1, 1, (J - 1) % 2)
            open_acc(True).then_inc(s.acc_done, 1)

        def experts_act(act, L, J):
            s = fs[L]

            def tile(j, par, cnt):
                for half in range(2):
                    u = 2 * j + half
                    act.wait_ge(s.g_done, u + 1)
                    after(act, s.a_done, u - 1)
                    nc.scalar.activation(act_s[half][:, :], PS[:, 0, :], ACT.Silu).then_inc(s.silu_done, 1)
                    act.wait_ge(s.h_done, u + 1)
                    after(act, s.d_done, u - 1)
                    nc.scalar.activation(hhh[half][:, :], hh[half][:, :], ACT.Copy).then_inc(s.hi_done, 1)

            loop_tiles(act, J, tile)

        def experts_dve(dve, L, J):
            s = fs[L]

            def tile(j, par, cnt):
                for half in range(2):
                    u = 2 * j + half
                    dve.wait_ge(s.u_done, u + 1)
                    dve.wait_ge(s.silu_done, u + 1)
                    nc.vector.tensor_tensor(act_s[half][:, :], act_s[half][:, :], PS[:, 1, :], ALU.mult).then_inc(s.a_done, 1)
                    dve.wait_ge(s.a_done, u + 1)
                    dve.wait_ge(s.c_done, u + 1)
                    nc.vector.tensor_tensor(hh[half][:, :], act_s[half][:, :], PS[:, 2, :], ALU.mult).then_inc(s.h_done, 1)
                    dve.wait_ge(s.hi_done, u + 1)
                    split_lo(hhl[half][:, :], hh[half][:, :], hhh[half][:, :]).then_inc(s.lo_done, 1)

            loop_tiles(dve, J, tile)

        def experts_pool(pool, L, J, start=0):
            s = fs[L]

            def tile(j, par, cnt):
                pool_wait(pool, (s.w_in, s.w_in1)[par], 16 * cnt + 16)
                if not (isinstance(j, int) and j == 0):
                    pool_wait(pool, s.d_done, 2 * j - 2)
                nc.gpsimd.tensor_copy(wh[par][:, :], wraw[par][:, :]).then_inc(s.w_split, 1)
                nc.gpsimd.tensor_copy(selj[par][:, :], sel[:, bass.ds(j * P, P)]).then_inc(s.w_split, 1)
                pool_wait(pool, s.w_split, 3 * j + 2)
                nc.gpsimd.tensor_tensor(wl[par][:, :], wraw[par][:, :], wh[par][:, :].bitcast(F32), ALU.subtract).then_inc(s.w_split, 1)

            loop_tiles(pool, J, tile)

        def experts_sp(sp, L, J, w_d):
            s = fs[L]

            def tile(j, par, cnt):
                after(sp, s.w_split, 3 * j - 3)
                sp.dma_start(wraw[par][:, :], w_d[bass.ds(j, 1), :, :].rearrange("a p n -> (a p) n")).then_inc((s.w_in, s.w_in1)[par], 16)

            loop_tiles(sp, J, tile)

        def rows_pe(pe, acc_ready, done, free):
            pe.wait_ge(acc_ready, 4)
            for b in range(B):
                after(pe, free, b - 1)
                for c in range(C):
                    m = nc.tensor.transpose(PS[:, b % 2, c * P:(c + 1) * P], yT[:, c, b * S:(b + 1) * S], ident[:, :])
                m.then_inc(done, 1)

        def acc_act(act, acc_done, out):
            for half in range(2):
                for c in range(C):
                    act.wait_ge(acc_done, 1)
                    nc.scalar.activation(yT[:, c, half * HALF:(half + 1) * HALF], acc(half, c), ACT.Copy).then_inc(out, 1)

        PRE_RING, PER_RING, PRE_RA, PRE_RD, PER_R = 6, 12, 4, 2, 6

        def attn_pe(pe):
            def proj(h, par, which, half, si):
                w, bank = which * D, PS[:, si % 4, :]
                for c in range(C):
                    m = three(pe, bank, ah[par][:, w + c * P:w + (c + 1) * P], al[par][:, w + c * P:w + (c + 1) * P],
                              tTh[:, c, half * HALF:(half + 1) * HALF], tTl[:, c, half * HALF:(half + 1) * HALF], c == 0, c == C - 1)
                m.then_inc(ring_done, 1)

            def values(par, half, si):
                for t in range(4):
                    t0 = half * HALF + t * S
                    for c in range(C):
                        m = nc.tensor.matmul(PS[:, si % 4, t * S:(t + 1) * S], tT[:, c, t0:t0 + S], araw[par][:, (2 * C + c) * P:(2 * C + c + 1) * P],
                                             start=(c == 0), stop=(c == C - 1))
                m.then_inc(ring_done, 1)

            def pairs(lhs, rhs, half, si):
                for t in range(4):
                    a0 = half * HALF + t * S
                    m = nc.tensor.matmul(PS[:, si % 4, t * S:(t + 1) * S], lhs[:, a0:a0 + S], rhs[:, a0:a0 + S], start=True, stop=True)
                m.then_inc(ring_done, 1)

            def turn(h, half, si):
                pe.wait_ge(norm_done, 2 * h + half + 1)
                for t in range(4):
                    m = nc.tensor.transpose(PS[:, si % 4, t * S:(t + 1) * S], sm[:, 4 * half + t, :], ident[:, :])
                m.then_inc(ring_done, 1)

            def wo(h, par):
                pe.wait_ge(aw_split, 4 * h + 4)
                for half in range(2):
                    for c in range(C):
                        w0 = 2 * D + c * P
                        m = three(pe, acc(half, c), ah[par][:, w0:w0 + P], al[par][:, w0:w0 + P],
                                  oTh[:, half * HALF:(half + 1) * HALF], oTl[:, half * HALF:(half + 1) * HALF], False, False, skip_group_check=True)
                m.then_inc(wo_done, 1)

            def head(h, par, first=False):
                si, n = PRE_RING, 1 - par
                a, d = PRE_RA + PER_R * h, PRE_RD + PER_R * h
                pe.wait_ge(ring_act, a)
                pe.wait_ge(ring_dve, d if first else d - 2)
                pairs(qT_[par], kT_[par], 0, si)
                pe.wait_ge(aw_split, 4 * h + 6)
                proj(h + 1, n, 0, 0, si + 1)
                pe.wait_ge(ring_dve, d if first else d - 1)
                pairs(qT_[par], kT_[par], 1, si + 2)
                pe.wait_ge(ring_dve, d)
                proj(h + 1, n, 0, 1, si + 3)
                if not first:
                    wo(h - 1, n)
                pe.wait_ge(ring_dve, d + 1)
                proj(h + 1, n, 1, 0, si + 4)
                pe.wait_ge(ring_act, a + 1)
                proj(h + 1, n, 1, 1, si + 5)
                pe.wait_ge(ring_dve, d + 2)
                turn(h, 0, si + 6)
                pe.wait_ge(ring_act, a + 2)
                turn(h, 1, si + 7)
                pe.wait_ge(ring_dve, d + 3)
                values(n, 0, si + 8)
                pe.wait_ge(ring_dve, d + 4)
                values(n, 1, si + 9)
                for half in range(2):
                    pe.wait_ge(ring_act, a + 3 + half)
                    pairs(v_[par], pT, half, si + 10 + half)

            def last_head(h, par):
                si, a, d = PRE_RING, PRE_RA + PER_R * h, PRE_RD + PER_R * h
                pe.wait_ge(ring_act, a)
                pe.wait_ge(ring_dve, d - 2)
                pairs(qT_[par], kT_[par], 0, si)
                pairs(qT_[par], kT_[par], 1, si + 1)
                pe.wait_ge(ring_dve, d)
                wo(h - 1, 1 - par)
                turn(h, 0, si + 2)
                turn(h, 1, si + 3)
                for half in range(2):
                    pe.wait_ge(ring_dve, d + 1 + half)
                    pe.wait_ge(ring_act, a + 1 + half)
                    pairs(v_[par], pT, half, si + 4 + half)
                pe.wait_ge(ring_dve, d + 4)
                wo(h, par)

            open_acc(False)
            pe.wait_ge(tlo_done, B)
            pe.wait_ge(aw_split, 2)
            for i, (which, half) in enumerate(((0, 0), (0, 1), (1, 0), (1, 1))):
                proj(0, 0, which, half, i)
            for half in range(2):
                pe.wait_ge(ring_act, half + 1)
                values(0, half, 4 + half)
            head(0, 0, True)
            with pe.Fori(0, (AH - 2) // 2) as i:
                head(2 * i + 1, 1)
                head(2 * i + 2, 0)
            last_head(AH - 1, 1)
            open_acc(True).then_inc(wo_done, 1)

        def attn_act(act):
            def copy(dst, half, r, si, done):
                act.wait_ge(ring_done, r + 1)
                nc.scalar.activation(dst[:, half * HALF:(half + 1) * HALF], PS[:, si % 4, :], ACT.Copy).then_inc(done, 1)

            def exps(h, half):
                act.wait_ge(masked, 2 * h + half + 1)
                for t in range(4):
                    b = 4 * half + t
                    nc.scalar.activation(sm[:, b, :], sm[:, b, :], ACT.Exp, bias=nmx[:, b:b + 1], scale=AD ** -0.5,
                                         accum_out=sums[:, b:b + 1]).then_inc(aexp_done, 1)

            def head(h, par, last=False):
                r, si, n = PRE_RING + h * PER_RING, PRE_RING, 1 - par
                at, vt = (2, 4) if last else (6, 10)
                for half in range(2):
                    exps(h, half)
                    if not last:
                        copy(qT_[n], half, r + 1 + 2 * half, si + 1 + 2 * half, ring_act)
                for half in range(2):
                    copy(pT, half, r + at + half, si + at + half, ring_act)
                if not last:
                    for half in range(2):
                        copy(v_[n], half, r + 8 + half, si + 8 + half, ring_act)
                for half in range(2):
                    copy(oTh, half, r + vt + half, si + vt + half, ahi_done)

            for half in range(2):
                copy(qT_[0], half, half, half, ring_act)
            for half in range(2):
                copy(v_[0], half, 4 + half, 4 + half, ring_act)
            head(0, 0)
            with act.Fori(0, (AH - 2) // 2) as i:
                head(2 * i + 1, 1)
                head(2 * i + 2, 0)
            head(AH - 1, 1, True)

        def attn_dve(dve, ch):
            v = nc.vector

            def keys(dst, half, r, si):
                dve.wait_ge(ring_done, r + 1)
                v.tensor_copy(dst[:, half * HALF:(half + 1) * HALF], PS[:, si % 4, :]).then_inc(ring_dve, 1)

            def low_part(h, half, si):
                dve.wait_ge(ahi_done, 2 * h + half + 1)
                cols = slice(half * HALF, (half + 1) * HALF)
                split_lo(oTl[:, cols], PS[:, si % 4, :], oTh[:, cols]).then_inc(ring_dve, 1)

            def mask(h, half, r, si, d):
                dve.wait_ge(ring_done, r + 1)
                part = sm[:, 4 * half:4 * half + 4, :]
                v.tensor_tensor(part, PS[:, si % 4, :].rearrange("p (t s) -> p t s", s=S),
                                causal[:, :].unsqueeze(1).broadcast_to([P, 4, S]), ALU.add).then_inc(ring_dve, 1)
                dve.wait_ge(ring_dve, d + 1)
                m4 = nmx[:, 4 * half:4 * half + 4]
                ch.link(v.tensor_reduce(m4, part, AX.X, ALU.max))
                v.tensor_scalar(m4, m4, -(AD ** -0.5), None, ALU.mult).then_inc(masked, 1)

            def norm(h, half):
                dve.wait_ge(aexp_done, 8 * h + 4 * half + 4)
                part = sm[:, 4 * half:4 * half + 4, :]
                r4 = rsum[:, 4 * half:4 * half + 4]
                ch.link(v.reciprocal(r4, sums[:, 4 * half:4 * half + 4]))
                v.tensor_tensor(part, part, r4.unsqueeze(2).broadcast_to([P, 4, S]), ALU.mult).then_inc(norm_done, 1)

            def head(h, par, last=False):
                r, si, n = PRE_RING + h * PER_RING, PRE_RING, 1 - par
                d = PRE_RD + PER_R * h
                step, vt = (1, 4) if last else (2, 10)
                for half in range(2):
                    mask(h, half, r + step * half, si + step * half, d + half)
                for half in range(2):
                    norm(h, half)
                if not last:
                    for half in range(2):
                        keys(kT_[n], half, r + 4 + half, si + 4 + half)
                for half in range(2):
                    low_part(h, half, si + vt + half)

            for half in range(2):
                keys(kT_[0], half, 2 + half, 2 + half)
            head(0, 0)
            start, steps = ch.base + ch.n, 8
            with dve.Fori(0, (AH - 2) // 2) as i:
                ch.base, ch.n = start + i * steps, 0
                head(2 * i + 1, 1)
                head(2 * i + 2, 0)
            ch.leave(start, steps, (AH - 2) // 2)
            head(AH - 1, 1, True)

        def attn_pool(pool):
            def split(h, par, dst, src, n, k):
                nc.gpsimd.tensor_copy(ah[par][:, dst:dst + n], araw[par][:, src:src + n]).then_inc(aw_split, 1)
                pool_wait(pool, aw_split, 4 * h + k + 1)
                nc.gpsimd.tensor_tensor(al[par][:, dst:dst + n], araw[par][:, src:src + n], ah[par][:, dst:dst + n].bitcast(F32), ALU.subtract).then_inc(aw_split, 1)

            def head(h, par, cnt, first=False):
                pool_wait(pool, aw_in[par], 16 * cnt + 16)
                if not first:
                    pool_wait(pool, ring_done, PRE_RING + (h - 2) * PER_RING - 2)
                split(h, par, 0, 0, 2 * D, 0)
                if not first:
                    pool_wait(pool, wo_done, h - 1)
                split(h, par, 2 * D, 3 * D, D, 2)

            head(0, 0, 0, True)
            head(1, 1, 0, True)
            with pool.Fori(1, AH // 2) as i:
                head(2 * i, 0, i)
                head(2 * i + 1, 1, i)

        def attn_sp(sp):
            def load(par, src):
                sp.dma_start(araw[par][:, :], src).then_inc(aw_in[par], 16)

            load(0, attn_d[0])
            load(1, attn_d[1])
            with sp.Fori(1, AH // 2) as i:
                for par in range(2):
                    h = 2 * i + par
                    sp.wait_ge(aw_split, 4 * h - 4)
                    sp.wait_ge(ring_done, PRE_RING + (h - 2) * PER_RING)
                    load(par, attn_d[bass.ds(h, 1), :, :].rearrange("a p n -> (a p) n"))

        Js = (J0, J1)
        Is = (I0, I1)

        @block.sync
        def _(sp):
            sp.dma_start(X[:, :, :], x_d.rearrange("b s d -> s b d")).then_inc(x_in, 16)
            for L in range(2):
                sp.dma_start(WX[L][:, :, :], wx_d[L]).then_inc(wx_in, 16)
            sp.dma_start(vecs[:, :, :].rearrange("p a d -> p (a d)"), vec_d.partition_broadcast(P)).then_inc(vec_in, 16)
            sp.dma_start(gates[:, :], gate_d.partition_broadcast(P)).then_inc(vec_in, 16)
            sp.dma_start(rw[:, :, 0:E0], rw0_d).then_inc(vec_in, 16)
            sp.dma_start(rw[:, :, E0:E0 + E1], rw1_d).then_inc(vec_in, 16)
            xattn_sp(sp, 0)
            barrier(sp, 1)
            experts_sp(sp, 0, J0, moe0_d)
            barrier(sp, 2)
            xattn_sp(sp, 1)
            barrier(sp, 3)
            attn_sp(sp)
            barrier(sp, 4)
            experts_sp(sp, 1, J1, moe1_d)
            for b in range(B):
                sp.wait_ge(fs[1].tile_out, b + 1)
                sp.dma_start(out_d[b], X[:, b, :]).then_inc(out_done, 16)
            sp.wait_ge(out_done, 16 * B)

        @block.gpsimd
        def _(pool):
            gp = nc.gpsimd
            gp.memset(ident[:, :], 0.0).then_inc(pool_chain, 1)
            gp.memset(identb[:, :], 0.0).then_inc(pool_chain, 1)
            gp.memset(head_rows[:, :], 1.0).then_inc(pool_chain, 1)
            pool.wait_ge(pool_chain, 3)
            for m in (ident, identb):
                gp.affine_select(out=m[:, :], in_=m[:, :], compare_op=ALU.not_equal, fill=1.0, base=0,
                                 pattern=[[-1, P]], channel_multiplier=1).then_inc(const_done, 1)
            gp.affine_select(out=head_rows[:, :], in_=head_rows[:, :], compare_op=ALU.is_ge, fill=0.0, base=0,
                             pattern=[[-XD, HT]], channel_multiplier=1).then_inc(const_done, 1)
            pool.wait_ge(const_done, 3)
            gp.affine_select(out=head_rows[:, :], in_=head_rows[:, :], compare_op=ALU.is_ge, fill=0.0, base=XD - 1,
                             pattern=[[XD, HT]], channel_multiplier=-1).then_inc(const_done, 1)
            xattn_pool(pool, 0)
            barrier(pool, 1)
            for L in range(2):
                power(pool, 2 + 4 * L)
                n, I, J = (E0, E1 + 2)[L], Is[L], Js[L]
                gp.memset(sel[:, :], 1.0).then_inc(pool_chain, 1)
                k = 4 + L * 3
                pool.wait_ge(pool_chain, k)
                for step, (base, sign) in enumerate(((0, 1), (I - 1, -1))):
                    for part in range(3):
                        v = sel[32 * part:32 * part + 32, 0:J * P]
                        i = gp.affine_select(out=v, in_=v, compare_op=ALU.is_ge, fill=0.0, base=base,
                                             pattern=[[sign, J * P]], channel_multiplier=-sign * I)
                    i.then_inc(pool_chain, 1)
                    pool.wait_ge(pool_chain, k + step + 1)
                experts_pool(pool, L, J)
                if L == 0:
                    barrier(pool, 2)
                    xattn_pool(pool, 1)
                    barrier(pool, 3)
                    power(pool, 4)
                    power(pool, 5)
                    gp.memset(causal[:, :], 0.0).then_inc(const_done, 1)
                    pool.wait_ge(const_done, 5)
                    gp.affine_select(out=causal[:, :], in_=causal[:, :], compare_op=ALU.is_ge, fill=NEG, base=0,
                                     pattern=[[-1, S]], channel_multiplier=1).then_inc(const_done, 1)
                    attn_pool(pool)
                    barrier(pool, 4)

        @block.scalar
        def _(act):
            act.wait_ge(vec_in, 64)
            nc.scalar.activation(tg[:, :], gates[:, :], ACT.Tanh).then_inc(tg_done, 1)
            act.wait_ge(const_done, 4)
            xattn_act(act, 0)
            barrier(act, 1)
            columns_act(act, fs[0].t_done, fs[0].thi)
            route_act(act, 0)
            experts_act(act, 0, J0)
            acc_act(act, fs[0].acc_done, fs[0].y_out)
            barrier(act, 2)
            xattn_act(act, 1)
            barrier(act, 3)
            columns_act(act, t_done, thi_done)
            attn_act(act)
            for half in range(2):
                for c in range(C):
                    act.wait_ge(wo_done, AH + 1)
                    nc.scalar.activation(ayT[:, c, half * HALF:(half + 1) * HALF], acc(half, c), ACT.Copy).then_inc(ay_out, 1)
            barrier(act, 4)
            columns_act(act, fs[1].t_done, fs[1].thi)
            route_act(act, 1)
            experts_act(act, 1, J1)
            acc_act(act, fs[1].acc_done, fs[1].y_out)

        @block.tensor
        def _(pe):
            pe.wait_ge(const_done, 2)
            xattn_pe(pe, 0)
            barrier(pe, 1)
            columns_pe(pe, fxn, fs[0].n_done, fs[0].t_done, fs[0].tlo)
            route_pe(pe, 0)
            experts_pe(pe, 0, J0)
            rows_pe(pe, fs[0].y_out, fs[0].yt_done, fs[0].y_free)
            barrier(pe, 2)
            xattn_pe(pe, 1)
            barrier(pe, 3)
            columns_pe(pe, gxn, n_done, t_done, tlo_done)
            attn_pe(pe)
            pe.wait_ge(ay_out, 4)
            for b in range(B):
                after(pe, ay_free, b - 1)
                for c in range(C):
                    m = nc.tensor.transpose(PS[:, b % 2, c * P:(c + 1) * P], ayT[:, c, b * S:(b + 1) * S], ident[:, :])
                m.then_inc(ayt_done, 1)
            barrier(pe, 4)
            columns_pe(pe, fxn, fs[1].n_done, fs[1].t_done, fs[1].tlo)
            route_pe(pe, 1)
            experts_pe(pe, 1, J1)
            rows_pe(pe, fs[1].y_out, fs[1].yt_done, fs[1].y_free)

        @block.vector
        def _(dve):
            v = nc.vector
            ch = Chain(dve, dve_chain)
            ch.link(v.memset(zeros[:, :].bitcast(F32), 0.0))
            ch.link(v.memset(mhalf[:, :], -0.5))
            for i in range(2):
                ch.link(v.memset(v17[i][:, :, :], 1.0))
            for e in range(E0):
                ch.link(v.memset(rank8[:, e:e + 1], float(E0 - e)))
            dve.wait_ge(x_in, 16)
            dve.wait_ge(vec_in, 64)
            dve.wait_ge(tg_done, 1)
            xattn_dve(dve, 0, ch)
            barrier(dve, 1)

            def normed(b, s_n, s_hi, s_lo, make):
                make(b)
                if b:
                    columns_lo(dve, b - 1, s_hi, s_lo)
                if b == B - 1:
                    columns_lo(dve, b, s_hi, s_lo)

            s = fs[0]
            ln_stats(dve, ch, X, 2)
            for b in range(B):
                after(dve, s.t_done, b - 1)
                normed(b, s.n_done, s.thi, s.tlo, lambda b: ln_scale(fxn[b % 2][:, :], X[:, b, :], b).then_inc(s.n_done, 1))
            route_dve(dve, 0, ch)
            experts_dve(dve, 0, J0)
            for b in range(B):
                dve.wait_ge(s.yt_done, b + 1)
                v.scalar_tensor_tensor(out=X[:, b, :], in0=PS[:, b % 2, 0:D], scalar=tg[:, 2:3], in1=X[:, b, :], op0=ALU.mult, op1=ALU.add).then_inc(s.y_free, 1)
            dve.wait_ge(s.y_free, B)
            barrier(dve, 2)
            for i in range(2):
                ch.link(v.memset(v17[i][:, :, :], 1.0))
            xattn_dve(dve, 1, ch)
            barrier(dve, 3)

            ln_stats(dve, ch, X, 4)
            for b in range(B):
                ch.link(ln_scale(Z[:, b, :], X[:, b, :], b))

            def row_scales(use, tmp):
                for b in range(B):
                    scale = mean_square(Z[:, b, :], tmp[:, :], ms[:, b:b + 1])
                    if b < B - 1:
                        ch.link(scale)
                scale.then_inc(stats_done, 1)
                dve.wait_ge(rstd_done, use)

            def scaled(out, b, weight):
                return v.scalar_tensor_tensor(out=out[b % 2][:, :], in0=Z[:, b, :], scalar=rstd[:, b:b + 1], in1=vec(weight), op0=ALU.mult, op1=ALU.mult)

            row_scales(5, gjunk)
            for b in range(B):
                after(dve, t_done, b - 1)
                normed(b, n_done, thi_done, tlo_done, lambda b: scaled(gxn, b, "ln1").then_inc(n_done, 1))
            dve.wait_ge(const_done, 6)
            attn_dve(dve, ch)
            for b in range(B):
                dve.wait_ge(ayt_done, b + 1)
                v.tensor_tensor(Z[:, b, :], PS[:, b % 2, 0:D], Z[:, b, :], ALU.add).then_inc(ay_free, 1)
            dve.wait_ge(ay_free, B)
            barrier(dve, 4)
            s = fs[1]
            row_scales(6, fjunk)
            for b in range(B):
                after(dve, s.t_done, b - 1)
                normed(b, s.n_done, s.thi, s.tlo, lambda b: scaled(fxn, b, "ln2").then_inc(s.n_done, 1))
            route_dve(dve, 1, ch)
            experts_dve(dve, 1, J1)
            for b in range(B):
                dve.wait_ge(s.yt_done, b + 1)
                v.tensor_tensor(Z[:, b, :], PS[:, b % 2, 0:D], Z[:, b, :], ALU.add).then_inc(s.y_free, 1)
                dve.wait_ge(s.y_free, b + 1)
                v.scalar_tensor_tensor(out=X[:, b, :], in0=Z[:, b, :], scalar=tg[:, 3:4], in1=X[:, b, :], op0=ALU.mult, op1=ALU.add).then_inc(s.tile_out, 1)


def kernel(**inputs):
    import numpy as np
    import concourse.bacc as bacc
    from concourse.bass_utils import run_bass_kernel_spmd

    a = {k: np.asarray(v) for k, v in inputs.items()}

    def columns(m):
        return m.reshape(C, P, -1).transpose(1, 0, 2)

    def cross(k, v, q, o):
        return columns(np.concatenate([m.T for m in (k, v, q, o)], axis=1))

    def expert_tiles(gate, up, down, J):
        pad = ((0, J * P - gate.shape[0]), (0, 0))
        g, u, d = (np.pad(m, pad) for m in (gate, up, down))
        cols = [m.reshape(J, P, C, P).transpose(0, 3, 2, 1).reshape(J, P, D) for m in (g, u)]
        return np.concatenate(cols + [d.reshape(J, P, D)], axis=2)

    def rows_of(w):
        return w.transpose(0, 2, 1).reshape(-1, D)

    heads = [a["L1_ffn_" + k].reshape(C, P, AH, AD).transpose(2, 1, 0, 3).reshape(AH, P, D) for k in ("wq", "wk", "wv")]
    arrays = {
        "ctx": a["ctx_2048"].transpose(2, 0, 1).reshape(C, P, B, S).transpose(2, 1, 0, 3),
        "x": a["x"],
        "wx": np.stack([cross(*(a["L0_xattn_" + k] for k in ("Wk", "Wv", "Wq", "Wo"))),
                        cross(*(a["L1_xattn_" + k] for k in ("k_img_w", "v_img_w", "q_w", "o_w")))]),
        "vec": np.concatenate([a[k] for k in (
            "L0_xattn_bk", "L0_xattn_bv", "L0_xattn_bq", "L0_xattn_bo", "L1_xattn_k_img_b", "L1_xattn_v_img_b",
            "L1_xattn_q_b", "L1_xattn_o_b", "L1_xattn_norm_k_img_w", "L1_xattn_norm_q_w", "L1_ffn_ln1_w", "L1_ffn_ln2_w")]),
        "gate": np.concatenate([a["g_xattn"], a["g_ffn"]]),
        "rw0": columns(a["L0_ffn_router_w"]),
        "rw1": columns(a["L1_ffn_gate_w"].T),
        "moe0": expert_tiles(rows_of(a["L0_ffn_gate_w"]), rows_of(a["L0_ffn_up_w"]), a["L0_ffn_down_w"].reshape(-1, D), J0),
        "moe1": expert_tiles(np.concatenate([a["L1_ffn_eg_w"].reshape(-1, D), a["L1_ffn_sg_w"]]),
                             np.concatenate([a["L1_ffn_eu_w"].reshape(-1, D), a["L1_ffn_su_w"]]),
                             np.concatenate([a["L1_ffn_ed_w"].transpose(0, 2, 1).reshape(-1, D), a["L1_ffn_sd_w"].T]), J1),
        "attn": np.concatenate(heads + [a["L1_ffn_wo"].reshape(AH, P, D)], axis=2),
    }
    arrays = {k: np.ascontiguousarray(v) for k, v in arrays.items()}
    nc = bacc.Bacc("TRN2", target_bir_lowering=False, num_devices=1)
    aps = [nc.dram_tensor(k, v.shape, mybir.dt.from_np(v.dtype), kind="ExternalInput").ap() for k, v in arrays.items()]
    out = nc.dram_tensor("out", (B, S, D), F32, kind="ExternalOutput").ap()
    build(nc, *aps, out)
    return run_bass_kernel_spmd(nc, [arrays], core_ids=[0]).results[0]["out"]
```

```python
from contextlib import ExitStack

import concourse.bass as bass
from concourse import mybir

F32 = mybir.dt.float32
F32R = mybir.dt.float32r
BF16 = mybir.dt.bfloat16
ALU = mybir.AluOpType
ACT = mybir.ActivationFunctionType
AX = mybir.AxisListType

B, S, D = 8, 128, 256
P = 128
T = B * S
C = D // P
XH, XD = 16, 16
AH, AD = 16, 128
E0, I0 = 8, 512
E1, I1, SI = 16, 176, 352
TOPK = 6
HALF = T // 2
NEG = -3.0e38
LN_EPS, RMS_EPS = 1e-5, 1e-6
HT = P // XD
SLOTS = T // P + E0 - 1
EW = 2 * C * I0 + I0 // P * D
SJ = -(-SI // P)
J1 = SJ + E1 * I1 // P
VEC = ["bk0", "bv0", "bq0", "bo0", "bk1", "bv1", "bq1", "bo1", "nk1", "nq1", "ln1", "ln2"]


class Chain:

    def __init__(self, eng, sem):
        self.eng, self.sem, self.base, self.n = eng, sem, 0, 0

    def link(self, ins):
        self.n += 1
        ins.then_inc(self.sem, 1)
        self.eng.wait_ge(self.sem, self.base + self.n)

    def leave(self, start, steps, count):
        assert self.n == steps, (self.n, steps)
        self.base, self.n = start + count * steps, 0


def after(eng, sem, n):
    if isinstance(n, int) and n <= 0:
        return
    eng.wait_ge(sem, n)


def build(nc, ctx_d, x_d, wx_d, vec_d, gate_d, rw0_d, rw1_d, moe0_d, moe1_d, attn_d, attnv_d, out_d):
    stack = ExitStack()
    with stack:
        def sb(name, shape, dt=F32, where=None):
            return (where or stack).enter_context(nc.sbuf_tensor(name, shape, dt))

        def sem(name):
            return stack.enter_context(nc.semaphore(name))

        PS = stack.enter_context(nc.psum_tensor("PS", [P, 8, 512], F32))

        X = sb("X", [P, B, D])
        WX = [sb(f"WX{i}", [P, C, 4 * D]) for i in range(2)]
        head_rows = sb("head_rows", [P, HT])
        vecs = sb("vecs", [P, len(VEC), D])
        gates = sb("gates", [P, 4])
        tg = sb("tg", [P, 4])
        ident = sb("ident", [P, P])
        identb = sb("identb", [P, P], BF16)
        zeros = sb("zeros", [P, 512], F32R)
        rank8 = sb("rank8", [P, E0])
        rw = sb("rw", [P, C, E0 + E1])
        sel = sb("sel", [3 * 32, E1 * I1], BF16)
        expert_ids = sb("expert_ids", [P, E0])
        upto = sb("upto", [P, E0, E0])
        earlier = sb("earlier", [P, P])
        ones = sb("ones", [P, P])
        tile_ids = sb("tile_ids", [P, SLOTS])
        st = sb("st", [P, B, 6])
        mv = sb("mv", [P, B, 2])
        ms = sb("ms", [P, B])
        rstd = sb("rstd", [P, B])
        mhalf = sb("mhalf", [P, B])
        kms = sb("kms", [P, 4])

        def vec(name):
            return vecs[:, VEC.index(name), :]

        w0 = ExitStack()
        WE = sb("WE", [P, E0, EW], where=w0)

        class Xb:
            def __init__(m, n, where):
                def buf(name, *shape):
                    return sb(f"x{n}_{name}", [P, *shape], where=where)

                m.xn, m.qs, m.junk, m.otmp = (buf(k, D) for k in ("xn", "qs", "junk", "otmp"))
                m.xT, m.cxT = buf("xT", C, S), buf("cxT", C, S)
                m.k8T = [buf(f"k8T{i}", C, HT, S) for i in range(2)]
                m.qT = [buf(f"qT{i}", C, S) for i in range(2)]
                m.prob = [buf(f"prob{i}", XH, S) for i in range(2)]
                m.probT = buf("probT", XH, S)
                m.mx, m.rden, m.cx = buf("mx", XH), buf("rden", XH), buf("cx", XH, XD)
                if n == 0:
                    m.cT = [buf(f"cT{i}", C, S) for i in range(2)]
                    m.kvs = buf("kvs", 2 * D)
                    m.v17 = buf("v17", B, XH, XD + 1)

        a = ExitStack()
        xb0 = Xb(0, a)
        a.close()
        e = ExitStack()
        FX = sb("FX", [P, B, D], where=e)
        rT = sb("rT", [P, C, T], where=e)
        xs_s = [sb(f"xs_s{i}", [P, D], where=e) for i in range(2)]
        xsT = [sb(f"xsT{i}", [P, C, P], where=e) for i in range(2)]
        gs = [sb(f"gs{i}", [P, I0], where=e) for i in range(2)]
        hs = sb("hs", [P, I0], where=e)
        hT = sb("hT", [P, I0 // P, P], where=e)
        y_s = [sb(f"y_s{i}", [P, D], where=e) for i in range(2)]
        kms8 = sb("kms8", [P, B], where=e)
        krs8 = sb("krs8", [P, B], where=e)
        kjunk = sb("kjunk", [P, D], where=e)
        route = sb("route", [P, B, E0], where=e)
        rexp = sb("rexp", [P, B, E0], where=e)
        hot = sb("hot", [P, B + 2, E0], where=e)
        sums_to = [sb(f"sums_to{n}", [P, 4 + B, E0], where=e) for n in (2, 4, 8)]
        rmax = sb("rmax", [P, B], where=e)
        rfirst = sb("rfirst", [P, B], where=e)
        place = sb("place", [P, B + 1, E0], where=e)
        more_than = sb("more_than", [P, E0, E0], where=e)
        tiles_of = sb("tiles_of", [P, E0], where=e)
        ends = sb("ends", [P, E0], where=e)
        starts = sb("starts", [P, E0], where=e)
        below = sb("below", [P, SLOTS, E0], where=e)
        posf = sb("posf", [P, B], where=e)
        pos = sb("pos", [P, B], mybir.dt.uint32, e)
        exf = sb("exf", [P, SLOTS], where=e)
        ex = sb("ex", [P, SLOTS], mybir.dt.int32, e)
        K1 = sb("K1", [P, B, D], where=e)
        V1 = sb("V1", [P, B, XH, XD + 1], where=e)
        e.close()
        w0.close()
        l1 = ExitStack()
        tT = sb("tT", [P, C, T], where=l1)
        tTh = sb("tTh", [P, C, T], F32R, l1)
        tTl = sb("tTl", [P, C, T], F32R, l1)
        Z = sb("Z", [P, B, D], where=l1)
        a1 = ExitStack()
        xb1 = Xb(1, a1)
        xb1.v17 = V1
        xbs = [xb0, xb1]
        a1.close()
        f = ExitStack()
        rows = 3 * 32
        selj = [sb(f"selj{i}", [rows, P], BF16, f) for i in range(2)]
        cwT = sb("cwT", [rows, T], BF16, f)
        wraw = [sb(f"wraw{i}", [P, 3 * D], where=f) for i in range(2)]
        wh = [sb(f"wh{i}", [P, 3 * D], F32R, f) for i in range(2)]
        wl = [sb(f"wl{i}", [P, 3 * D], F32R, f) for i in range(2)]
        act_s = [sb(f"act_s{i}", [P, HALF], where=f) for i in range(2)]
        hh = [sb(f"hh{i}", [P, HALF], where=f) for i in range(2)]
        hhh = [sb(f"hhh{i}", [P, HALF], F32R, f) for i in range(2)]
        hhl = [sb(f"hhl{i}", [P, HALF], F32R, f) for i in range(2)]
        yT = sb("yT", [P, C, T], where=f)
        lg = sb("lg", [P, B, E1], where=f)
        pr = sb("pr", [P, B, E1], where=f)
        wk = sb("wk", [P, B, E1], where=f)
        cw = sb("cw", [P, B, E1], where=f)
        cr = sb("cr", [P, B, E1], where=f)
        top8 = sb("top8", [P, B, 8], where=f)
        red = sb("red", [P, B], where=f)
        cw3 = sb("cw3", [P, B, 3, 32], BF16, f)
        fxn = [sb(f"fxn{i}", [P, D], where=f) for i in range(2)]
        f.close()
        g = ExitStack()
        ayT = sb("ayT", [P, C, T], where=g)
        araw = [sb(f"araw{i}", [P, 3 * D], where=g) for i in range(2)]
        ah = [sb(f"ah{i}", [P, 3 * D], F32R, g) for i in range(2)]
        al = [sb(f"al{i}", [P, 3 * D], F32R, g) for i in range(2)]
        qT_ = [sb(f"aqT{i}", [P, T], where=g) for i in range(2)]
        kT_ = [sb(f"akT{i}", [P, T], where=g) for i in range(2)]
        avraw = sb("avraw", [P, C, 2 * AD], where=g)
        avh = sb("avh", [P, C, 2 * AD], F32R, g)
        avl = sb("avl", [P, C, 2 * AD], F32R, g)
        v4 = sb("v4", [P, 4, T], where=g)
        sm = sb("sm", [P, B, S], where=g)
        pT = sb("pT", [P, T], where=g)
        oTh = sb("oTh", [P, T], F32R, g)
        oTl = sb("oTl", [P, T], F32R, g)
        nmx = sb("nmx", [P, B], where=g)
        sums = sb("sums", [P, B], where=g)
        rsum = sb("rsum", [P, B], where=g)
        causal = sb("causal", [P, S], where=g)
        gxn = [sb(f"gxn{i}", [P, D], where=g) for i in range(2)]
        g.close()
        l1.close()

        xs_d = nc.dram_tensor("xs_d", (SLOTS * P, D), F32).ap()
        ys_d = nc.dram_tensor("ys_d", (SLOTS * P, D), F32).ap()

        x_in = [sem("x_in0"), sem("x_in1")]
        gate_in, vec_in, late_in, out_done = sem("gate_in"), sem("vec_in"), sem("late_in"), sem("out_done")
        wx_in = [sem("wx_in0"), sem("wx_in1")]
        const_done, tg_done = sem("const_done"), sem("tg_done")
        pool_turns, stats_done, rstd_done = sem("pool_turns"), sem("stats_done"), sem("rstd_done")
        dve_chain, pool_chain = sem("dve_chain"), sem("pool_chain")
        phase_end = sem("phase_end")

        class Xs:
            def __init__(s, n):
                s.ln_done = sem(f"x{n}_ln_done")
                s.small_done = sem(f"x{n}_small_done")
                s.act_free = sem(f"x{n}_act_free")
                s.dve_free = sem(f"x{n}_dve_free")
                s.tr_done = sem(f"x{n}_tr_done")
                s.tr_free = sem(f"x{n}_tr_free")
                s.q_ready = sem(f"x{n}_q_ready")
                s.v_ready = sem(f"x{n}_v_ready")
                s.normed = sem(f"x{n}_normed")
                s.q_power = sem(f"x{n}_q_power")
                s.scores_done = sem(f"x{n}_scores_done")
                s.sub_done = sem(f"x{n}_sub_done")
                s.exp_done = sem(f"x{n}_exp_done")
                s.ctx_in = [sem(f"x{n}_ctx_in{i}") for i in range(2)]

        class f1:
            n_done = sem("f1_n_done")
            t_done = sem("f1_t_done")
            thi = sem("f1_thi")
            tlo = sem("f1_tlo")
            lg_done = sem("f1_lg_done")
            lg_out = sem("f1_lg_out")
            ex_done = sem("f1_ex_done")
            cw_done = sem("f1_cw_done")
            ct_done = sem("f1_ct_done")
            cwt_ready = sem("f1_cwt_ready")
            w_in = [sem(f"f1_w_in{i}") for i in range(2)]
            sel_ready = sem("f1_sel_ready")
            w_split = sem("f1_w_split")
            g_done = sem("f1_g_done")
            u_done = sem("f1_u_done")
            c_done = sem("f1_c_done")
            d_done = sem("f1_d_done")
            silu_done = sem("f1_silu_done")
            a_done = sem("f1_a_done")
            h_done = sem("f1_h_done")
            hi_done = sem("f1_hi_done")
            lo_done = sem("f1_lo_done")
            y_out = sem("f1_y_out")
            yt_done = sem("f1_yt_done")
            tile_out = sem("f1_tile_out")

        xs = [Xs(0), Xs(1)]

        class Es:
            n_done, t_done, t_free, lg_done, ex_done, hot_done, place_done, pos_done = (
                sem("e_" + k) for k in ("n_done", "t_done", "t_free", "lg_done", "ex_done", "hot_done", "place_done", "pos_done"))
            w_in, zero_in, scattered, ctx_in = (sem("e_" + k) for k in ("w_in", "zero_in", "scattered", "ctx_in"))
            gathered = [sem(f"e_gathered{b}") for b in range(B)]
            kv_done, kv_free, kms_done, krs_done = (sem("e_" + k) for k in ("kv_done", "kv_free", "kms_done", "krs_done"))
            k1_ready, kt_done, kt_free = (sem("e_" + k) for k in ("k1_ready", "kt_done", "kt_free"))
            xs_in = [sem("e_xs_in0"), sem("e_xs_in1")]
            y_out = [sem("e_y_out0"), sem("e_y_out1")]
            xt_done, xt_ready, g_done, u_done, silu_done = (sem("e_" + k) for k in ("xt_done", "xt_ready", "g_done", "u_done", "silu_done"))
            h_ready, ht_done, ht_ready, d_done, y_ready = (sem("e_" + k) for k in ("h_ready", "ht_done", "ht_ready", "d_done", "y_ready"))
            sums_done, experts_done, zeroed = sem("e_sums_done"), sem("e_experts_done"), sem("e_zeroed")
        squared, z_done, eps_done = sem("squared"), sem("z_done"), sem("eps_done")
        n_done, t_done, thi_done, tlo_done = (sem("n_" + k) for k in ("n_done", "t_done", "thi_done", "tlo_done"))
        aw_in = [sem("aw_in0"), sem("aw_in1")]
        av_in, av_split = sem("av_in"), sem("av_split")
        aw_split, ring_done, ring_act, ring_dve, ahi_done = (
            sem(k) for k in ("aw_split", "ring_done", "ring_act", "ring_dve", "ahi_done"))
        masked, aexp_done, norm_done, wo_done = (sem(k) for k in ("masked", "aexp_done", "norm_done", "wo_done"))
        ay_out, ayt_done, ay_free = (sem(k) for k in ("ay_out", "ayt_done", "ay_free"))

        block = stack.enter_context(nc.Block())

        def pool_wait(pool, sm_, n):
            after(pool, sm_, n)
            if not isinstance(n, int):
                pool.sem_inc(pool_turns, 1)

        def barrier(eng, k):
            eng.drain().then_inc(phase_end, 1)
            eng.wait_ge(phase_end, 5 * k)

        def three(pe, out, wh_, wl_, xh_, xl_, first, last, **kw):
            nc.tensor.matmul(out, wh_, xh_, start=first, stop=False, **kw)
            nc.tensor.matmul(out, wh_, xl_, start=False, stop=False, **kw)
            return nc.tensor.matmul(out, wl_, xh_, start=False, stop=last, **kw)

        PRE_SMALL, PER_SMALL, PRE_D, PER_D = (11, 8), (7, 6), (6, 3), (4, 3)
        PRE_A, PER_A = 5, 3
        FULL = B - 3
        LOOPED = FULL // 2 * 2

        def counts(L, n, par):
            if isinstance(n, int) and n > FULL:
                short = n - FULL
                k = PRE_SMALL[L] + FULL * PER_SMALL[L] + 3 * short + 1
                return k, k, PRE_A + PER_A * FULL + short + 1, PRE_D[L] + PER_D[L] * FULL + 2 * short
            k = PRE_SMALL[L] + n * PER_SMALL[L]
            return k, PRE_SMALL[L] + par * PER_SMALL[L], PRE_A + n * PER_A, PRE_D[L] + n * PER_D[L]

        def parts_of(n):
            return [not isinstance(n, int) or n + ahead < B for ahead in (1, 2, 3)]

        def small(i):
            return PS[:, 6 + i % 2, :]

        def xattn_pe(pe, L):
            s, m_, W = xs[L], xbs[L], WX[L]

            def t1(b, si):
                pe.wait_ge(s.ln_done, b + 1)
                for c in range(C):
                    m = nc.tensor.transpose(small(si)[:, c * P:(c + 1) * P], m_.xn[:, c * P:(c + 1) * P], ident[:, :])
                m.then_inc(s.small_done, 1)

            def proj(cols, w0, n, si):
                for c in range(C):
                    m = nc.tensor.matmul(small(si)[:, 0:n], cols[:, c, :], W[:, c, w0:w0 + n], start=(c == 0), stop=(c == C - 1))
                m.then_inc(s.small_done, 1)

            def kv(par, loads, si):
                pe.wait_ge(s.ctx_in[par], 16 * loads)
                proj(m_.cT[par], 0, 2 * D, si)

            def t2(b, si):
                if L:
                    pe.wait_ge(s.normed, b + 1)
                for c in range(C):
                    cols = slice(c * P, (c + 1) * P)
                    if L == 0:
                        nc.tensor.transpose(small(si)[:, cols], m_.kvs[:, cols], ident[:, :])
                    m = nc.tensor.transpose(small(si)[:, D + c * P:D + (c + 1) * P], m_.qs[:, cols], ident[:, :])
                m.then_inc(s.small_done, 1)

            def scores(par, j, first=0, last=4):
                c, h = j // 2, 4 * (j % 2)
                m = nc.tensor.matmul(PS[:, j, first * S:last * S], m_.qT[par][:, c, :], m_.k8T[par][:, c, h + first:h + last, :], start=True, stop=True)
                if j % 2 and last == 4:
                    m.then_inc(s.scores_done, 1)

            def pt(n, par, first):
                for i in (first, first + 1):
                    if i % 2 == 0:
                        pe.wait_ge(s.exp_done, 2 * n + i // 2 + 1)
                    if i >= 2:
                        pe.wait_ge(s.tr_free, 4 * n + i - 1)
                    for t in range(4):
                        m = nc.tensor.transpose(PS[:, 4 + i % 2, t * P:(t + 1) * P], m_.prob[par][:, 4 * i + t, :], ident[:, :])
                    m.then_inc(s.tr_done, 1)

            def pv(n, par, si, j):
                pe.wait_ge(s.tr_free, 4 * n + j + 1)
                o = small(si)[:, 0:XH * (XD + 1)].rearrange("p (h d) -> p h d", d=XD + 1)
                for h in range(4 * j, 4 * j + 4):
                    m = nc.tensor.matmul(o[:, h, :], m_.probT[:, h, :], m_.v17[:, bass.ds(n, 1), h, :].rearrange("p a d -> p (a d)"), start=True, stop=True)
                if j == 3:
                    m.then_inc(s.small_done, 1)

            def t3(si):
                for c in range(C):
                    m = nc.tensor.transpose(small(si)[:, c * P:(c + 1) * P], m_.cx[:, :, :].rearrange("p h d -> p (h d)")[:, c * P:(c + 1) * P], ident[:, :])
                m.then_inc(s.small_done, 1)

            def sequence(n, par, loads=None):
                k, si, a, d = counts(L, n, par)
                has_s, has_t2, has_next = parts_of(n)
                pt(n, par, 0)
                if has_next and not L:
                    pe.wait_ge(s.dve_free, d - 1)
                    kv(1 - par, loads, si)
                    si, d = si + 1, d + 1
                pt(n, par, 2)
                if has_t2:
                    pe.wait_ge(s.dve_free, d - 1)
                    t2(n + 2, si)
                    si, a = si + 1, a + 1
                if has_s:
                    pe.wait_ge(s.sub_done, 2 * n + 2)
                    scores(1 - par, 0)
                pe.wait_ge(s.dve_free, d)
                if L == 0:
                    pe.wait_ge(s.v_ready, n + 1)
                for j in range(4):
                    pv(n, par, si, j)
                    if has_s and j < 2:
                        scores(1 - par, j + 1)
                    elif has_s and j == 2:
                        scores(1 - par, 3, 0, 2)
                pe.wait_ge(s.act_free, a)
                if has_next:
                    t1(n + 3, si + 1)
                if has_s:
                    scores(1 - par, 3, 2, 4)
                if has_next:
                    pe.wait_ge(s.dve_free, d + 1)
                    t3(si + 2)
                    pe.wait_ge(s.act_free, a + 1)
                    proj(m_.xT, 2 * D, D, si + 3)
                    si, a = si + 2, a + 1
                else:
                    pe.wait_ge(s.dve_free, d + 1)
                    t3(si + 1)
                pe.wait_ge(s.act_free, a + 1)
                proj(m_.cxT, 3 * D, D, si + 2)

            def first_scores(j0, j1):
                for j in range(j0, j1):
                    scores(0, j)

            pe.wait_ge(wx_in[L], 16)
            if L == 0:
                kv(0, 1, 0)
                t1(0, 1)
                pe.wait_ge(s.dve_free, 1)
                pe.wait_ge(s.act_free, 1)
                proj(m_.xT, 2 * D, D, 2)
                t1(1, 3)
                pe.wait_ge(s.dve_free, 2)
                t2(0, 4)
                pe.wait_ge(s.act_free, 2)
                kv(1, 1, 5)
                pe.wait_ge(s.act_free, 3)
                proj(m_.xT, 2 * D, D, 6)
                pe.wait_ge(s.dve_free, 4)
                t2(1, 7)
                first_scores(0, 4)
            else:
                t1(0, 0)
                pe.wait_ge(s.act_free, 1)
                proj(m_.xT, 2 * D, D, 1)
                t1(1, 2)
                pe.wait_ge(s.dve_free, 1)
                t2(0, 3)
                pe.wait_ge(s.act_free, 3)
                first_scores(0, 2)
                proj(m_.xT, 2 * D, D, 4)
                first_scores(2, 4)
                pe.wait_ge(s.dve_free, 2)
                t2(1, 5)
            if L == 0:
                t1(2, 8)
                pe.wait_ge(s.act_free, 4)
                kv(0, 2, 9)
                pe.wait_ge(s.act_free, 5)
                proj(m_.xT, 2 * D, D, 10)
            else:
                t1(2, 6)
                pe.wait_ge(s.act_free, 5)
                proj(m_.xT, 2 * D, D, 7)
            with pe.Fori(0, LOOPED // 2) as i:
                sequence(2 * i, 0, i + 2)
                sequence(2 * i + 1, 1, i + 3)
            for n in range(LOOPED, B):
                sequence(n, n % 2, (n + 3) // 2 + 1)

        def split_lo(lo, src, hi):
            return nc.vector.tensor_tensor(lo, src, hi.bitcast(F32), ALU.subtract)

        def xattn_act(act, L):
            s, m_ = xs[L], xbs[L]

            def copy_cols(si, k, dst):
                act.wait_ge(s.small_done, k + 1)
                nc.scalar.activation(dst[:, :, :].rearrange("p c s -> p (c s)"), small(si)[:, 0:D], ACT.Copy).then_inc(s.act_free, 1)

            def masked_keys(kc, par):
                for h in range(HT):
                    nc.scalar.activation(m_.k8T[par][:, :, h, :], kc, ACT.Copy, scale=head_rows[:, h:h + 1])

            def masked_keys1(b, par):
                masked_keys(K1[:, bass.ds(b, 1), :].rearrange("p a (c s) -> p (a c) s", c=C), par)

            def t2(b, si, k, par):
                act.wait_ge(s.small_done, k + 1)
                if L == 0:
                    masked_keys(small(si)[:, 0:D].rearrange("p (c s) -> p c s", c=C), par)
                nc.scalar.activation(m_.qT[par][:, :, :].rearrange("p c s -> p (c s)"), small(si)[:, D:2 * D], ACT.Copy).then_inc(s.act_free, 1)
                if L and not (isinstance(b, int) and b < 2):
                    masked_keys1(b, par)

            def exps(b, par, gq):
                act.wait_ge(s.sub_done, 2 * b + gq + 1)
                pr_ = m_.prob[par][:, 8 * gq:8 * gq + 8, :]
                nc.scalar.activation(pr_, pr_, ACT.Exp, scale=XD ** -0.5).then_inc(s.exp_done, 1)

            def pt(n, i):
                act.wait_ge(s.tr_done, 4 * n + i + 1)
                nc.scalar.activation(m_.probT[:, 4 * i:4 * i + 4, :].rearrange("p t s -> p (t s)"), PS[:, 4 + i % 2, :], ACT.Copy).then_inc(s.tr_free, 1)

            def sequence(n, par):
                k, si, _, _ = counts(L, n, par)
                has_s, has_t2, has_next = parts_of(n)
                for i in range(4):
                    pt(n, i)
                if L and isinstance(n, int) and n == B - 1:
                    squares_act(act, z_done, 0, MOST)
                if has_next and not L:
                    k, si = k + 1, si + 1
                if has_t2:
                    t2(n + 2, si, k, par)
                    k, si = k + 1, si + 1
                if has_s:
                    exps(n + 1, 1 - par, 0)
                if has_next:
                    copy_cols(si + 1, k + 1, m_.xT)
                    k, si = k + 1, si + 1
                copy_cols(si + 1, k + 1, m_.cxT)
                if has_s:
                    exps(n + 1, 1 - par, 1)

            if L:
                for b in range(2):
                    masked_keys1(b, b)
                key_columns(act, MOST, B)
            uses = (0, 2, 3, 5, 6) if L else (1, 3, 4, 7, 8)
            copy_cols(uses[0], uses[0], m_.xT)
            copy_cols(uses[1], uses[1], m_.xT)
            t2(0, uses[2], uses[2], 0)
            if L:
                exps(0, 0, 0)
            t2(1, uses[3], uses[3], 1)
            if L == 0:
                exps(0, 0, 0)
            copy_cols(uses[4], uses[4], m_.xT)
            exps(0, 0, 1)
            with act.Fori(0, LOOPED // 2) as i:
                sequence(2 * i, 0)
                sequence(2 * i + 1, 1)
            for n in range(LOOPED, B):
                sequence(n, n % 2)

        def mean_square(src, tmp, dst):
            return nc.vector.tensor_tensor_reduce(out=tmp, in0=src, in1=src, scale=1.0 / D, scalar=RMS_EPS, op0=ALU.mult, op1=ALU.add, accum_out=dst)

        EARLY, MOST, FIRST = B // 2, B - 2, 2
        POWERS = [("ln1", 0, EARLY), ("ln1", EARLY, B), ("ln2", 0, MOST), ("ln2", MOST, B), ("ln3", 0, FIRST), ("ln3", FIRST, B),
                  ("ln4", 0, MOST), ("rms1", 0, MOST), ("ln4", MOST, B), ("rms1", MOST, B), ("rms2", 0, EARLY), ("rms2", EARLY, B)]

        def power(pool, norm, b0=0):
            use = [(n, a) for n, a, _ in POWERS].index((norm, b0))
            b1 = POWERS[use][2]
            if norm.startswith("ln"):
                pool.wait_ge(stats_done, 1 + sum(n.startswith("ln") for n, _, _ in POWERS[:use]))
            else:
                pool.wait_ge(squared, b1 if norm == "rms1" else B + b1)
                nc.gpsimd.tensor_scalar(ms[:, b0:b1], ms[:, b0:b1], RMS_EPS, None, ALU.add).then_inc(eps_done, 1)
                pool.wait_ge(eps_done, 1 + sum(n.startswith("rms") for n, _, _ in POWERS[:use]))
            nc.gpsimd.tensor_tensor(rstd[:, b0:b1], ms[:, b0:b1], mhalf[:, b0:b1], ALU.pow).then_inc(rstd_done, 1)

        def powered(dve, norm, b0=0):
            dve.wait_ge(rstd_done, 1 + [(n, a) for n, a, _ in POWERS].index((norm, b0)))

        def moments(ch, b0, b1):
            for b in range(b0, b1):
                i = nc.vector.bn_aggr(mv[:, b, :], st[:, b, :])
            ch.link(i)
            nc.vector.tensor_scalar(ms[:, b0:b1].unsqueeze(2), mv[:, b0:b1, 1:2], LN_EPS, None, ALU.add).then_inc(stats_done, 1)

        def ln_scale(out, src, b):
            return nc.vector.tensor_scalar(out, src, mv[:, b, 0:1], rstd[:, b:b + 1], ALU.subtract, ALU.mult)

        def xattn_ln(L, b):
            nc.vector.tensor_scalar(xbs[L].xn[:, :], X[:, b, :], mv[:, bass.ds(b, 1), 0], rstd[:, bass.ds(b, 1)], ALU.subtract, ALU.mult).then_inc(xs[L].ln_done, 1)

        def xattn_dve(dve, L, ch):
            s, m_ = xs[L], xbs[L]

            def ln(b):
                xattn_ln(L, b)

            def kv(b, si, k, d, t2=0):
                dve.wait_ge(s.small_done, k + 1 + t2)
                after(dve, s.v_ready, b)
                nc.vector.tensor_tensor(m_.kvs[:, :], small(si)[:, :], vecs[:, 0:2, :].rearrange("p a d -> p (a d)"), ALU.add).then_inc(s.dve_free, 1)

            def q(b, si, k, d):
                dve.wait_ge(s.small_done, k + 1)
                nc.vector.tensor_tensor(m_.qs[:, :], small(si)[:, 0:D], vec(f"bq{L}"), ALU.add).then_inc(s.dve_free, 1)
                if L:
                    dve.wait_ge(s.dve_free, d + 1)
                    mean_square(m_.qs[:, :], m_.junk[:, :], kms[:, 0:1]).then_inc(s.q_ready, 1)

            def normalise(b):
                dve.wait_ge(s.q_power, b + 1)
                nc.vector.scalar_tensor_tensor(out=m_.qs[:, :], in0=m_.qs[:, :], scalar=kms[:, 1:2], in1=vec("nq1"), op0=ALU.mult, op1=ALU.mult).then_inc(s.normed, 1)

            def softmax(b, par, gq):
                dve.wait_ge(s.scores_done, 2 * b + gq + 1)
                sc = PS[:, 2 * gq:2 * gq + 2, :].rearrange("p a (t s) -> p (a t) s", s=S)
                m8 = m_.mx[:, 8 * gq:8 * gq + 8]
                ch.link(nc.vector.tensor_reduce(m8, sc, AX.X, ALU.max))
                nc.vector.tensor_tensor(m_.prob[par][:, 8 * gq:8 * gq + 8, :], sc, m8.unsqueeze(2).broadcast_to([P, 8, S]), ALU.subtract).then_inc(s.sub_done, 1)

            def pv(si, k):
                dve.wait_ge(s.small_done, k + 1)
                o = small(si)[:, 0:XH * (XD + 1)].rearrange("p (h d) -> p h d", d=XD + 1)
                ch.link(nc.vector.reciprocal(m_.rden[:, :].unsqueeze(2), o[:, :, XD:XD + 1]))
                nc.vector.tensor_tensor(m_.cx[:, :, :], o[:, :, 0:XD], m_.rden[:, :].unsqueeze(2).broadcast_to([P, XH, XD]), ALU.mult).then_inc(s.dve_free, 1)

            def o(n, si, k, d):
                dve.wait_ge(s.small_done, k + 1)
                nc.vector.tensor_tensor(m_.otmp[:, :], small(si)[:, 0:D], vec(f"bo{L}"), ALU.add).then_inc(s.dve_free, 1)
                dve.wait_ge(s.dve_free, d + 1)
                ch.link(nc.vector.scalar_tensor_tensor(out=X[:, n, :], in0=m_.otmp[:, :], scalar=tg[:, L:L + 1], in1=X[:, n, :], op0=ALU.mult, op1=ALU.add))
                stats = nc.vector.bn_stats(st[:, n, :], X[:, n, :])
                if isinstance(n, int) and n in (MOST - 1, B - 1):
                    ch.link(stats)

            def sequence(n, par, more=True):
                k, si, _, d = counts(L, n, par)
                has_s, has_t2, has_next = parts_of(n)
                if has_next and not L:
                    kv(n + 3, si, k, d, 1)
                    k, si, d = k + 1, si + 1, d + 1
                if has_t2:
                    k, si = k + 1, si + 1
                if has_s:
                    softmax(n + 1, 1 - par, 0)
                pv(si, k)
                if has_s:
                    softmax(n + 1, 1 - par, 1)
                if has_next:
                    q(n + 3, si + 3, k + 3, d + 1)
                    if more:
                        ln(n + 4)
                    o(n, si + 4, k + 4, d + 2)
                    if L:
                        normalise(n + 3)
                else:
                    o(n, si + 2, k + 2, d + 1)

            if L == 0:
                powered(dve, "ln1")
                ln(0)
                for b in range(EARLY, B):
                    i = nc.vector.bn_stats(st[:, b, :], X[:, b, :])
                ch.link(i)
                moments(ch, EARLY, B)
                dve.wait_ge(vec_in, 16)
                dve.wait_ge(tg_done, 1)
                kv(0, 0, 0, 0)
                dve.wait_ge(s.small_done, 2)
                ln(1)
                q(0, 2, 2, 1)
                kv(1, 5, 5, 2)
                q(1, 6, 6, 3)
                ln(2)
                softmax(0, 0, 0)
                kv(2, 9, 9, 4)
                softmax(0, 0, 1)
                q(2, 10, 10, 5)
            else:
                for b in range(B):
                    add_experts(dve, ch, b)
                    if b == FIRST - 1:
                        moments(ch, 0, FIRST)
                        normalise_keys(dve, MOST, B, 2)
                    if b == 3:
                        powered(dve, "ln3")
                        ln(0)
                    if b == 5:
                        dve.wait_ge(s.small_done, 1)
                        ln(1)
                    if b == 6:
                        q(0, 1, 1, 0)
                moments(ch, FIRST, B)
                normalise(0)
                softmax(0, 0, 0)
                q(1, 4, 4, 1)
                powered(dve, "ln3", FIRST)
                ln(2)
                normalise(1)
                softmax(0, 0, 1)
                q(2, 7, 7, 2)
                normalise(2)
            ln(3)
            if L == 0:
                powered(dve, "ln1", EARLY)
            start, steps = ch.base + ch.n, 8
            with dve.Fori(0, LOOPED // 2) as i:
                ch.base, ch.n = start + i * steps, 0
                sequence(2 * i, 0)
                sequence(2 * i + 1, 1)
            ch.leave(start, steps, LOOPED // 2)
            for n in range(LOOPED, B):
                if n == MOST:
                    moments(ch, 0, MOST)
                sequence(n, n % 2, n + 4 < B)
                if n == MOST and L:
                    powered(dve, "ln4")
                    for b in range(MOST):
                        ln_scale(Z[:, b, :], X[:, b, :], b).then_inc(z_done, 1)

        def xattn_pool(pool, L):
            s, m_ = xs[L], xbs[L]

            def values(b, kv_read):
                pool_wait(pool, s.dve_free, kv_read)
                nc.gpsimd.tensor_copy(m_.v17[:, bass.ds(b, 1), :, 0:XD].rearrange("p a h d -> p (a h) d"),
                                      m_.kvs[:, D:2 * D].rearrange("p (h d) -> p h d", d=XD)).then_inc(s.v_ready, 1)

            def queries(b):
                pool_wait(pool, s.q_ready, b + 1)
                nc.gpsimd.tensor_tensor(kms[:, 1:2], kms[:, 0:1], mhalf[:, 0:1], ALU.pow).then_inc(s.q_power, 1)

            if L:
                queries(0)
                power(pool, "ln3", FIRST)
                with pool.Fori(1, B) as b:
                    queries(b)
            else:
                power(pool, "ln1")
                power(pool, "ln1", EARLY)
                for b in range(3):
                    values(b, 2 * b + 1)
                with pool.Fori(0, LOOPED) as n:
                    values(n + 3, PRE_D[0] + PER_D[0] * n + 1)
                for n in range(LOOPED, FULL):
                    values(n + 3, PRE_D[0] + PER_D[0] * n + 1)

        def xattn_sp(sp):
            s = xs[0]

            def load(b):
                sp.dma_start(xb0.cT[b % 2][:, :, :], ctx_d[b]).then_inc(s.ctx_in[b % 2], 16)

            def expert_weights(e):
                sp.dma_start(WE[:, e, :], moe0_d[e]).then_inc(Es.w_in, 16)

            load(0)
            sp.dma_start(WX[0][:, :, :], wx_d[0]).then_inc(wx_in[0], 16)
            sp.dma_start(vecs[:, 0:4, :].rearrange("p a d -> p (a d)"), vec_d[0:4 * D].partition_broadcast(P)).then_inc(vec_in, 16)
            load(1)
            sp.dma_start(rw[:, :, 0:E0], rw0_d).then_inc(late_in, 16)
            sp.dma_start(rw[:, :, E0:E0 + E1], rw1_d).then_inc(late_in, 16)
            sp.dma_start(vecs[:, 4:, :].rearrange("p a d -> p (a d)"), vec_d[4 * D:].partition_broadcast(P)).then_inc(late_in, 16)
            sp.dma_start(WX[1][:, :, :], wx_d[1]).then_inc(wx_in[1], 16)
            expert_weights(0)
            expert_weights(1)
            for b in range(2, B):
                sp.wait_ge(s.small_done, {2: 2, 3: 6, 4: 10}.get(b, PRE_SMALL[0] + PER_SMALL[0] * (b - 5) + 1))
                load(b)
                expert_weights(b)
            sp.wait_ge(Es.zeroed, 1)
            sp.dma_start(xs_d.rearrange("(j p) n -> p j n", p=P), zeros[:, 0:D].bitcast(F32).unsqueeze(1).broadcast_to([P, SLOTS, D])).then_inc(Es.zero_in, 16)

        def columns_pe(pe, src, ready, done, lo_done, first_half):
            for b in range(B):
                if b == B - 1:
                    first_half()
                pe.wait_ge(ready, b + 1)
                after(pe, lo_done, b - 3)
                for c in range(C):
                    m = nc.tensor.transpose(PS[:, 4 + b % 4, c * P:(c + 1) * P], src[b % 2][:, c * P:(c + 1) * P], ident[:, :])
                m.then_inc(done, 1)

        def column_bank(b):
            return PS[:, 4 + b % 4, 0:D].rearrange("p (c s) -> p c s", c=C)

        def columns_act(act, done, hi_done, before=lambda b: None):
            for b in range(B):
                act.wait_ge(done, b + 1)
                nc.scalar.activation(tT[:, :, b * S:(b + 1) * S], column_bank(b), ACT.Copy)
                nc.scalar.activation(tTh[:, :, b * S:(b + 1) * S], column_bank(b), ACT.Copy).then_inc(hi_done, 1)
                before(b + 1)

        def columns_lo(dve, b, hi_done, lo_done):
            dve.wait_ge(hi_done, b + 1)
            split_lo(tTl[:, :, b * S:(b + 1) * S], column_bank(b), tTh[:, :, b * S:(b + 1) * S]).then_inc(lo_done, 1)

        def squares_act(act, ready, b0=0, b1=B):
            sq = tT[:, :, :].rearrange("p c t -> p (c t)")
            for b in range(b0, b1):
                act.wait_ge(ready, b + 1)
                nc.scalar.activation(sq[:, b * D:(b + 1) * D], Z[:, b, :], ACT.Square, scale=D ** -0.5, accum_out=ms[:, b:b + 1]).then_inc(squared, 1)

        def loop_tiles(eng, body):
            for j in range(SJ):
                body(j, j % 2, j // 2)
            with eng.Fori(0, (J1 - SJ) // 2) as i:
                body(2 * i + SJ, 1, i + 1)
                body(2 * i + SJ + 1, 0, i + 2)

        def is_shared(j):
            return isinstance(j, int) and j < SJ

        def acc(half, c):
            return PS[:, 4 + 2 * half + c, :]

        def open_acc():
            for i in range(2 * C):
                nc.tensor.matmul(PS[:, 4 + i, :], zeros[:, 0:P], zeros[:, :], start=True, stop=False, skip_group_check=True)

        def moe_pe(pe):
            s = f1
            pe.wait_ge(late_in, 48)

            def logits():
                for b in range(B):
                    pe.wait_ge(s.tlo, b + 1)
                    for c in range(C):
                        m = nc.tensor.matmul(PS[:, 2, b * E1:(b + 1) * E1], tT[:, c, b * S:(b + 1) * S], rw[:, c, E0:], start=(c == 0), stop=(c == C - 1))
                m.then_inc(s.lg_done, 1)

            def product(u, half, par, mat):
                after(pe, (s.silu_done, s.a_done)[mat], u)
                t0 = half * HALF
                for c in range(C):
                    w0 = mat * D + c * P
                    m = three(pe, PS[:, mat, :], wh[par][:, w0:w0 + P], wl[par][:, w0:w0 + P],
                              tTh[:, c, t0:t0 + HALF], tTl[:, c, t0:t0 + HALF], c == 0, c == C - 1)
                m.then_inc((s.g_done, s.u_done)[mat], 1)

            def first_gate():
                pe.wait_ge(s.tlo, B // 2)
                pe.wait_ge(s.w_split, 2)
                product(0, 0, 0, 0)

            columns_pe(pe, fxn, s.n_done, s.t_done, s.tlo, first_gate)
            product(0, 0, 0, 1)
            logits()

            def down(u, half, par, split):
                opens = isinstance(u, int) and u < 2
                pe.wait_ge(s.w_split, split)
                pe.wait_ge(s.lo_done, u + 1)
                for c in range(C):
                    w0 = 2 * D + c * P
                    m = three(pe, acc(half, c), wh[par][:, w0:w0 + P], wl[par][:, w0:w0 + P], hhh[half][:, :], hhl[half][:, :], opens, True, skip_group_check=True)
                m.then_inc(s.d_done, 1)

            def tile(j, par, cnt):
                pe.wait_ge(s.w_split, 4 * j + 2)
                for half in range(2):
                    u = 2 * j + half
                    for mat in range(2):
                        if not (is_first(j) and half == 0):
                            product(u, half, par, mat)
                    if not is_shared(j):
                        if half == 0:
                            pe.wait_ge(s.sel_ready, j - SJ + 1)
                            pe.wait_ge(s.cwt_ready, 1)
                        pe.wait_ge(s.h_done, u)
                        nc.tensor.matmul(PS[:, 2, :], selj[par][:, :], cwT[:, half * HALF:(half + 1) * HALF], start=True, stop=True).then_inc(s.c_done, 1)
                    if half:
                        down(u - 1, 0, par, 4 * j + 4)
                    elif not is_first(j):
                        down(u - 1, 1, 1 - par, 4 * j)
                if isinstance(j, int) and j == SJ - 1:
                    pe.wait_ge(s.cw_done, 1)
                    psb = PS[:, 3, :].bitcast(BF16)
                    for b in range(B):
                        m = nc.tensor.transpose(psb[0:rows, b * P:(b + 1) * P], cw3[:, b, :, :].rearrange("p a e -> p (a e)"), identb[:, :])
                    m.then_inc(s.ct_done, 1)

            loop_tiles(pe, tile)
            pe.wait_ge(s.lo_done, 2 * J1)
            rows_pe(pe, yT, s.y_out, s.yt_done, s.tile_out, 0, B // 2)
            down(2 * J1 - 1, 1, (J1 - 1) % 2, 4 * J1)
            rows_pe(pe, yT, s.y_out, s.yt_done, s.tile_out, B // 2)

        def moe_act(act):
            s = f1
            def tile(j, par, cnt):
                for half in range(2):
                    if is_first(j) and half:
                        act.wait_ge(s.lg_out, 1)
                        nc.scalar.activation(pr[:, :, :], lg[:, :, :], ACT.Exp).then_inc(s.ex_done, 1)
                    u = 2 * j + half
                    act.wait_ge(s.g_done, u + 1)
                    after(act, s.a_done, u - 1)
                    nc.scalar.activation(act_s[half][:, :], PS[:, 0, :], ACT.Silu).then_inc(s.silu_done, 1)
                    act.wait_ge(s.h_done, u + 1)
                    after(act, s.d_done, u - 1)
                    nc.scalar.activation(hhh[half][:, :], hh[half][:, :], ACT.Copy).then_inc(s.hi_done, 1)
                if isinstance(j, int) and j == SJ - 1:
                    act.wait_ge(s.ct_done, 1)
                    nc.scalar.activation(cwT[:, :], PS[0:rows, 3, :].bitcast(BF16), ACT.Copy).then_inc(s.cwt_ready, 1)

            loop_tiles(act, tile)

        def moe_dve(dve, ch):
            s, v = f1, nc.vector

            def wide(x):
                return x.unsqueeze(2).broadcast_to([P, B, E1])

            def unit(u, half, shared):
                dve.wait_ge(s.u_done, u + 1)
                dve.wait_ge(s.silu_done, u + 1)
                if shared:
                    v.tensor_tensor(hh[half][:, :], act_s[half][:, :], PS[:, 1, :], ALU.mult).then_inc(s.h_done, 1)
                    dve.wait_ge(s.h_done, u + 1)
                    dve.sem_inc(s.a_done, 1)
                else:
                    v.tensor_tensor(act_s[half][:, :], act_s[half][:, :], PS[:, 1, :], ALU.mult).then_inc(s.a_done, 1)
                    dve.wait_ge(s.a_done, u + 1)
                    dve.wait_ge(s.c_done, u - 2 * SJ + 1)
                    v.tensor_tensor(hh[half][:, :], act_s[half][:, :], PS[:, 2, :], ALU.mult).then_inc(s.h_done, 1)
                dve.wait_ge(s.hi_done, u + 1)
                split_lo(hhl[half][:, :], hh[half][:, :], hhh[half][:, :]).then_inc(s.lo_done, 1)

            def logits():
                dve.wait_ge(s.lg_done, 1)
                scores = PS[:, 2, 0:B * E1].rearrange("p (b e) -> p b e", e=E1)
                ch.link(v.tensor_reduce(red[:, :], scores, AX.X, ALU.max))
                v.tensor_tensor(lg[:, :, :], scores, wide(red[:, :]), ALU.subtract).then_inc(s.lg_out, 1)
                ch.link(v.memset(cw3[:, :, :, :], 0.0))

            def probabilities():
                dve.wait_ge(s.ex_done, 1)
                ch.link(v.tensor_reduce(red[:, :], pr[:, :, :], AX.X, ALU.add))
                ch.link(v.reciprocal(red[:, :], red[:, :]))
                ch.link(v.tensor_tensor(pr[:, :, :], pr[:, :, :], wide(red[:, :]), ALU.mult))

            def largest():
                for b in range(B):
                    i = v.max(top8[:, b, :], pr[:, b, :])
                ch.link(i)
                ch.link(v.memset(top8[:, :, TOPK:8], -1.0))

            def chosen():
                for b in range(B):
                    i = v.match_replace(wk[:, b, :], top8[:, b, :], pr[:, b, :], -2.0)
                ch.link(i)
                ch.link(v.tensor_tensor(wk[:, :, :], wk[:, :, :], pr[:, :, :], ALU.not_equal))
                ch.link(v.tensor_tensor(wk[:, :, :], wk[:, :, :], pr[:, :, :], ALU.mult))

            def weights():
                ch.link(v.tensor_reduce(red[:, :], wk[:, :, :], AX.X, ALU.add))
                ch.link(v.reciprocal(red[:, :], red[:, :]))
                ch.link(v.tensor_tensor(cw[:, :, :], wk[:, :, :], wide(red[:, :]), ALU.mult))
                src = cw
                for part in range(2):
                    ch.link(v.tensor_copy(cw3[:, :, part, 0:E1], src[:, :, :]))
                    ch.link(v.tensor_tensor(cr[:, :, :], src[:, :, :], cw3[:, :, part, 0:E1], ALU.subtract))
                    src = cr
                v.tensor_copy(cw3[:, :, 2, 0:E1], cr[:, :, :]).then_inc(s.cw_done, 1)

            def residual(b):
                ch.link(v.scalar_tensor_tensor(out=X[:, b:b + 2, :], in0=Z[:, b:b + 2, :], scalar=tg[:, 3:4], in1=X[:, b:b + 2, :], op0=ALU.mult, op1=ALU.add))

            for u, step in enumerate((logits, probabilities, largest, chosen, weights, None)):
                unit(u, u % 2, True)
                if step:
                    step()
                if u >= 2:
                    residual(2 * u - 4)
            with dve.Fori(0, (J1 - SJ) // 2) as i:
                for k in range(4):
                    unit(4 * i + 2 * SJ + k, k % 2, False)

        def moe_pool(pool):
            s = f1

            def split(j, par, a0, a1, k):
                nc.gpsimd.tensor_copy(wh[par][:, a0:a1], wraw[par][:, a0:a1]).then_inc(s.w_split, 1)
                pool_wait(pool, s.w_split, 4 * j + k + 1)
                nc.gpsimd.tensor_tensor(wl[par][:, a0:a1], wraw[par][:, a0:a1], wh[par][:, a0:a1].bitcast(F32), ALU.subtract).then_inc(s.w_split, 1)

            def tile(j, par, cnt):
                pool_wait(pool, s.w_in[par], 16 * cnt + 16)
                early = isinstance(j, int) and j < 2
                if not early:
                    pool_wait(pool, s.u_done, 2 * j - 2)
                split(j, par, 0, 2 * D, 0)
                if not early:
                    pool_wait(pool, s.d_done, 2 * j - 2)
                split(j, par, 2 * D, 3 * D, 2)
                if not is_shared(j):
                    nc.gpsimd.tensor_copy(selj[par][:, :], sel[:, bass.ds((j - SJ) * P, P)]).then_inc(s.sel_ready, 1)

            loop_tiles(pool, tile)

        def moe_sp(sp):
            s = f1

            def tile(j, par, cnt):
                after(sp, s.w_split, 4 * j - 4)
                sp.dma_start(wraw[par][:, :], moe1_d[bass.ds(j, 1), :, :].rearrange("a p n -> (a p) n")).then_inc(s.w_in[par], 16)

            loop_tiles(sp, tile)

        def rows_pe(pe, cols, out, done, free, b0=0, b1=B):
            for b in range(b0, b1):
                pe.wait_ge(out, C * (1 + b // (B // 2)))
                after(pe, free, b - 3)
                for c in range(C):
                    m = nc.tensor.transpose(PS[:, b % 4, c * P:(c + 1) * P], cols[:, c, b * S:(b + 1) * S], ident[:, :])
                m.then_inc(done, 1)

        def acc_act(act, cols, acc_done, halves_done, out):
            for half in range(2):
                act.wait_ge(acc_done, halves_done[half])
                for c in range(C):
                    nc.scalar.activation(cols[:, c, half * HALF:(half + 1) * HALF], acc(half, c), ACT.Copy).then_inc(out, 1)

        def slots(eng, body):
            for j in range(3):
                body(j, j % 2, (j - 3) // 2 if j % 2 else (j - 4) // 2)
            pairs = (SLOTS - 5) // 2
            with eng.Fori(0, pairs) as i:
                body(2 * i + 3, 1, i)
                body(2 * i + 4, 0, i)
            for j in (SLOTS - 2, SLOTS - 1):
                body(j, j % 2, pairs)

        def is_last(j):
            return isinstance(j, int) and j == SLOTS - 1

        def is_first(j):
            return isinstance(j, int) and j == 0

        def tile_rows(d, j):
            return d.rearrange("(j p) n -> j p n", p=P)[bass.ds(j, 1), :, :].rearrange("a p n -> (a p) n")

        def ffn_pe(pe):
            s = Es
            pe.wait_ge(late_in, 48)
            for b in range(B):
                pe.wait_ge(s.n_done, b + 1)
                after(pe, s.t_free, b - 3)
                for c in range(C):
                    m = nc.tensor.transpose(PS[:, 4 + b % 4, c * P:(c + 1) * P], FX[:, b, c * P:(c + 1) * P], ident[:, :])
                m.then_inc(s.t_done, 1)
            for b in range(B):
                pe.wait_ge(s.t_free, b + 1)
                for c in range(C):
                    m = nc.tensor.matmul(PS[:, 2, b * E0:(b + 1) * E0], rT[:, c, b * S:(b + 1) * S], rw[:, c, 0:E0], start=(c == 0), stop=(c == C - 1))
            m.then_inc(s.lg_done, 1)
            pe.wait_ge(s.hot_done, 1)
            pl = PS[:, 3, 0:(B + 1) * E0].rearrange("p (b e) -> p b e", e=E0)
            nc.tensor.matmul(pl, earlier[:, :], hot[:, 1:, :], start=True, stop=False)
            pe.wait_ge(s.sums_done, 1)
            nc.tensor.matmul(pl, ones[:, :], sums_to[2][:, 3:, :], start=False, stop=True).then_inc(s.place_done, 1)

            def keys_values(b):
                for c in range(C):
                    m = nc.tensor.matmul(kv_bank(b), rT[:, c, b * S:(b + 1) * S], WX[1][:, c, 0:2 * D], start=(c == 0), stop=(c == C - 1))
                m.then_inc(s.kv_done, 1)

            pe.wait_ge(s.ctx_in, 16 * C)
            pe.wait_ge(wx_in[1], 16)
            for b in range(MOST):
                after(pe, s.kv_free, 2 * b - 6)
                keys_values(b)

            def columns(par, loads):
                pe.wait_ge(s.xs_in[par], 16 * loads)
                for c in range(C):
                    m = nc.tensor.transpose(PS[:, 5, c * P:(c + 1) * P], xs_s[par][:, c * P:(c + 1) * P], ident[:, :])
                m.then_inc(s.xt_done, 1)

            def up(e, par, mat, done):
                w = WE[:, bass.ds(e, 1), mat * C * I0:(mat + 1) * C * I0].rearrange("p a (c n) -> p (a c) n", c=C)
                for c in range(C):
                    m = nc.tensor.matmul(PS[:, 2 * mat + par, :], xsT[par][:, c, :], w[:, c, :], start=(c == 0), stop=(c == C - 1))
                m.then_inc(done, 1)

            def turn_hidden(j):
                pe.wait_ge(s.h_ready, j + 1)
                for k in range(I0 // P):
                    m = nc.tensor.transpose(PS[:, 4, k * P:(k + 1) * P], hs[:, k * P:(k + 1) * P], ident[:, :])
                m.then_inc(s.ht_done, 1)

            def down(j, par):
                e = pe.value_load(ex[0:1, bass.ds(j, 1)], min_val=0, max_val=E0 - 1)
                pe.wait_ge(s.ht_ready, j + 1)
                w = WE[:, bass.ds(e, 1), 2 * C * I0:EW].rearrange("p a (k n) -> p (a k) n", n=D)
                for k in range(I0 // P):
                    m = nc.tensor.matmul(PS[:, 6 + par, 0:D], hT[:, k, :], w[:, k, :], start=(k == 0), stop=(k == I0 // P - 1))
                m.then_inc(s.d_done, 1)

            def tile(j, par, i):
                e = pe.value_load(ex[0:1, bass.ds(j, 1)], min_val=0, max_val=E0 - 1)
                pe.wait_ge(s.xt_ready, j + 1)
                up(e, par, 0, s.g_done)
                if not is_first(j):
                    turn_hidden(j - 1)
                if not is_last(j):
                    columns(1 - par, i + 3)
                up(e, par, 1, s.u_done)
                if not is_first(j):
                    down(j - 1, 1 - par)

            pe.wait_ge(s.experts_done, 1)
            pe.wait_ge(s.w_in, 16 * E0)
            pe.wait_ge(s.kv_free, 2 * MOST)
            columns(0, 1)
            slots(pe, tile)
            turn_hidden(SLOTS - 1)
            down(SLOTS - 1, (SLOTS - 1) % 2)
            for b in range(MOST, B):
                keys_values(b)
            for b in range(B):
                pe.wait_ge(s.k1_ready, 1 if b < MOST else 2)
                after(pe, s.kt_free, b - 3)
                for c in range(C):
                    m = nc.tensor.transpose(PS[:, b % 4, c * P:(c + 1) * P], K1[:, b, c * P:(c + 1) * P], ident[:, :])
                m.then_inc(s.kt_done, 1)

        def key_columns(act, b0, b1):
            for b in range(b0, b1):
                act.wait_ge(Es.kt_done, b + 1)
                nc.scalar.activation(K1[:, b, :], PS[:, b % 4, 0:D], ACT.Copy).then_inc(Es.kt_free, 1)

        def ffn_act(act):
            s = Es
            for b in range(B):
                act.wait_ge(s.t_done, b + 1)
                nc.scalar.activation(rT[:, :, b * S:(b + 1) * S], column_bank(b), ACT.Copy).then_inc(s.t_free, 1)
            act.wait_ge(s.lg_done, 1)
            nc.scalar.activation(rexp[:, :, :].rearrange("p b e -> p (b e)"), PS[:, 2, 0:B * E0], ACT.Exp, scale=-1.0).then_inc(s.ex_done, 1)

            def columns(j, par):
                act.wait_ge(s.xt_done, j + 1)
                nc.scalar.activation(xsT[par][:, :, :].rearrange("p c s -> p (c s)"), PS[:, 5, 0:D], ACT.Copy).then_inc(s.xt_ready, 1)

            def hidden_columns(j):
                act.wait_ge(s.ht_done, j + 1)
                nc.scalar.activation(hT[:, :, :].rearrange("p k s -> p (k s)"), PS[:, 4, :], ACT.Copy).then_inc(s.ht_ready, 1)

            def tile(j, par, i):
                act.wait_ge(s.g_done, j + 1)
                nc.scalar.activation(gs[par][:, :], PS[:, par, :], ACT.Silu).then_inc(s.silu_done, 1)
                if not is_first(j):
                    hidden_columns(j - 1)
                if not is_last(j):
                    columns(j + 1, 1 - par)

            columns(0, 0)
            slots(act, tile)
            hidden_columns(SLOTS - 1)
            key_columns(act, 0, MOST)

        def kv_bank(b):
            return PS[:, 4 + (b % 4 if b < MOST else b - MOST), :]

        def normalise_keys(dve, b0, b1, group):
            dve.wait_ge(Es.krs_done, group)
            for b in range(b0, b1):
                i = nc.vector.scalar_tensor_tensor(out=K1[:, b, :], in0=K1[:, b, :], scalar=krs8[:, b:b + 1], in1=vec("nk1"), op0=ALU.mult, op1=ALU.mult)
            i.then_inc(Es.k1_ready, 1)

        def add_experts(dve, ch, b):
            dve.wait_ge(Es.gathered[b], 16)
            ch.link(nc.vector.scalar_tensor_tensor(out=X[:, b, :], in0=FX[:, b, :], scalar=rmax[:, b:b + 1], in1=X[:, b, :], op0=ALU.mult, op1=ALU.add))
            stats = nc.vector.bn_stats(st[:, b, :], X[:, b, :])
            if b in (FIRST - 1, B - 1):
                ch.link(stats)

        def ffn_dve(dve, ch):
            s, v = Es, nc.vector
            powered(dve, "ln2")
            for b in range(B):
                if b == MOST:
                    powered(dve, "ln2", MOST)
                ln_scale(FX[:, b, :], X[:, b, :], b).then_inc(s.n_done, 1)
            v.memset(hot[:, 0, :], 0.0)
            v.memset(hot[:, B + 1, :], 0.0)
            for sums_ in sums_to:
                i = v.memset(sums_[:, 0:4, :], 0.0)
            ch.link(i)
            dve.wait_ge(s.ex_done, 1)
            ch.link(v.tensor_scalar(rexp[:, :, :], rexp[:, :, :], 1.0, None, ALU.add))
            ch.link(v.reciprocal(route[:, :, :], rexp[:, :, :]))
            ch.link(v.tensor_reduce(rmax[:, :], route[:, :, :], AX.X, ALU.max))
            ch.link(v.tensor_tensor(rexp[:, :, :], route[:, :, :], rmax[:, :].unsqueeze(2).broadcast_to([P, B, E0]), ALU.is_equal))
            ch.link(v.tensor_tensor(rexp[:, :, :], rexp[:, :, :], rank8[:, :].unsqueeze(1).broadcast_to([P, B, E0]), ALU.mult))
            ch.link(v.tensor_reduce(rfirst[:, :], rexp[:, :, :], AX.X, ALU.max))
            tokens_hot = hot[:, 1:B + 1, :]
            v.tensor_tensor(tokens_hot, rexp[:, :, :], rfirst[:, :].unsqueeze(2).broadcast_to([P, B, E0]), ALU.is_equal).then_inc(s.hot_done, 1)
            dve.wait_ge(s.hot_done, 1)
            ch.link(v.tensor_tensor(sums_to[0][:, 4:, :], tokens_hot, hot[:, 0:B, :], ALU.add))
            ch.link(v.tensor_tensor(sums_to[1][:, 4:, :], sums_to[0][:, 4:, :], sums_to[0][:, 2:B + 2, :], ALU.add))
            v.tensor_tensor(sums_to[2][:, 4:, :], sums_to[1][:, 4:, :], sums_to[1][:, 0:B, :], ALU.add).then_inc(s.sums_done, 1)
            ch.link(v.tensor_scalar(rmax[:, :], rmax[:, :], tg[:, 2:3], None, ALU.mult))
            dve.wait_ge(s.place_done, 1)
            ch.link(v.tensor_copy(place[:, :, :].rearrange("p b e -> p (b e)"), PS[:, 3, 0:(B + 1) * E0]))
            ch.link(v.tensor_scalar(starts[:, :], place[:, B, :], 1.0 / P, None, ALU.mult))
            ch.link(v.tensor_tensor(more_than[:, :, :], starts[:, :].unsqueeze(2).broadcast_to([P, E0, B]),
                                    expert_ids[:, :].unsqueeze(1).broadcast_to([P, E0, B]), ALU.is_gt))
            ch.link(v.tensor_reduce(tiles_of[:, :], more_than[:, :, :], AX.X, ALU.add))
            ch.link(v.tensor_tensor(more_than[:, :, :], upto[:, :, :], tiles_of[:, :].unsqueeze(1).broadcast_to([P, E0, E0]), ALU.mult))
            ch.link(v.tensor_reduce(ends[:, :], more_than[:, :, :], AX.X, ALU.add))
            ch.link(v.tensor_tensor(starts[:, :], ends[:, :], tiles_of[:, :], ALU.subtract))
            ch.link(v.tensor_scalar(starts[:, :], starts[:, :], float(P), None, ALU.mult))
            ch.link(v.tensor_tensor(place[:, 0:B, :], place[:, 0:B, :], starts[:, :].unsqueeze(1).broadcast_to([P, B, E0]), ALU.add))
            ch.link(v.tensor_tensor(place[:, 0:B, :], place[:, 0:B, :], tokens_hot, ALU.mult))
            ch.link(v.tensor_reduce(posf[:, :], place[:, 0:B, :], AX.X, ALU.add))
            v.tensor_copy(pos[:, :], posf[:, :]).then_inc(s.pos_done, 1)
            ch.link(v.tensor_tensor(below[:, :, :], ends[:, :].unsqueeze(1).broadcast_to([P, SLOTS, E0]),
                                    tile_ids[:, :].unsqueeze(2).broadcast_to([P, SLOTS, E0]), ALU.is_le))
            ch.link(v.tensor_reduce(exf[:, :], below[:, :, :], AX.X, ALU.add))
            ch.link(v.tensor_scalar(exf[:, :], exf[:, :], float(E0 - 1), None, ALU.min))
            v.tensor_copy(ex[:, :], exf[:, :]).then_inc(s.experts_done, 1)

            def keys_values(b0, b1):
                for b in range(b0, b1):
                    dve.wait_ge(s.kv_done, b + 1)
                    v.tensor_tensor(K1[:, b, :], kv_bank(b)[:, 0:D], vec("bk1"), ALU.add).then_inc(s.kv_free, 1)
                    v.tensor_tensor(V1[:, b, :, 0:XD], kv_bank(b)[:, D:2 * D].rearrange("p (h d) -> p h d", d=XD),
                                    vec("bv1").rearrange("p (h d) -> p h d", d=XD), ALU.add).then_inc(s.kv_free, 1)
                    dve.wait_ge(s.kv_free, 2 * b + 1)
                    i = mean_square(K1[:, b, :], kjunk[:, :], kms8[:, b:b + 1])
                    if b < b1 - 1:
                        ch.link(i)
                i.then_inc(s.kms_done, 1)

            dve.wait_ge(late_in, 48)
            ch.link(v.memset(V1[:, :, :, XD:XD + 1], 1.0))
            keys_values(0, MOST)
            normalise_keys(dve, 0, MOST, 1)

            def output_rows(j, par, stores):
                dve.wait_ge(s.d_done, j + 1)
                after(dve, s.y_out[par], 16 * stores)
                v.tensor_copy(y_s[par][:, :], PS[:, 6 + par, 0:D]).then_inc(s.y_ready, 1)

            def tile(j, par, i):
                dve.wait_ge(s.u_done, j + 1)
                dve.wait_ge(s.silu_done, j + 1)
                v.tensor_tensor(hs[:, :], gs[par][:, :], PS[:, 2 + par, :], ALU.mult).then_inc(s.h_ready, 1)
                if not is_first(j):
                    output_rows(j - 1, 1 - par, i + 1)

            slots(dve, tile)
            output_rows(SLOTS - 1, (SLOTS - 1) % 2, (SLOTS - 1) // 2)
            dve.wait_ge(s.kms_done, 1)
            keys_values(MOST, B)

        def ffn_pool(pool):
            s = Es
            power(pool, "ln2", MOST)
            pool.wait_ge(s.n_done, B)
            pool.wait_ge(s.zero_in, 16)
            pool.wait_ge(s.pos_done, 1)
            for b in range(B):
                nc.gpsimd.indirect_dma_start(xs_d, bass.IndirectOffsetOnAxis(pos[:, b:b + 1], 0), FX[:, b, :], None).then_inc(s.scattered, 16)
            def keys_power(b0, b1, group):
                pool.wait_ge(s.kms_done, group)
                nc.gpsimd.tensor_tensor(krs8[:, b0:b1], kms8[:, b0:b1], mhalf[:, b0:b1], ALU.pow).then_inc(s.krs_done, 1)

            keys_power(0, MOST, 1)
            for par in range(2):
                pool.wait_ge(s.y_out[par], 16 * ((SLOTS + 1 - par) // 2))
            for b in range(B):
                nc.gpsimd.indirect_dma_start(FX[:, b, :], None, ys_d, bass.IndirectOffsetOnAxis(pos[:, b:b + 1], 0)).then_inc(s.gathered[b], 16)
                if b == FIRST:
                    keys_power(MOST, B, 2)
                if b == FIRST + 2:
                    power(pool, "ln3")

        def ffn_sp(sp):
            s = Es

            def load(j, par):
                sp.dma_start(xs_s[par][:, :], tile_rows(xs_d, j)).then_inc(s.xs_in[par], 16)

            def store(j, par):
                sp.wait_ge(s.y_ready, j + 1)
                sp.dma_start(tile_rows(ys_d, j), y_s[par][:, :]).then_inc(s.y_out[par], 16)

            def tile(j, par, i):
                if not (isinstance(j, int) and j + 2 >= SLOTS):
                    sp.wait_ge(s.xt_done, j + 1)
                    load(j + 2, par)
                if not is_first(j):
                    store(j - 1, 1 - par)

            sp.wait_ge(s.lg_done, 1)
            for c in range(C):
                sp.dma_start(rT[:, c, :].rearrange("p (b s) -> p b s", b=B), ctx_d[:, :, c, :].rearrange("b p s -> p b s")).then_inc(s.ctx_in, 16)
            sp.wait_ge(s.scattered, 16 * B)
            load(0, 0)
            load(1, 1)
            slots(sp, tile)
            store(SLOTS - 1, (SLOTS - 1) % 2)

        PRE_RING, PER_RING, PRE_RA, PRE_RD, PER_R = 8, 12, 6, 2, 6
        LOOPS = (AH - 4) // 4

        def attn_pe(pe):
            def proj(h, par, which, half, si):
                w, bank = which * D, PS[:, si % 4, :]
                for c in range(C):
                    m = three(pe, bank, ah[par][:, w + c * P:w + (c + 1) * P], al[par][:, w + c * P:w + (c + 1) * P],
                              tTh[:, c, half * HALF:(half + 1) * HALF], tTl[:, c, half * HALF:(half + 1) * HALF], c == 0, c == C - 1)
                m.then_inc(ring_done, 1)

            def values(k, si):
                for t in range(2):
                    t0 = (2 * k + t) * S
                    for c in range(C):
                        m = three(pe, PS[:, si % 4, t * 2 * AD:(t + 1) * 2 * AD], tTh[:, c, t0:t0 + S], tTl[:, c, t0:t0 + S],
                                  avh[:, c, :], avl[:, c, :], c == 0, c == C - 1)
                m.then_inc(ring_done, 1)

            def pairs(lhs, rhs, half, si):
                for t in range(4):
                    a0 = half * HALF + t * S
                    m = nc.tensor.matmul(PS[:, si % 4, t * S:(t + 1) * S], lhs[:, a0:a0 + S], rhs[:, a0:a0 + S], start=True, stop=True)
                m.then_inc(ring_done, 1)

            def turn(h, half, si):
                pe.wait_ge(norm_done, 2 * h + half + 1)
                for t in range(4):
                    m = nc.tensor.transpose(PS[:, si % 4, t * S:(t + 1) * S], sm[:, 4 * half + t, :], ident[:, :])
                m.then_inc(ring_done, 1)

            def wo(h, par, last=False):
                pe.wait_ge(aw_split, 4 * h + 4)
                for half in range(2):
                    for c in range(C):
                        w0 = 2 * D + c * P
                        m = three(pe, acc(half, c), ah[par][:, w0:w0 + P], al[par][:, w0:w0 + P],
                                  oTh[:, half * HALF:(half + 1) * HALF], oTl[:, half * HALF:(half + 1) * HALF], False, True, skip_group_check=True)
                    if half or last:
                        m.then_inc(wo_done, 1)

            def head(h, place, pair, first=False):
                si, par, n = PRE_RING, place % 2, 1 - place % 2
                a, d = PRE_RA + PER_R * h, PRE_RD + PER_R * h
                pe.wait_ge(ring_act, a)
                pe.wait_ge(ring_dve, d if first else d - 2)
                pairs(qT_[par], kT_[par], 0, si)
                pe.wait_ge(aw_split, 4 * h + 6)
                proj(h + 1, n, 0, 0, si + 1)
                pe.wait_ge(ring_dve, d if first else d - 1)
                pairs(qT_[par], kT_[par], 1, si + 2)
                pe.wait_ge(ring_dve, d)
                proj(h + 1, n, 0, 1, si + 3)
                if not first:
                    wo(h - 1, n)
                pe.wait_ge(ring_dve, d + 1)
                proj(h + 1, n, 1, 0, si + 4)
                pe.wait_ge(ring_act, a + 1)
                proj(h + 1, n, 1, 1, si + 5)
                pe.wait_ge(ring_dve, d + 2)
                turn(h, 0, si + 6)
                pe.wait_ge(ring_act, a + 2)
                turn(h, 1, si + 7)
                if pair is not None:
                    pe.wait_ge(av_split, 2 * pair + 2)
                    for u in range(2):
                        pe.wait_ge(ring_dve, d + 3 + u)
                        values(2 * par + u, si + 8 + u)
                for half in range(2):
                    pe.wait_ge(ring_act, a + 3 + half)
                    if pair is None:
                        pe.wait_ge(ring_dve, d + 3 + half)
                    pairs(v4[:, place, :], pT, half, si + (8 if pair is None else 10) + half)

            def last_head(h, par):
                si, a, d = PRE_RING - 2, PRE_RA + PER_R * h - 2, PRE_RD + PER_R * h
                pe.wait_ge(ring_act, a)
                pe.wait_ge(ring_dve, d - 2)
                pairs(qT_[par], kT_[par], 0, si)
                pairs(qT_[par], kT_[par], 1, si + 1)
                pe.wait_ge(ring_dve, d)
                wo(h - 1, 1 - par)
                turn(h, 0, si + 2)
                turn(h, 1, si + 3)
                for half in range(2):
                    pe.wait_ge(ring_dve, d + 1 + half)
                    pe.wait_ge(ring_act, a + 1 + half)
                    pairs(v4[:, h % 4, :], pT, half, si + 4 + half)
                pe.wait_ge(ring_dve, d + 4)
                wo(h, par, True)

            def first_queries():
                pe.wait_ge(tlo_done, B // 2)
                pe.wait_ge(aw_split, 2)
                proj(0, 0, 0, 0, 0)

            columns_pe(pe, gxn, n_done, t_done, tlo_done, first_queries)
            pe.wait_ge(tlo_done, B)
            for i, (which, half) in enumerate(((0, 1), (1, 0), (1, 1))):
                proj(0, 0, which, half, i + 1)
            open_acc()
            pe.wait_ge(av_split, 2)
            for k in range(4):
                pe.wait_ge((ring_act, ring_dve)[k // 2], k % 2 + 1)
                values(k, 4 + k)
            head(0, 0, 1, True)
            with pe.Fori(0, LOOPS) as i:
                for k in range(1, 5):
                    head(4 * i + k, k % 4, 2 * i + k // 2 + 1)
            head(AH - 3, 1, AH // 2 - 1)
            head(AH - 2, 2, None)
            last_head(AH - 1, 1)

        def attn_act(act):
            def copy(dst, half, r, si, done):
                act.wait_ge(ring_done, r + 1)
                nc.scalar.activation(dst[:, half * HALF:(half + 1) * HALF], PS[:, si % 4, :], ACT.Copy).then_inc(done, 1)

            def exps(h, half):
                act.wait_ge(masked, 2 * h + half + 1)
                for t in range(4):
                    b = 4 * half + t
                    nc.scalar.activation(sm[:, b, :], sm[:, b, :], ACT.Exp, bias=nmx[:, b:b + 1], scale=AD ** -0.5,
                                         accum_out=sums[:, b:b + 1]).then_inc(aexp_done, 1)

            def values(k, place, r, si):
                act.wait_ge(ring_done, r + 1)
                nc.scalar.activation(v4[:, place:place + 2, 2 * k * S:(2 * k + 2) * S].rearrange("p s (t d) -> p s t d", d=AD),
                                     PS[:, si % 4, :].rearrange("p (t s d) -> p s t d", s=2, d=AD), ACT.Copy).then_inc(ring_act, 1)

            def head(h, place, last=False, makes_values=True):
                par, n, late = place % 2, 1 - place % 2, 2 if last else 0
                r, si = PRE_RING + h * PER_RING - late, PRE_RING - late
                at, vt = (2, 4) if last else (6, 10 if makes_values else 8)
                for half in range(2):
                    exps(h, half)
                    if not last:
                        copy(qT_[n], half, r + 1 + 2 * half, si + 1 + 2 * half, ring_act)
                for half in range(2):
                    copy(pT, half, r + at + half, si + at + half, ring_act)
                if makes_values:
                    for u in range(2):
                        values(2 * par + u, (place // 2 * 2 + 2) % 4, r + 8 + u, si + 8 + u)
                for half in range(2):
                    copy(oTh, half, r + vt + half, si + vt + half, ahi_done)

            for half in range(2):
                copy(qT_[0], half, half, half, ring_act)
            for k in range(4):
                values(k, 0, 4 + k, 4 + k)
            head(0, 0)
            with act.Fori(0, LOOPS) as i:
                for k in range(1, 5):
                    head(4 * i + k, k % 4)
            head(AH - 3, 1)
            head(AH - 2, 2, makes_values=False)
            head(AH - 1, 3, True, False)

        def attn_dve(dve, ch):
            v = nc.vector

            def keys(dst, half, r, si):
                dve.wait_ge(ring_done, r + 1)
                v.tensor_copy(dst[:, half * HALF:(half + 1) * HALF], PS[:, si % 4, :]).then_inc(ring_dve, 1)

            def low_part(h, half, si):
                dve.wait_ge(ahi_done, 2 * h + half + 1)
                cols = slice(half * HALF, (half + 1) * HALF)
                split_lo(oTl[:, cols], PS[:, si % 4, :], oTh[:, cols]).then_inc(ring_dve, 1)

            def mask(h, half, r, si, d):
                dve.wait_ge(ring_done, r + 1)
                part = sm[:, 4 * half:4 * half + 4, :]
                v.tensor_tensor(part, PS[:, si % 4, :].rearrange("p (t s) -> p t s", s=S),
                                causal[:, :].unsqueeze(1).broadcast_to([P, 4, S]), ALU.add).then_inc(ring_dve, 1)
                dve.wait_ge(ring_dve, d + 1)
                m4 = nmx[:, 4 * half:4 * half + 4]
                ch.link(v.tensor_reduce(m4, part, AX.X, ALU.max))
                v.tensor_scalar(m4, m4, -(AD ** -0.5), None, ALU.mult).then_inc(masked, 1)

            def norm(h, half):
                dve.wait_ge(aexp_done, 8 * h + 4 * half + 4)
                part = sm[:, 4 * half:4 * half + 4, :]
                r4 = rsum[:, 4 * half:4 * half + 4]
                ch.link(v.reciprocal(r4, sums[:, 4 * half:4 * half + 4]))
                v.tensor_tensor(part, part, r4.unsqueeze(2).broadcast_to([P, 4, S]), ALU.mult).then_inc(norm_done, 1)

            def head(h, par, last=False, with_values=True):
                n, late = 1 - par, 2 if last else 0
                r, si, d = PRE_RING + h * PER_RING - late, PRE_RING - late, PRE_RD + PER_R * h
                step, vt = (1, 4) if last else (2, 10 if with_values else 8)
                for half in range(2):
                    mask(h, half, r + step * half, si + step * half, d + half)
                for half in range(2):
                    norm(h, half)
                if not last:
                    for half in range(2):
                        keys(kT_[n], half, r + 4 + half, si + 4 + half)
                for half in range(2):
                    low_part(h, half, si + vt + half)

            for half in range(2):
                keys(kT_[0], half, 2 + half, 2 + half)
            head(0, 0)
            start, steps = ch.base + ch.n, 16
            with dve.Fori(0, LOOPS) as i:
                ch.base, ch.n = start + i * steps, 0
                for k in range(1, 5):
                    head(4 * i + k, k % 2)
            ch.leave(start, steps, LOOPS)
            head(AH - 3, 1)
            head(AH - 2, 0, with_values=False)
            head(AH - 1, 1, True)

        def attn_pool(pool):
            def split(h, par, dst, src, n, k):
                nc.gpsimd.tensor_copy(ah[par][:, dst:dst + n], araw[par][:, src:src + n]).then_inc(aw_split, 1)
                pool_wait(pool, aw_split, 4 * h + k + 1)
                nc.gpsimd.tensor_tensor(al[par][:, dst:dst + n], araw[par][:, src:src + n], ah[par][:, dst:dst + n].bitcast(F32), ALU.subtract).then_inc(aw_split, 1)

            def value_weights(m):
                pool_wait(pool, av_in, 16 * m + 16)
                if isinstance(m, int) and m == 1:
                    pool_wait(pool, ring_done, PRE_RING)
                elif not (isinstance(m, int) and m == 0):
                    pool_wait(pool, ring_done, PRE_RING + (2 * m - 3) * PER_RING + 10)
                nc.gpsimd.tensor_copy(avh[:, :, :], avraw[:, :, :]).then_inc(av_split, 1)
                pool_wait(pool, av_split, 2 * m + 1)
                nc.gpsimd.tensor_tensor(avl[:, :, :], avraw[:, :, :], avh[:, :, :].bitcast(F32), ALU.subtract).then_inc(av_split, 1)

            def head(h, par, cnt, first=False, pair=None):
                pool_wait(pool, aw_in[par], 16 * cnt + 16)
                if not first:
                    pool_wait(pool, ring_done, PRE_RING + (h - 2) * PER_RING - 4)
                split(h, par, 0, 0, 2 * D, 0)
                if isinstance(h, int) and h == 0:
                    power(pool, "rms1", MOST)
                if pair is not None:
                    value_weights(pair)
                if not first:
                    pool_wait(pool, wo_done, h - 1)
                split(h, par, 2 * D, 2 * D, D, 2)

            head(0, 0, 0, True, 0)
            nc.gpsimd.memset(causal[:, :], 0.0).then_inc(const_done, 1)
            pool.wait_ge(const_done, 5)
            nc.gpsimd.affine_select(out=causal[:, :], in_=causal[:, :], compare_op=ALU.is_ge, fill=NEG, base=0,
                                    pattern=[[-1, S]], channel_multiplier=1).then_inc(const_done, 1)
            head(1, 1, 0, True, 1)
            with pool.Fori(1, AH // 2 - 1) as i:
                head(2 * i, 0, i)
                head(2 * i + 1, 1, i, pair=i + 1)
            head(AH - 2, 0, AH // 2 - 1)
            head(AH - 1, 1, AH // 2 - 1)

        def attn_sp(sp):
            def load(par, src):
                sp.dma_start(araw[par][:, :], src).then_inc(aw_in[par], 16)

            def load_values(m):
                after(sp, av_split, 2 * m)
                sp.dma_start(avraw[:, :, :].rearrange("p c n -> p (c n)"), attnv_d[bass.ds(m, 1), :, :].rearrange("a p n -> (a p) n")).then_inc(av_in, 16)

            def load_heads(i):
                for par in range(2):
                    sp.wait_ge(aw_split, 4 * (2 * i + par) - 4)
                    load(par, attn_d[bass.ds(2 * i + par, 1), :, :].rearrange("a p n -> (a p) n"))

            load(0, attn_d[0])
            load_values(0)
            load(1, attn_d[1])
            load_values(1)
            with sp.Fori(1, AH // 2 - 1) as i:
                load_heads(i)
                load_values(i + 1)
            load_heads(AH // 2 - 1)

        @block.sync
        def _(sp):
            for half in range(2):
                b0 = half * B // 2
                sp.dma_start(X[:, b0:b0 + B // 2, :], x_d[b0:b0 + B // 2].rearrange("b s d -> s b d")).then_inc(x_in[half], 16)
            sp.dma_start(gates[:, :], gate_d.partition_broadcast(P)).then_inc(gate_in, 16)
            xattn_sp(sp)
            barrier(sp, 1)
            ffn_sp(sp)
            barrier(sp, 2)
            attn_sp(sp)
            barrier(sp, 3)
            moe_sp(sp)
            for b in range(B):
                sp.wait_ge(f1.tile_out, b + 1)
                sp.dma_start(out_d[b], X[:, b, :]).then_inc(out_done, 16)
            sp.wait_ge(out_done, 16 * B)

        @block.gpsimd
        def _(pool):
            gp = nc.gpsimd
            gp.memset(ident[:, :], 0.0).then_inc(pool_chain, 1)
            gp.memset(identb[:, :], 0.0).then_inc(pool_chain, 1)
            for m in (head_rows, earlier, ones):
                gp.memset(m[:, :], 1.0).then_inc(pool_chain, 1)
            pool.wait_ge(pool_chain, 5)
            gp.affine_select(out=earlier[:, :], in_=earlier[:, :], compare_op=ALU.is_ge, fill=0.0, base=-1,
                             pattern=[[1, P]], channel_multiplier=-1).then_inc(pool_chain, 1)
            for m in (ident, identb):
                gp.affine_select(out=m[:, :], in_=m[:, :], compare_op=ALU.not_equal, fill=1.0, base=0,
                                 pattern=[[-1, P]], channel_multiplier=1).then_inc(const_done, 1)
            gp.affine_select(out=head_rows[:, :], in_=head_rows[:, :], compare_op=ALU.is_ge, fill=0.0, base=0,
                             pattern=[[-XD, HT]], channel_multiplier=1).then_inc(const_done, 1)
            pool.wait_ge(const_done, 3)
            gp.affine_select(out=head_rows[:, :], in_=head_rows[:, :], compare_op=ALU.is_ge, fill=0.0, base=XD - 1,
                             pattern=[[XD, HT]], channel_multiplier=-1).then_inc(const_done, 1)
            xattn_pool(pool, 0)
            power(pool, "ln2")
            gp.memset(sel[:, :], 1.0).then_inc(pool_chain, 1)
            pool.wait_ge(pool_chain, 7)
            for step, (base, sign) in enumerate(((0, 1), (I1 - 1, -1))):
                for part in range(3):
                    v = sel[32 * part:32 * part + 32, :]
                    i = gp.affine_select(out=v, in_=v, compare_op=ALU.is_ge, fill=0.0, base=base,
                                         pattern=[[sign, E1 * I1]], channel_multiplier=-sign * I1)
                i.then_inc(pool_chain, 1)
                pool.wait_ge(pool_chain, 8 + step)
            barrier(pool, 1)
            ffn_pool(pool)
            xattn_pool(pool, 1)
            power(pool, "ln4")
            power(pool, "rms1")
            barrier(pool, 2)
            power(pool, "ln4", MOST)
            attn_pool(pool)
            barrier(pool, 3)
            power(pool, "rms2")
            power(pool, "rms2", EARLY)
            moe_pool(pool)

        @block.scalar
        def _(act):
            act.wait_ge(gate_in, 16)
            nc.scalar.activation(tg[:, :], gates[:, :], ACT.Tanh).then_inc(tg_done, 1)
            act.wait_ge(const_done, 4)
            xattn_act(act, 0)
            barrier(act, 1)
            ffn_act(act)
            xattn_act(act, 1)
            barrier(act, 2)

            def last_squares(b):
                if b == 2:
                    squares_act(act, z_done, MOST, B)
                if b == 4:
                    act.wait_ge(squared, B)

            columns_act(act, t_done, thi_done, last_squares)
            attn_act(act)
            acc_act(act, ayT, wo_done, (AH, AH + 1), ay_out)
            squares_act(act, ay_free, 0, EARLY)
            barrier(act, 3)
            squares_act(act, ay_free, EARLY, B)
            act.wait_ge(squared, 2 * B)
            columns_act(act, f1.t_done, f1.thi)
            moe_act(act)
            acc_act(act, yT, f1.d_done, (2 * J1 - 1, 2 * J1), f1.y_out)

        @block.tensor
        def _(pe):
            pe.wait_ge(const_done, 2)
            xattn_pe(pe, 0)
            barrier(pe, 1)
            ffn_pe(pe)
            xattn_pe(pe, 1)
            barrier(pe, 2)
            attn_pe(pe)
            rows_pe(pe, ayT, ay_out, ayt_done, ay_free)
            barrier(pe, 3)
            moe_pe(pe)

        @block.vector
        def _(dve):
            v = nc.vector
            ch = Chain(dve, dve_chain)
            ch.link(v.memset(zeros[:, :].bitcast(F32), 0.0))
            dve.sem_inc(Es.zeroed, 1)
            ch.link(v.memset(mhalf[:, :], -0.5))
            ch.link(v.memset(upto[:, :, :], 0.0))
            for e in range(E0):
                v.memset(expert_ids[:, e:e + 1], float(e))
                v.memset(upto[:, e, 0:e + 1], 1.0)
            for j in range(SLOTS):
                v.memset(tile_ids[:, j:j + 1], float(j))
            ch.link(v.memset(xb0.v17[:, :, :, XD:XD + 1], 1.0))
            for e in range(E0):
                ch.link(v.memset(rank8[:, e:e + 1], float(E0 - e)))
            dve.wait_ge(x_in[0], 16)
            for b in range(EARLY):
                i = v.bn_stats(st[:, b, :], X[:, b, :])
            ch.link(i)
            moments(ch, 0, EARLY)
            dve.wait_ge(x_in[1], 16)
            xattn_dve(dve, 0, ch)
            barrier(dve, 1)
            moments(ch, MOST, B)

            def normed(b, s_n, s_hi, s_lo, make):
                make(b)
                if b > 1:
                    columns_lo(dve, b - 2, s_hi, s_lo)
                if b == B - 1:
                    columns_lo(dve, b - 1, s_hi, s_lo)
                    columns_lo(dve, b, s_hi, s_lo)

            ffn_dve(dve, ch)
            xattn_dve(dve, 1, ch)
            barrier(dve, 2)
            moments(ch, MOST, B)

            powered(dve, "rms1")

            def scaled(out, b, weight):
                return v.scalar_tensor_tensor(out=out[b % 2][:, :], in0=Z[:, b, :], scalar=rstd[:, b:b + 1], in1=vec(weight), op0=ALU.mult, op1=ALU.mult)

            for b in range(B):
                after(dve, t_done, b - 1)
                if b == 2:
                    powered(dve, "ln4", MOST)
                    for k in range(MOST, B):
                        ln_scale(Z[:, k, :], X[:, k, :], k).then_inc(z_done, 1)
                if b == MOST:
                    powered(dve, "rms1", MOST)
                normed(b, n_done, thi_done, tlo_done, lambda b: scaled(gxn, b, "ln1").then_inc(n_done, 1))
            dve.wait_ge(const_done, 6)
            attn_dve(dve, ch)
            for b in range(B):
                dve.wait_ge(ayt_done, b + 1)
                v.tensor_tensor(Z[:, b, :], PS[:, b % 4, 0:D], Z[:, b, :], ALU.add).then_inc(ay_free, 1)
            dve.wait_ge(ay_free, B)
            barrier(dve, 3)
            s = f1
            powered(dve, "rms2")
            for b in range(B):
                after(dve, s.t_done, b - 1)
                if b == EARLY:
                    powered(dve, "rms2", EARLY)
                normed(b, s.n_done, s.thi, s.tlo, lambda b: scaled(fxn, b, "ln2").then_inc(s.n_done, 1))
            moe_dve(dve, ch)
            for b in range(B):
                dve.wait_ge(s.yt_done, b + 1)
                v.scalar_tensor_tensor(out=X[:, b, :], in0=PS[:, b % 4, 0:D], scalar=tg[:, 3:4], in1=X[:, b, :], op0=ALU.mult, op1=ALU.add).then_inc(s.tile_out, 1)


def kernel(**inputs):
    import numpy as np
    import concourse.bacc as bacc
    from concourse.bass_utils import run_bass_kernel_spmd

    a = {k: np.asarray(v) for k, v in inputs.items()}

    def columns(m):
        return m.reshape(C, P, -1).transpose(1, 0, 2)

    def cross(k, v, q, o):
        return columns(np.concatenate([m.T for m in (k, v, q, o)], axis=1))

    def expert_tiles(gate, up, down, J):
        pad = ((0, J * P - gate.shape[0]), (0, 0))
        g, u, d = (np.pad(m, pad) for m in (gate, up, down))
        cols = [m.reshape(J, P, C, P).transpose(0, 3, 2, 1).reshape(J, P, D) for m in (g, u)]
        return np.concatenate(cols + [d.reshape(J, P, D)], axis=2)

    def by_partition(w):
        return w.reshape(E0, -1, P, w.shape[2]).transpose(0, 2, 1, 3).reshape(E0, P, -1)

    heads = [a["L1_ffn_" + k].reshape(C, P, AH, AD).transpose(2, 1, 0, 3).reshape(AH, P, D) for k in ("wq", "wk")]
    arrays = {
        "ctx": a["ctx_2048"].transpose(2, 0, 1).reshape(C, P, B, S).transpose(2, 1, 0, 3),
        "x": a["x"],
        "wx": np.stack([cross(*(a["L0_xattn_" + k] for k in ("Wk", "Wv", "Wq", "Wo"))),
                        cross(*(a["L1_xattn_" + k] for k in ("k_img_w", "v_img_w", "q_w", "o_w")))]),
        "vec": np.concatenate([a[k] for k in (
            "L0_xattn_bk", "L0_xattn_bv", "L0_xattn_bq", "L0_xattn_bo", "L1_xattn_k_img_b", "L1_xattn_v_img_b",
            "L1_xattn_q_b", "L1_xattn_o_b", "L1_xattn_norm_k_img_w", "L1_xattn_norm_q_w", "L1_ffn_ln1_w", "L1_ffn_ln2_w")]),
        "gate": np.concatenate([a["g_xattn"], a["g_ffn"]]),
        "rw0": columns(a["L0_ffn_router_w"]),
        "rw1": columns(a["L1_ffn_gate_w"].T),
        "moe0": np.concatenate([by_partition(a["L0_ffn_" + k]) for k in ("gate_w", "up_w", "down_w")], axis=2),
        "moe1": np.concatenate([
            expert_tiles(a["L1_ffn_sg_w"], a["L1_ffn_su_w"], a["L1_ffn_sd_w"].T, SJ),
            expert_tiles(a["L1_ffn_eg_w"].reshape(-1, D), a["L1_ffn_eu_w"].reshape(-1, D),
                         a["L1_ffn_ed_w"].transpose(0, 2, 1).reshape(-1, D), J1 - SJ)]),
        "attn": np.concatenate(heads + [a["L1_ffn_wo"].reshape(AH, P, D)], axis=2),
        "attn_v": a["L1_ffn_wv"].reshape(C, P, AH // 2, 2 * AD).transpose(2, 1, 0, 3).reshape(AH // 2, P, C * 2 * AD),
    }
    arrays = {k: np.ascontiguousarray(v) for k, v in arrays.items()}
    nc = bacc.Bacc("TRN2", target_bir_lowering=False, num_devices=1)
    aps = [nc.dram_tensor(k, v.shape, mybir.dt.from_np(v.dtype), kind="ExternalInput").ap() for k, v in arrays.items()]
    out = nc.dram_tensor("out", (B, S, D), F32, kind="ExternalOutput").ap()
    build(nc, *aps, out)
    return run_bass_kernel_spmd(nc, [arrays], core_ids=[0]).results[0]["out"]
```
